# Optimizing a Trainium2 kernel written in Bass

```python
import numpy as np
import jax
import jax.numpy as jnp

def _softmax(x, axis=-1):
    return jax.nn.softmax(x, axis=axis)

def _gelu(x):
    return jax.nn.gelu(x, approximate=True)

def _silu(x):
    return jax.nn.silu(x)

def _sigmoid(x):
    return jax.nn.sigmoid(x)

def _layernorm(x, axis=-1, eps=1e-05):
    m = jnp.mean(x, axis=axis, keepdims=True)
    v = jnp.var(x, axis=axis, keepdims=True)
    return (x - m) / jnp.sqrt(v + eps)

def _scatter_add(tgt, idx, src, axis=0):
    return tgt.at[idx].add(src)

def _segment_sum(src, seg, n):
    return jax.ops.segment_sum(src, seg, n)
kernel_name = 'mk_xattn_ffn_d2_seqx_r8_18182c'

def setup_inputs(seed: int=0):
    np.random.seed(seed)
    _w = jnp.asarray

    def _rec_inputs():
        import jax
        import jax.numpy as jnp
        _rk = jax.random.key(seed)
        x = 7.22e-05 + 1 * jax.random.normal(jax.random.fold_in(_rk, 1), (32, 64, 256), jnp.float32)
        _lenS = 64 - jax.random.randint(jax.random.fold_in(_rk, 7), (32,), 0, max(1, 64 // 4) + 1, jnp.int32)
        _lenS2 = 64 - jax.random.randint(jax.random.fold_in(_rk, 8), (32,), 0, max(1, 64 // 4) + 1, jnp.int32)
        _ctx_2048P = jax.random.normal(jax.random.fold_in(_rk, 11), (32, 16, 256), jnp.float32)
        _ctx_2048c = jax.random.dirichlet(jax.random.fold_in(_rk, 511), 0.3 * jnp.ones((16,), jnp.float32), (32, 64))
        _ctx_2048t = jnp.einsum('bsk,bkd->bsd', _ctx_2048c, _ctx_2048P)
        _ctx_2048t = _ctx_2048t * jax.lax.rsqrt(jnp.mean(jnp.square(_ctx_2048t)) + 1e-12) * 0.953939
        ctx_2048 = -0.000514642 + 1.00011 * (_ctx_2048t + 0.3 * jax.random.normal(jax.random.fold_in(_rk, 611), (32, 64, 256), jnp.float32))
        itok_BxS_0_1023 = jax.random.randint(jax.random.fold_in(_rk, 12), (32, 64), 0, 128, jnp.int32)
        return (x, ctx_2048, itok_BxS_0_1023)
    x, ctx_2048, itok_BxS_0_1023 = _rec_inputs()

    def _L0_xattn_setup():
        import jax, jax.numpy as jnp
        import numpy as np
        HIDDEN = 256
        NUM_HEADS = 16
        NUM_KV_HEADS = 4
        HEAD_DIM = 128
        ROPE_THETA = 10000.0
        EPS = 1e-06

        def rms_norm(x, w, eps=EPS):
            var = jnp.mean(jnp.square(x), axis=-1, keepdims=True)
            return x * jax.lax.rsqrt(var + eps) * w

        def rope_cache(L, head_dim, theta, dtype):
            inv_freq = 1.0 / theta ** (jnp.arange(0, head_dim, 2, dtype=jnp.float32) / head_dim)
            t = jnp.arange(L, dtype=jnp.float32)
            freqs = jnp.outer(t, inv_freq)
            emb = jnp.concatenate([freqs, freqs], -1)
            cos = jnp.cos(emb).astype(dtype)[None, :, None, :]
            sin = jnp.sin(emb).astype(dtype)[None, :, None, :]
            return (cos, sin)

        def rotate_half(x):
            x1, x2 = jnp.split(x, 2, axis=-1)
            return jnp.concatenate([-x2, x1], axis=-1)
        key = jax.random.key(seed)
        ks = jax.random.split(key, 10)
        B, L, T = (2, 256, 64)
        q_out = NUM_HEADS * HEAD_DIM
        kv_out = NUM_KV_HEADS * HEAD_DIM
        s = lambda fan_in: 1.0 / np.sqrt(fan_in)
        return {'x': jax.random.normal(ks[0], (B, L, HIDDEN), jnp.float32), 'h_ctx_kv': jax.random.normal(ks[1], (B, T, HIDDEN), jnp.float32), 'wq': jax.random.normal(ks[2], (HIDDEN, q_out), jnp.float32) * s(HIDDEN), 'wk': jax.random.normal(ks[3], (HIDDEN, kv_out), jnp.float32) * s(HIDDEN), 'wv': jax.random.normal(ks[4], (HIDDEN, kv_out), jnp.float32) * s(HIDDEN), 'wo': jax.random.normal(ks[5], (q_out, HIDDEN), jnp.float32) * s(q_out), 'wk_ctx': jax.random.normal(ks[6], (HIDDEN, kv_out), jnp.float32) * s(HIDDEN), 'wv_ctx': jax.random.normal(ks[7], (HIDDEN, kv_out), jnp.float32) * s(HIDDEN), 'q_norm_w': jnp.ones((HEAD_DIM,), jnp.float32), 'k_norm_w': jnp.ones((HEAD_DIM,), jnp.float32)}
    _L0_xattn_all = _L0_xattn_setup()
    _L0_xattn_in = {k: v for k, v in _L0_xattn_all.items() if k in ('wq', 'wk', 'wv', 'wo', 'wk_ctx', 'wv_ctx', 'q_norm_w', 'k_norm_w')}
    del _L0_xattn_all

    def _L0_ffn_setup():
        import math
        import jax, jax.numpy as jnp
        import numpy as np
        DIM = 256
        RANK = 8
        B, T = (4, 512)

        def _orthogonal(key, n):
            a = jax.random.normal(key, (n, n), dtype=jnp.float32)
            q, r = jnp.linalg.qr(a)
            q = q * jnp.sign(jnp.diagonal(r))[None, :]
            return q
        key = jax.random.key(seed)
        kx, kf = jax.random.split(key)
        x = jax.random.normal(kx, (B, T, DIM), dtype=jnp.float32)
        fkeys = jax.random.split(kf, RANK)
        factors = jnp.stack([_orthogonal(fkeys[r], DIM) * (r + 1) ** (-0.5) for r in range(RANK)])
        bias = jnp.zeros((DIM,), dtype=jnp.float32)
        return {'x': x, 'factors': factors, 'bias': bias}
    _L0_ffn_all = _L0_ffn_setup()
    _L0_ffn_in = {k: v for k, v in _L0_ffn_all.items() if k in ('factors', 'bias')}
    del _L0_ffn_all

    def _L1_xattn_setup():
        import jax, jax.numpy as jnp
        import numpy as np
        B, Lq, Lk = (2, 512, 128)
        Q_DIM, KV_DIM = (256, 256)
        H, HD = (16, 128)
        KVC, QC, R = (64, 96, 64)
        LOOKBACK = 8
        NEG = -1e+30

        def _rope(x, L):
            half = x.shape[-1] // 2
            inv_freq = 1.0 / 10000.0 ** (jnp.arange(half, dtype=jnp.float32) / half)
            ang = jnp.arange(L, dtype=jnp.float32)[:, None] * inv_freq
            cos, sin = (jnp.cos(ang), jnp.sin(ang))
            x1, x2 = (x[..., :half], x[..., half:])
            return jnp.concatenate([x1 * cos - x2 * sin, x1 * sin + x2 * cos], axis=-1)
        key = jax.random.key(seed)
        ks = jax.random.split(key, 11)

        def w(k, shape, fan_in):
            return jax.random.normal(k, shape, jnp.float32) / np.sqrt(fan_in).astype(np.float32)
        return {'q': jax.random.normal(ks[0], (B, Lq, Q_DIM), jnp.float32), 'kv': jax.random.normal(ks[1], (B, Lk, KV_DIM), jnp.float32), 'seg_id': jnp.sort(jax.random.randint(ks[2], (B, Lq), 0, Lk), axis=-1), 'W_kvc': w(ks[3], (KV_DIM, KVC), KV_DIM), 'W_dq': w(ks[4], (Q_DIM, QC), Q_DIM), 'W_uq': w(ks[5], (QC, H * HD), QC), 'W_qr': w(ks[6], (QC, H * R), QC), 'W_uk': w(ks[7], (KVC, H * HD), KVC), 'W_kr': w(ks[8], (KVC, R), KVC), 'W_uv': w(ks[9], (KVC, H * HD), KVC), 'W_o': w(ks[10], (H * HD, Q_DIM), H * HD)}
    _L1_xattn_all = _L1_xattn_setup()
    _L1_xattn_in = {k: v for k, v in _L1_xattn_all.items() if k in ('W_kvc', 'W_dq', 'W_uq', 'W_qr', 'W_uk', 'W_kr', 'W_uv', 'W_o')}
    del _L1_xattn_all

    def _L1_ffn_setup():
        import jax, jax.numpy as jnp
        import numpy as np
        B_, S, D = (2, 256, 256)
        F_ = 1024
        R = 16
        H = 16
        HD = D // H
        MOD_SCALE = 0.1
        EPS = 1e-06

        def _rmsnorm(x, w):
            v = jnp.mean(x * x, axis=-1, keepdims=True)
            return x * jax.lax.rsqrt(v + EPS) * w

        def _attention(x, Wq, Wk, Wv, Wo):
            b, s, d = x.shape
            q = (x @ Wq.T).reshape(b, s, H, HD)
            k = (x @ Wk.T).reshape(b, s, H, HD)
            v = (x @ Wv.T).reshape(b, s, H, HD)
            scores = jnp.einsum('bqhd,bkhd->bhqk', q, k) / np.sqrt(HD).astype(np.float32)
            causal = jnp.tril(jnp.ones((s, s), bool))
            scores = jnp.where(causal, scores, jnp.finfo(scores.dtype).min)
            probs = jax.nn.softmax(scores, axis=-1)
            out = jnp.einsum('bhqk,bkhd->bqhd', probs, v).reshape(b, s, d)
            return out @ Wo.T
        key = jax.random.key(seed)
        ks = jax.random.split(key, 12)
        sd = 0.02
        return {'hidden_states': jax.random.normal(ks[0], (B_, S, D), jnp.float32), 'ln1_w': jnp.ones((D,), jnp.float32), 'ln2_w': jnp.ones((D,), jnp.float32), 'Wq': jax.random.normal(ks[1], (D, D), jnp.float32) * sd, 'Wk': jax.random.normal(ks[2], (D, D), jnp.float32) * sd, 'Wv': jax.random.normal(ks[3], (D, D), jnp.float32) * sd, 'Wo': jax.random.normal(ks[4], (D, D), jnp.float32) * sd, 'A': jax.random.normal(ks[5], (D, R), jnp.float32) * (0.01 / np.sqrt(D)), 'B': jax.random.normal(ks[6], (R, F_), jnp.float32) * (0.01 / np.sqrt(R)), 'W_in_base': jax.random.normal(ks[7], (F_, D), jnp.float32) * sd, 'W_up_base': jax.random.normal(ks[8], (F_, D), jnp.float32) * sd, 'W_down': jax.random.normal(ks[9], (D, F_), jnp.float32) * sd}
    _L1_ffn_all = _L1_ffn_setup()
    _L1_ffn_in = {k: v for k, v in _L1_ffn_all.items() if k in ('ln1_w', 'ln2_w', 'Wq', 'Wk', 'Wv', 'Wo', 'A', 'B', 'W_in_base', 'W_up_base', 'W_down')}
    del _L1_ffn_all
    return {'x': x, 'ctx_2048': ctx_2048, 'itok_BxS_0_1023': itok_BxS_0_1023, 'L0_xattn_wq': _L0_xattn_in['wq'], 'L0_xattn_wk': _L0_xattn_in['wk'], 'L0_xattn_wv': _L0_xattn_in['wv'], 'L0_xattn_wo': _L0_xattn_in['wo'], 'L0_xattn_wk_ctx': _L0_xattn_in['wk_ctx'], 'L0_xattn_wv_ctx': _L0_xattn_in['wv_ctx'], 'L0_xattn_q_norm_w': _L0_xattn_in['q_norm_w'], 'L0_xattn_k_norm_w': _L0_xattn_in['k_norm_w'], 'L0_ffn_factors': _L0_ffn_in['factors'], 'L0_ffn_bias': _L0_ffn_in['bias'], 'L1_xattn_W_kvc': _L1_xattn_in['W_kvc'], 'L1_xattn_W_dq': _L1_xattn_in['W_dq'], 'L1_xattn_W_uq': _L1_xattn_in['W_uq'], 'L1_xattn_W_qr': _L1_xattn_in['W_qr'], 'L1_xattn_W_uk': _L1_xattn_in['W_uk'], 'L1_xattn_W_kr': _L1_xattn_in['W_kr'], 'L1_xattn_W_uv': _L1_xattn_in['W_uv'], 'L1_xattn_W_o': _L1_xattn_in['W_o'], 'L1_ffn_ln1_w': _L1_ffn_in['ln1_w'], 'L1_ffn_ln2_w': _L1_ffn_in['ln2_w'], 'L1_ffn_Wq': _L1_ffn_in['Wq'], 'L1_ffn_Wk': _L1_ffn_in['Wk'], 'L1_ffn_Wv': _L1_ffn_in['Wv'], 'L1_ffn_Wo': _L1_ffn_in['Wo'], 'L1_ffn_A': _L1_ffn_in['A'], 'L1_ffn_B': _L1_ffn_in['B'], 'L1_ffn_W_in_base': _L1_ffn_in['W_in_base'], 'L1_ffn_W_up_base': _L1_ffn_in['W_up_base'], 'L1_ffn_W_down': _L1_ffn_in['W_down']}

def reference(x, ctx_2048, itok_BxS_0_1023, L0_xattn_wq, L0_xattn_wk, L0_xattn_wv, L0_xattn_wo, L0_xattn_wk_ctx, L0_xattn_wv_ctx, L0_xattn_q_norm_w, L0_xattn_k_norm_w, L0_ffn_factors, L0_ffn_bias, L1_xattn_W_kvc, L1_xattn_W_dq, L1_xattn_W_uq, L1_xattn_W_qr, L1_xattn_W_uk, L1_xattn_W_kr, L1_xattn_W_uv, L1_xattn_W_o, L1_ffn_ln1_w, L1_ffn_ln2_w, L1_ffn_Wq, L1_ffn_Wk, L1_ffn_Wv, L1_ffn_Wo, L1_ffn_A, L1_ffn_B, L1_ffn_W_in_base, L1_ffn_W_up_base, L1_ffn_W_down):
    import jax
    import jax.numpy as jnp

    def _L0_xattn_ref(x, h_ctx_kv, wq, wk, wv, wo, wk_ctx, wv_ctx, q_norm_w, k_norm_w):
        import jax, jax.numpy as jnp
        import numpy as np
        HIDDEN = 256
        NUM_HEADS = 16
        NUM_KV_HEADS = 4
        HEAD_DIM = 128
        ROPE_THETA = 10000.0
        EPS = 1e-06

        def rms_norm(x, w, eps=EPS):
            var = jnp.mean(jnp.square(x), axis=-1, keepdims=True)
            return x * jax.lax.rsqrt(var + eps) * w

        def rope_cache(L, head_dim, theta, dtype):
            inv_freq = 1.0 / theta ** (jnp.arange(0, head_dim, 2, dtype=jnp.float32) / head_dim)
            t = jnp.arange(L, dtype=jnp.float32)
            freqs = jnp.outer(t, inv_freq)
            emb = jnp.concatenate([freqs, freqs], -1)
            cos = jnp.cos(emb).astype(dtype)[None, :, None, :]
            sin = jnp.sin(emb).astype(dtype)[None, :, None, :]
            return (cos, sin)

        def rotate_half(x):
            x1, x2 = jnp.split(x, 2, axis=-1)
            return jnp.concatenate([-x2, x1], axis=-1)
        B, L, _ = x.shape
        T = h_ctx_kv.shape[1]
        rep = NUM_HEADS // NUM_KV_HEADS
        q = (x @ wq).reshape(B, L, NUM_HEADS, HEAD_DIM)
        k = (x @ wk).reshape(B, L, NUM_KV_HEADS, HEAD_DIM)
        v = (x @ wv).reshape(B, L, NUM_KV_HEADS, HEAD_DIM)
        q = rms_norm(q, q_norm_w)
        k = rms_norm(k, k_norm_w)
        k_ctx = (h_ctx_kv @ wk_ctx).reshape(B, T, NUM_KV_HEADS, HEAD_DIM)
        v_ctx = (h_ctx_kv @ wv_ctx).reshape(B, T, NUM_KV_HEADS, HEAD_DIM)
        k_ctx = rms_norm(k_ctx, k_norm_w)
        cos, sin = rope_cache(L, HEAD_DIM, ROPE_THETA, x.dtype)
        q = q * cos + rotate_half(q) * sin
        k = k * cos + rotate_half(k) * sin
        k_full = jnp.concatenate([k_ctx, k], axis=1)
        v_full = jnp.concatenate([v_ctx, v], axis=1)
        k_full = jnp.repeat(k_full, rep, axis=2)
        v_full = jnpp_repeat = jnp.repeat(v_full, rep, axis=2)
        i = jnp.arange(L)[:, None]
        j = jnp.arange(L)[None, :]
        causal = jnp.where(j > i, -jnp.inf, 0.0).astype(x.dtype)
        mask = jnp.concatenate([jnp.zeros((L, T), x.dtype), causal], axis=1)
        scale = 1.0 / np.sqrt(HEAD_DIM)
        scores = jnp.einsum('blhd,bmhd->bhlm', q, k_full) * scale + mask
        probs = jax.nn.softmax(scores, axis=-1)
        out = jnp.einsum('bhlm,bmhd->blhd', probs, v_full)
        out = out.reshape(B, L, NUM_HEADS * HEAD_DIM)
        return out @ wo

    def _L0_ffn_ref(x, factors, bias):
        import math
        import jax, jax.numpy as jnp
        import numpy as np
        DIM = 256
        RANK = 8
        B, T = (4, 512)

        def _orthogonal(key, n):
            a = jax.random.normal(key, (n, n), dtype=jnp.float32)
            q, r = jnp.linalg.qr(a)
            q = q * jnp.sign(jnp.diagonal(r))[None, :]
            return q
        rank = factors.shape[0]
        mixed = jnp.einsum('btd,rde->bte', x, factors)
        mixed = mixed / math.sqrt(rank) + bias
        return mixed

    def _L1_xattn_ref(q, kv, seg_id, W_kvc, W_dq, W_uq, W_qr, W_uk, W_kr, W_uv, W_o):
        import jax, jax.numpy as jnp
        import numpy as np
        B, Lq, Lk = (2, 512, 128)
        Q_DIM, KV_DIM = (256, 256)
        H, HD = (16, 128)
        KVC, QC, R = (64, 96, 64)
        LOOKBACK = 8
        NEG = -1e+30

        def _rope(x, L):
            half = x.shape[-1] // 2
            inv_freq = 1.0 / 10000.0 ** (jnp.arange(half, dtype=jnp.float32) / half)
            ang = jnp.arange(L, dtype=jnp.float32)[:, None] * inv_freq
            cos, sin = (jnp.cos(ang), jnp.sin(ang))
            x1, x2 = (x[..., :half], x[..., half:])
            return jnp.concatenate([x1 * cos - x2 * sin, x1 * sin + x2 * cos], axis=-1)
        b, lq, _ = q.shape
        lk = kv.shape[1]
        kv_c = kv @ W_kvc
        q_c = q @ W_dq
        q_nope = (q_c @ W_uq).reshape(b, lq, H, HD).transpose(0, 2, 1, 3)
        q_rope = (q_c @ W_qr).reshape(b, lq, H, R).transpose(0, 2, 1, 3)
        k_nope = (kv_c @ W_uk).reshape(b, lk, H, HD)
        v = (kv_c @ W_uv).reshape(b, lk, H, HD)
        k_rope = kv_c @ W_kr
        q_rope = _rope(q_rope, lq)
        k_rope = _rope(k_rope, lk)
        scale = 1.0 / np.sqrt(HD + R).astype(np.float32)
        scores = (jnp.einsum('bhqd,bkhd->bhqk', q_nope, k_nope) + jnp.einsum('bhqr,bkr->bhqk', q_rope, k_rope)) * scale
        k_ids = jnp.arange(lk)[None, None, :]
        qs = seg_id[:, :, None]
        good = (k_ids <= qs) & (k_ids >= qs - LOOKBACK)
        scores = jnp.where(good[:, None, :, :], scores, NEG)
        attn = jax.nn.softmax(scores, axis=-1)
        out = jnp.einsum('bhqk,bkhd->bqhd', attn, v).reshape(b, lq, H * HD)
        return out @ W_o

    def _L1_ffn_ref(hidden_states, ln1_w, ln2_w, Wq, Wk, Wv, Wo, A, B, W_in_base, W_up_base, W_down):
        import jax, jax.numpy as jnp
        import numpy as np
        B_, S, D = (2, 256, 256)
        F_ = 1024
        R = 16
        H = 16
        HD = D // H
        MOD_SCALE = 0.1
        EPS = 1e-06

        def _rmsnorm(x, w):
            v = jnp.mean(x * x, axis=-1, keepdims=True)
            return x * jax.lax.rsqrt(v + EPS) * w

        def _attention(x, Wq, Wk, Wv, Wo):
            b, s, d = x.shape
            q = (x @ Wq.T).reshape(b, s, H, HD)
            k = (x @ Wk.T).reshape(b, s, H, HD)
            v = (x @ Wv.T).reshape(b, s, H, HD)
            scores = jnp.einsum('bqhd,bkhd->bhqk', q, k) / np.sqrt(HD).astype(np.float32)
            causal = jnp.tril(jnp.ones((s, s), bool))
            scores = jnp.where(causal, scores, jnp.finfo(scores.dtype).min)
            probs = jax.nn.softmax(scores, axis=-1)
            out = jnp.einsum('bhqk,bkhd->bqhd', probs, v).reshape(b, s, d)
            return out @ Wo.T
        residual = hidden_states
        x = _rmsnorm(hidden_states, ln1_w)
        attn = _attention(x, Wq, Wk, Wv, Wo)
        mod = MOD_SCALE * jnp.tanh(attn @ A)
        h = _rmsnorm(residual, ln2_w)
        gate_pre = h @ W_in_base.T + mod * (h @ A) @ B
        gate = jax.nn.silu(gate_pre)
        up = h @ W_up_base.T
        mlp_out = gate * up @ W_down.T
        return residual + mlp_out
    x = x + _L0_xattn_ref(_layernorm(x, axis=-1), ctx_2048, L0_xattn_wq, L0_xattn_wk, L0_xattn_wv, L0_xattn_wo, L0_xattn_wk_ctx, L0_xattn_wv_ctx, L0_xattn_q_norm_w, L0_xattn_k_norm_w)
    x = x + _L0_ffn_ref(_layernorm(x, axis=-1), L0_ffn_factors, L0_ffn_bias)
    x = x + _L1_xattn_ref(_layernorm(x, axis=-1), ctx_2048, itok_BxS_0_1023, L1_xattn_W_kvc, L1_xattn_W_dq, L1_xattn_W_uq, L1_xattn_W_qr, L1_xattn_W_uk, L1_xattn_W_kr, L1_xattn_W_uv, L1_xattn_W_o)
    x = x + _L1_ffn_ref(_layernorm(x, axis=-1), L1_ffn_ln1_w, L1_ffn_ln2_w, L1_ffn_Wq, L1_ffn_Wk, L1_ffn_Wv, L1_ffn_Wo, L1_ffn_A, L1_ffn_B, L1_ffn_W_in_base, L1_ffn_W_up_base, L1_ffn_W_down)
    return x

_drawn_inputs = setup_inputs


def setup_inputs(seed=0):
    import zlib

    import numpy as np

    out = dict(_drawn_inputs(seed))
    spreads = {'L0_xattn_q_norm_w': (1.0, 0.2),
     'L0_xattn_k_norm_w': (1.0, 0.2),
     'L0_ffn_bias': (0.0, 0.1),
     'L1_ffn_ln1_w': (1.0, 0.6),
     'L1_ffn_ln2_w': (1.0, 0.6)}
    factors = {'L1_ffn_Wq': 64.0,
     'L1_ffn_Wk': 64.0,
     'L1_ffn_Wv': 64.0,
     'L1_ffn_Wo': 64.0,
     'L1_ffn_A': 64.0,
     'L1_ffn_B': 64.0,
     'L1_ffn_W_in_base': 3.801,
     'L1_ffn_W_up_base': 3.765,
     'L1_ffn_W_down': 3.759}
    for name, (base, spread) in spreads.items():
        noise = np.random.default_rng([zlib.crc32(name.encode()), seed]).standard_normal(out[name].shape)
        drawn = base * np.exp(spread * noise) if base else spread * noise
        out[name] = jnp.asarray(drawn.astype(out[name].dtype))
    for name, factor in factors.items():
        out[name] = (out[name] * factor).astype(out[name].dtype)
    return out
```

```python
from contextlib import ExitStack, nullcontext

import numpy as np

import concourse.bass as bass
from concourse import mybir

P = 128
D = 256
CK = D // P
SEQ = 64
NSEQ = 32
NTOK = NSEQ * SEQ
TT = NTOK // P
T = 256
ST = T // SEQ
NT = NTOK // T
X0 = 2
H = 16
G = 4
HD = 128
UNITS = H // 2
MASKED = -float(2 ** 100)

F32 = mybir.dt.float32
F32R = mybir.dt.float32r
BF16 = mybir.dt.bfloat16
ALU = mybir.AluOpType
ACT = mybir.ActivationFunctionType
AX = mybir.AxisListType.X


def ds(start, size):
    return bass.ds(start, size)


def along(ap, axis, n):
    shape = list(ap.shape)
    shape.insert(axis, n)
    return ap.unsqueeze(axis).broadcast_to(shape)


class Taken:

    def __init__(self, nc, ctx):
        self.nc, self.all = nc, []
        self.stack = ctx.enter_context(ExitStack())
        ctx.callback(self.clear)

    def take(self, name):
        self.all.append(self.stack.enter_context(self.nc.semaphore(name)))
        return self.all[-1]

    def clear(self):
        with self.nc.Block() as block:
            @block.gpsimd
            def _(pool):
                for s in self.all:
                    pool.sem_clear(s)


class Signals:

    CREDIT = 16

    def __init__(self, taken, names, less=()):
        self.sem = {n: taken.take(n) for n in names}
        self.credit = {n: self.CREDIT - (1 if n in less else 0) for n in names}

    def __getitem__(self, name):
        return self.sem[name]

    def give_credit(self, eng, names):
        for n in names:
            eng.sem_inc(self.sem[n], self.credit[n])

    def need(self, eng, name, count):
        if isinstance(count, int) and count <= 0:
            return
        eng.wait_ge(self.sem[name], count + self.CREDIT)


def matmul3(pe, out, left, right, start, stop, skip=False):
    (lh, ll), (rh, rl) = left, right
    pe.matmul(out, ll, rh, start=start, stop=False, skip_group_check=skip)
    pe.matmul(out, lh, rl, start=False, stop=False, skip_group_check=skip)
    return pe.matmul(out, lh, rh, start=False, stop=stop, skip_group_check=skip)


def layer0_attention(nc, dram, xres, consts):
    ident = consts["ident"]
    with ExitStack() as ctx:
        taken = Taken(nc, ctx)
        def sb(name, shape, dt=F32):
            return ctx.enter_context(nc.sbuf_tensor(name, shape, dt))

        def bank(name, shape=(P, 512)):
            return ctx.enter_context(nc.psum_tensor(name, list(shape), F32))

        KVC = G * HD
        QC = H * HD
        w_hi = sb("a_w_hi", [P, 4 * CK * KVC + CK * QC], F32R)
        w_lo = sb("a_w_lo", [P, 4 * CK * KVC + CK * QC], F32R)
        wo = sb("a_wo", [P, H, D])
        keysT = sb("a_keysT", [P, 2, ST, G, P])
        vals = sb("a_vals", [P, 2, ST, KVC])
        xnT_hi = sb("a_xnT_hi", [P, 2, CK, T], F32R)
        xnT_lo = sb("a_xnT_lo", [P, 2, CK, T], F32R)
        cT = sb("a_cT", [P, 2, CK, T])
        cT_hi = sb("a_cT_hi", [P, CK, T], F32R)
        cT_lo = sb("a_cT_lo", [P, CK, T], F32R)
        xn = sb("a_xn", [P, 2, D])
        cos_d = sb("a_cos_d", [P, SEQ])
        sin_d = sb("a_sin_d", [P, SEQ])
        cos_t = sb("a_cos_t", [P, HD])
        sin_t = sb("a_sin_t", [P, HD])
        kw_t = sb("a_kw_t", [P, HD])
        kw_d = sb("a_kw_d", [P, 1])
        qw_d = sb("a_qw_d", [P, 1])
        sq = sb("a_sq", [P, 2, ST, 2, SEQ])
        qc = sb("a_qc", [P, 2, ST, 2, SEQ])
        qs = sb("a_qs", [P, 2, ST, 2, SEQ])
        qT = sb("a_qT", [P, 2, ST, 2, SEQ])
        q_ms = sb("a_q_ms", [P, 2, ST])
        q_rs = sb("a_q_rs", [P, 2, ST])
        s_max = sb("a_s_max", [P, 2, ST])
        s_bias = sb("a_s_bias", [P, 2, ST])
        s_sum = sb("a_s_sum", [P, 2, ST])
        s_inv = sb("a_s_inv", [P, 2, ST])
        prob = sb("a_prob", [P, 2, ST, P])
        probT = sb("a_probT", [P, 2, ST, P])
        attT = sb("a_attT", [P, 2, 2, T])
        k_sq = sb("a_k_sq", [P, G, HD])
        k_ms = sb("a_k_ms", [P, G])
        k_rs = sb("a_k_rs", [P, G])
        kn = sb("a_kn", [P, G, HD])
        kc = sb("a_kc", [P, G, HD])
        ks = sb("a_ks", [P, G, HD])
        kr = sb("a_kr", [P, G, HD])
        bst = sb("a_bst", [P, 2, 6])
        mv = sb("a_mv", [P, 2, 2])
        var = sb("a_var", [P, 2])
        rstd = sb("a_rstd", [P, 2])
        spare = sb("a_spare", [P, 1])

        q_ps = [bank(f"a_q_ps{k}") for k in range(2)]
        s_ps = [bank(f"a_s_ps{k}") for k in range(2)]
        t_ps = bank("a_t_ps")
        o_ps = bank("a_o_ps")
        out_ps = bank("a_out_ps")
        m_ps = bank("a_m_ps")

        PE_S = ["q_ready", "st_ready", "s_ready", "t_ready", "pv_ready", "out_ready", "m_ready"]
        ACT_S = ["sq_done", "exp_done", "ot_done", "ksq_done", "m_free_act", "xhi_done", "chi_done"]
        DVE_S = ["rope_done", "ms_done", "nb_done", "pt_done", "inv_done", "x_done", "kms_done", "kn_done",
                 "kq_done", "var_done", "xn_done", "xlo_done", "clo_done", "bst_done", "mv_done", "max_done", "kred_done"]
        POOL_S = ["qr_done", "qrs_done", "pn_done", "krs_done", "kr_done", "rstd_done", "kc_done"]
        sg = Signals(taken, PE_S + ACT_S + DVE_S + POOL_S, less=("ot_done",))
        need = sg.need
        w_in = [taken.take(f"w_in{k}") for k in range(4)]
        c_in = [taken.take(f"c_in{k}") for k in range(2)]
        small_in = taken.take("small_in")
        x_in = taken.take("tokens_in")
        wo_in = taken.take("wo_in")
        whi_done = taken.take("whi_done")
        wlo_done = taken.take("wlo_done")
        tab_done = taken.take("tab_done")

        stage = [vals[:, 0].rearrange("p s n -> p (s n)"), vals[:, 1].rearrange("p s n -> p (s n)"),
                 keysT[:, 0].rearrange("p s g n -> p (s g n)"), keysT[:, 1].rearrange("p s g n -> p (s g n)")]
        CH = 2048

        def kv_weight(kind, which, c):
            at = ((0 if kind == "c" else 2) + which) * CK * KVC + c * KVC
            return w_hi[:, at:at + KVC], w_lo[:, at:at + KVC]

        def q_weight(head, c):
            at = 4 * CK * KVC + c * QC + head * HD
            return w_hi[:, at:at + HD], w_lo[:, at:at + HD]

        USES = [("K", "c", 0), ("KT", "c", 0), ("K", "c", 1), ("KT", "c", 1), ("V", "c", 0), ("V", "c", 1),
                ("LN", "s", 0), ("V", "s", 0), ("K", "s", 0), ("K", "s", 1), ("KT", "s", 0), ("V", "s", 1),
                ("KT", "s", 1)]
        FIRST = [("K", "c", 0), ("K", "c", 1), ("V", "c", 0), ("KT", "c", 0), ("V", "c", 1), ("KT", "c", 1),
                 ("LN", "s", 0), ("K", "s", 0), ("V", "s", 0), ("K", "s", 1), ("V", "s", 1), ("KT", "s", 0),
                 ("KT", "s", 1)]
        FIRST_BANKS = [m_ps, s_ps[0], s_ps[1], t_ps, out_ps]
        NU = len(USES)

        def use_of(tile, use):
            if isinstance(tile, int) and tile == 0:
                return FIRST[use], FIRST_BANKS[use % len(FIRST_BANKS)]
            return USES[use], m_ps

        MIDDLE = [None, 1, 3, 5, 7, None, 10, 12]
        LATE = [0, 2, 4, 6, 8, 9, 11, None]
        SQ_AT = 2
        LAST_C = USES.index(("V", "c", 1)) + 1
        FIRST_LAST_C = FIRST.index(("V", "c", 1)) + 1
        KSEQ = {("c", 0): 0, ("c", 1): 1, ("s", 0): 2, ("s", 1): 3}

        block = ctx.enter_context(nc.Block())

        @block.sync
        def _(sp):
            for k, names in enumerate([("wk_ctx", "wv_ctx"), ("wk", "wv")]):
                for m, name in enumerate(names):
                    sp.dma_start(stage[k][:, m * CK * KVC:(m + 1) * CK * KVC].rearrange("p (c n) -> p c n", c=CK),
                                 dram[name].rearrange("(c p) n -> p c n", p=P)).then_inc(w_in[k], 16)
                if k == 0:
                    sp.dma_start(cT[:, 0], dram["ctxT"][:, 0:T].rearrange("(c p) n -> p c n", p=P)).then_inc(c_in[0], 16)
            for name, tile in (("cos_d", cos_d), ("sin_d", sin_d), ("cos_t", cos_t), ("sin_t", sin_t)):
                sp.dma_start(tile[:], dram[name]).then_inc(small_in, 16)
            sp.dma_start(kw_t[:], dram["k_norm_w"].partition_broadcast(P)).then_inc(small_in, 16)
            sp.dma_start(kw_d[:], dram["k_norm_w"].rearrange("(p a) -> p a", a=1)).then_inc(small_in, 16)
            sp.dma_start(qw_d[:], dram["q_norm_w"].rearrange("(p a) -> p a", a=1)).then_inc(small_in, 16)
            for c in range(CK):
                sp.dma_start(stage[2 + c], dram["wq"][c * P:(c + 1) * P, :]).then_inc(w_in[2 + c], 16)
            sp.dma_start(xres[:, X0:X0 + TT, :], dram["x"].rearrange("(t p) d -> p t d", p=P)).then_inc(x_in, 16)
            sp.dma_start(cT[:, 1], dram["ctxT"][:, T:2 * T].rearrange("(c p) n -> p c n", p=P)).then_inc(c_in[1], 16)
            sp.dma_start(wo[:], dram["wo"].rearrange("(h p) n -> p h n", p=P)).then_inc(wo_in, 16)
            with sp.Fori(0, NT // 2 - 1) as j:
                for a in range(2):
                    need(sp, "clo_done", 2 * j + a + 1)
                    sp.dma_start(cT[:, a], dram["ctxT"][:, ds((2 * j + a + 2) * T, T)].rearrange("(c p) n -> p c n", p=P)
                                 ).then_inc(c_in[a], 16)
            for a in range(2):
                need(sp, "clo_done", NT - 1 + a)
                sp.dma_start(cT[:, a], dram["ctxT"][:, 0:T].rearrange("(c p) n -> p c n", p=P)).then_inc(c_in[a], 16)
            for a in range(2):
                sp.wait_ge(c_in[a], 16 * (NT // 2 + 1))

        @block.gpsimd
        def _(pool):
            sg.give_credit(pool, POOL_S)
            def key_rms(tile, src, half):
                n = 4 * tile + KSEQ[(src, half)]
                need(pool, "kms_done", n + 1)
                need(pool, "kn_done", n)
                pool.tensor_tensor(k_rs[:], k_ms[:], consts["minus_half"][:, 0:G],
                                   ALU.pow).then_inc(sg["krs_done"], 1)

            def key_cos(tile, half):
                need(pool, "kn_done", 4 * tile + KSEQ[("s", half)] + 1)
                pool.tensor_tensor(kc[:], kn[:], along(cos_t[:], 1, G), ALU.mult).then_inc(sg["kc_done"], 1)

            def key_add(tile, half):
                m = 2 * tile + half
                need(pool, "kc_done", m + 1)
                need(pool, "kq_done", m + 1)
                if half == 1:
                    order = FIRST if isinstance(tile, int) else USES
                    need(pool, "m_ready", NU * tile + order.index(("KT", "s", 0)) + 1)
                pool.tensor_tensor(kr[:], kc[:], ks[:], ALU.add).then_inc(sg["kr_done"], 1)

            def norm_pool(tile):
                need(pool, "var_done", tile + 1)
                pool.tensor_tensor(rstd[:], var[:], consts["minus_half"][:, 0:2], ALU.pow).then_inc(sg["rstd_done"], 1)

            def add_rope(n, b):
                need(pool, "rope_done", n + 1)
                need(pool, "s_ready", n - 1)
                pool.tensor_tensor(qT[:, b], qc[:, b], qs[:, b], ALU.add).then_inc(sg["qr_done"], 1)

            key_rms(0, "c", 0)
            key_rms(0, "c", 1)
            norm_pool(0)
            pool.wait_ge(tab_done, 1)
            for half in range(2):
                key_rms(0, "s", half)
                key_cos(0, half)
                if half == 0:
                    key_add(0, 0)
            key_add(0, 1)
            add_rope(0, 0)
            with pool.Fori(0, NT // 2) as j:
                for a in range(2):
                    for p in range(UNITS):
                        n, b, tile = 16 * j + 8 * a + p, p % 2, 2 * j + a
                        kind, src, half = USES[LATE[p - 1]] if p and LATE[p - 1] is not None else ("", "", 0)
                        need(pool, "ms_done", n + 1)
                        need(pool, "exp_done", n - 1)
                        pool.tensor_tensor(q_rs[:, b], q_ms[:, b], consts["minus_half"][:, 0:ST],
                                           ALU.pow).then_inc(sg["qrs_done"], 1)
                        if kind == "K":
                            key_rms(tile + 1, src, half)
                        if kind == "K" and src == "s":
                            key_cos(tile + 1, half)
                        if p == 2:
                            norm_pool(tile + 1)
                        need(pool, "inv_done", n + 1)
                        pool.tensor_tensor(prob[:, b], prob[:, b], along(s_inv[:, b], 2, P),
                                           ALU.mult).then_inc(sg["pn_done"], 1)
                        add_rope(n + 1, 1 - b)
                        if kind == "K" and src == "s":
                            key_add(tile + 1, half)

        @block.scalar
        def _(act):
            sg.give_credit(act, ACT_S)
            def high_weight(k):
                act.wait_ge(w_in[k], 32 if k < 2 else 16)
                act.activation(w_hi[:, k * CH:(k + 1) * CH], stage[k], ACT.Copy).then_inc(whi_done, 1)

            high_weight(0)
            act.wait_ge(c_in[0], 16)
            act.activation(cT_hi[:], cT[:, 0], ACT.Copy).then_inc(sg["chi_done"], 1)
            high_weight(1)

            def misc_act(tile, use, par):
                (kind, src, half), ps = use_of(tile, use)
                if kind == "K":
                    need(act, "m_ready", NU * tile + use + 1)
                    need(act, "kred_done", 4 * tile + KSEQ[(src, half)])
                    act.activation(k_sq[:], ps[:].rearrange("p (g d) -> p g d", g=G), ACT.Square
                                   ).then_inc(sg["ksq_done"], 1)
                elif kind == "V":
                    need(act, "m_ready", NU * tile + use + 1)
                    need(act, "pv_ready", 8 * (tile - 1))
                    keys = slice(0, SEQ) if src == "c" else slice(SEQ, P)
                    for s in range(2):
                        last = act.activation(vals[keys, par, 2 * half + s, :], ps[s * SEQ:(s + 1) * SEQ, :], ACT.Copy)
                    last.then_inc(sg["m_free_act"], 1)
                elif kind == "KT":
                    need(act, "m_ready", NU * tile + use + 1)
                    need(act, "s_ready", 8 * (tile - 1))
                    keys = slice(0, SEQ) if src == "c" else slice(SEQ, P)
                    dst = keysT[:, par, 2 * half:2 * half + 2, :, keys].rearrange("p s g k -> p g s k")
                    act.activation(dst, ps[:].rearrange("p (g s k) -> p g s k", g=G, s=2), ACT.Copy,
                                   scale=kw_d[:, 0:1] if src == "c" else 1.0).then_inc(sg["m_free_act"], 1)
                else:
                    need(act, "m_ready", NU * tile + use + 1)
                    need(act, "q_ready", 8 * (tile - 1))
                    act.activation(xnT_hi[:, par], ps[:].rearrange("p (c t) -> p c t", c=CK), ACT.Copy
                                   ).then_inc(sg["xhi_done"], 1)

            def square(n, b):
                need(act, "q_ready", n + 1)
                need(act, "st_ready", n - 1)
                act.activation(sq[:, b].rearrange("p s h t -> p h s t"),
                               q_ps[b][:].rearrange("p (h s t) -> p h s t", h=2, s=ST), ACT.Square
                               ).then_inc(sg["sq_done"], 1)

            act.wait_ge(small_in, 7 * 16)
            for use in range(NU):
                if use in (1, 2):
                    high_weight(use + 1)
                if use in (2, 3):
                    act.wait_ge(wlo_done, 2 if use == 2 else 4)
                misc_act(0, use, 0)
                if use == FIRST_LAST_C:
                    act.wait_ge(c_in[1], 16)
                    need(act, "m_ready", FIRST_LAST_C)
                    act.activation(cT_hi[:], cT[:, 1], ACT.Copy).then_inc(sg["chi_done"], 1)
            square(0, 0)
            act.wait_ge(wlo_done, 5)
            with act.Fori(0, NT // 2) as j:
                for a in range(2):
                    for p in range(UNITS):
                        n, b, tile = 16 * j + 8 * a + p, p % 2, 2 * j + a
                        if p and LATE[p - 1] is not None:
                            misc_act(tile + 1, LATE[p - 1], 1 - a)
                        need(act, "nb_done", n + 1)
                        need(act, "t_ready", n - 1)
                        need(act, "inv_done", n - 1)
                        for s in range(ST):
                            if s == SQ_AT:
                                square(n + 1, 1 - b)
                            last = act.activation(prob[:, b, s], s_ps[b][:, s * P:(s + 1) * P], ACT.Exp,
                                                  bias=s_bias[:, b, s:s + 1], scale=q_rs[:, b, s:s + 1],
                                                  accum_out=s_sum[:, b, s:s + 1])
                        last.then_inc(sg["exp_done"], 1)
                        if MIDDLE[p] is not None:
                            misc_act(tile + 1, MIDDLE[p], 1 - a)
                        need(act, "pv_ready", n)
                        need(act, "out_ready", n - 2)
                        act.activation(attT[:, 1 - b].rearrange("p h (s t) -> p h s t", s=ST),
                                       o_ps[:].rearrange("p (s h t) -> p h s t", s=ST, h=2), ACT.Copy
                                       ).then_inc(sg["ot_done"], 1)
                        if p == 5:
                            act.wait_ge(c_in[a], 16 * (j + 2))
                            need(act, "m_ready", NU * (tile + 1) + LAST_C)
                            act.activation(cT_hi[:], cT[:, a], ACT.Copy).then_inc(sg["chi_done"], 1)
            N = NT * UNITS
            need(act, "pv_ready", N)
            need(act, "out_ready", N - 2)
            act.activation(attT[:, 1].rearrange("p h (s t) -> p h s t", s=ST),
                           o_ps[:].rearrange("p (s h t) -> p h s t", s=ST, h=2), ACT.Copy).then_inc(sg["ot_done"], 1)

        @block.vector
        def _(dve):
            sg.give_credit(dve, DVE_S)
            def split_context(par, count):
                need(dve, "chi_done", count)
                dve.tensor_tensor(cT_lo[:], cT[:, par], cT_hi[:].bitcast(F32), ALU.subtract).then_inc(sg["clo_done"], 1)

            def x_tile(row):
                return xres[:, X0 + row, :] if isinstance(row, int) else xres[:, ds(X0 + row, 1), :].rearrange("p a d -> p (a d)")

            def norm_stats(tile, row0):
                for t in range(2):
                    last = dve.bn_stats(bst[:, t], x_tile(row0 + t))
                last.then_inc(sg["bst_done"], 1)
                need(dve, "bst_done", tile + 1)
                dve.memset(spare[:], 0.0)
                for t in range(2):
                    last = dve.bn_aggr(mv[:, t], bst[:, t])
                last.then_inc(sg["mv_done"], 1)
                need(dve, "mv_done", tile + 1)
                dve.tensor_scalar(var[:], mv[:, :, 1], 1e-5, None, ALU.add).then_inc(sg["var_done"], 1)

            def norm_x(tile, row0):
                need(dve, "rstd_done", tile + 1)
                for t in range(2):
                    last = dve.tensor_scalar(xn[:, t], x_tile(row0 + t), mv[:, t, 0:1], rstd[:, t:t + 1],
                                             ALU.subtract, ALU.mult)
                last.then_inc(sg["xn_done"], 1)

            def key_stats(tile, src, half):
                n = 4 * tile + KSEQ[(src, half)]
                need(dve, "ksq_done", n + 1)
                dve.tensor_reduce(k_ms[:], k_sq[:], AX, ALU.add).then_inc(sg["kred_done"], 1)
                need(dve, "kred_done", n + 1)
                dve.tensor_scalar(k_ms[:], k_ms[:], 1.0 / HD, 1e-6, ALU.mult, ALU.add).then_inc(sg["kms_done"], 1)

            def key_norm(tile, src, half, use):
                ps = use_of(tile, use)[1]
                n = 4 * tile + KSEQ[(src, half)]
                need(dve, "krs_done", n + 1)
                need(dve, "m_ready", NU * tile + use + 1)
                dve.tensor_tensor(kn[:], ps[:].rearrange("p (g d) -> p g d", g=G), along(k_rs[:], 2, HD),
                                  ALU.mult).then_inc(sg["kn_done"], 1)

            def key_sin(tile, half):
                need(dve, "kn_done", 4 * tile + KSEQ[("s", half)] + 1)
                need(dve, "kr_done", 2 * tile + half)
                dve.tensor_tensor(ks[:, :, 0:HD // 2], kn[:, :, HD // 2:], along(sin_t[:, 0:HD // 2], 1, G), ALU.mult)
                dve.tensor_tensor(ks[:, :, HD // 2:], kn[:, :, 0:HD // 2], along(sin_t[:, HD // 2:], 1, G),
                                  ALU.mult).then_inc(sg["kq_done"], 1)

            def low_x(tile, par):
                ps = use_of(tile, FIRST.index(("LN", "s", 0)))[1]
                need(dve, "xhi_done", tile + 1)
                dve.tensor_tensor(xnT_lo[:, par], ps[:].rearrange("p (c t) -> p c t", c=CK),
                                  xnT_hi[:, par].bitcast(F32), ALU.subtract).then_inc(sg["xlo_done"], 1)

            def rope(n, b, between=lambda: None):
                need(dve, "sq_done", n + 1)
                need(dve, "qr_done", n - 1)
                q = q_ps[b][:].rearrange("p (h s t) -> p s h t", h=2, s=ST)
                half = P // 2
                cw = cos_d[:].unsqueeze(1).unsqueeze(1).broadcast_to([P, ST, 2, SEQ])
                sw = sin_d[:].unsqueeze(1).unsqueeze(1).broadcast_to([P, ST, 2, SEQ])
                dve.tensor_tensor(qc[:, b], q, cw, ALU.mult)
                between()
                dve.tensor_tensor(qs[0:half, b], q[half:P], sw[half:P], ALU.mult)
                dve.tensor_tensor(qs[half:P, b], q[0:half], sw[0:half], ALU.mult).then_inc(sg["rope_done"], 1)

            def low_weight(k):
                dve.wait_ge(whi_done, k + 1)
                dve.tensor_tensor(w_lo[:, k * CH:(k + 1) * CH], stage[k], w_hi[:, k * CH:(k + 1) * CH].bitcast(F32),
                                  ALU.subtract).then_inc(wlo_done, 1)

            low_weight(0)
            split_context(0, 1)
            low_weight(1)
            key_stats(0, "c", 0)
            key_norm(0, "c", 0, 0)
            low_weight(2)
            key_stats(0, "c", 1)
            low_weight(3)
            need(dve, "m_ready", FIRST.index(("KT", "c", 0)) + 1)
            key_norm(0, "c", 1, 1)
            dve.wait_ge(small_in, 7 * 16)
            dve.tensor_scalar(cos_d[:], cos_d[:], qw_d[:, 0:1], None, ALU.mult)
            dve.tensor_scalar(sin_d[:], sin_d[:], qw_d[:, 0:1], None, ALU.mult)
            dve.tensor_tensor(cos_t[:], cos_t[:], kw_t[:], ALU.mult)
            dve.tensor_tensor(sin_t[:, 0:HD // 2], sin_t[:, 0:HD // 2], kw_t[:, HD // 2:], ALU.mult)
            dve.tensor_tensor(sin_t[:, HD // 2:], sin_t[:, HD // 2:], kw_t[:, 0:HD // 2], ALU.mult).then_inc(tab_done, 1)
            dve.wait_ge(x_in, 16)
            norm_stats(0, 0)
            norm_x(0, 0)
            split_context(1, 2)
            low_x(0, 0)
            dve.memset(o_ps[:], 0.0).then_inc(wlo_done, 1)
            for half in range(2):
                use = FIRST.index(("K", "s", half))
                key_stats(0, "s", half)
                key_norm(0, "s", half, use)
                if half == 0:
                    dve.wait_ge(tab_done, 1)
                key_sin(0, half)
            rope(0, 0)
            with dve.Fori(0, NT // 2) as j:
                for a in range(2):
                    for p in range(UNITS):
                        n, b = 16 * j + 8 * a + p, p % 2
                        tile = 2 * j + a
                        late = LATE[p - 1] if p else None
                        kind, src, half = USES[late] if late is not None else ("", "", 0)
                        if kind == "K":
                            key_stats(tile + 1, src, half)
                        elif kind == "LN":
                            low_x(tile + 1, 1 - a)
                        need(dve, "st_ready", n + 1)
                        need(dve, "qrs_done", n - 1)
                        dve.tensor_scalar(q_ms[:, b], q_ps[b][:, 0:ST], HD * 1e-6, None, ALU.add).then_inc(sg["ms_done"], 1)
                        with dve.If(j > 0) if 8 * a + p == 0 else nullcontext():
                            need(dve, "t_ready", n)
                            need(dve, "pv_ready", n - 2)
                            dve.tensor_copy(probT[:, 1 - b], t_ps[:].rearrange("p (s r) -> p s r", s=ST)
                                            ).then_inc(sg["pt_done"], 1)
                        if p == 2:
                            with dve.If(j > 0) if a == 0 else nullcontext():
                                need(dve, "out_ready", 8 * tile)
                                dve.tensor_tensor(xres[:, ds(X0 + 2 * tile - 2, 2), :], out_ps[:].rearrange("p (t d) -> p t d", t=2),
                                                  xres[:, ds(X0 + 2 * tile - 2, 2), :], ALU.add).then_inc(sg["x_done"], 1)
                        need(dve, "s_ready", n + 1)
                        dve.tensor_reduce(s_max[:, b], s_ps[b][:].rearrange("p (s k) -> p s k", s=ST), AX, ALU.max
                                          ).then_inc(sg["max_done"], 1)
                        need(dve, "qrs_done", n + 1)
                        need(dve, "max_done", n + 1)
                        need(dve, "exp_done", n - 1)
                        dve.scalar_tensor_tensor(s_bias[:, b], s_max[:, b], -1.0, q_rs[:, b], ALU.mult, ALU.mult
                                                 ).then_inc(sg["nb_done"], 1)
                        if kind == "K":
                            key_norm(tile + 1, src, half, late)

                        def invert():
                            need(dve, "exp_done", n + 1)
                            need(dve, "pn_done", n - 1)
                            dve.reciprocal(s_inv[:, b], s_sum[:, b]).then_inc(sg["inv_done"], 1)

                        rope(n + 1, 1 - b, between=invert)
                        if kind == "K" and src == "s":
                            key_sin(tile + 1, half)
                        if p == 1:
                            norm_stats(tile + 1, 2 * tile + 2)
                        if p == 2:
                            norm_x(tile + 1, 2 * tile + 2)
                        if p == 6:
                            split_context(a, tile + 3)
            N = NT * UNITS
            need(dve, "t_ready", N)
            need(dve, "pv_ready", N - 2)
            dve.tensor_copy(probT[:, 1], t_ps[:].rearrange("p (s r) -> p s r", s=ST)).then_inc(sg["pt_done"], 1)
            need(dve, "out_ready", N)
            dve.tensor_tensor(xres[:, X0 + TT - 2:X0 + TT, :], out_ps[:].rearrange("p (t d) -> p t d", t=2),
                              xres[:, X0 + TT - 2:X0 + TT, :], ALU.add).then_inc(sg["x_done"], 1)

        @block.tensor
        def _(pe):
            sg.give_credit(pe, PE_S)
            EVACS = sum(1 for use in USES if use[0] in ("V", "KT"))

            def bank_free(tile, use):
                order, back = (USES, 1)
                if isinstance(tile, int) and tile == 0:
                    order, back = FIRST, len(FIRST_BANKS)
                elif use == 0:
                    return
                use -= back
                if use < 0:
                    return
                kind, src, half = order[use]
                if kind == "K":
                    need(pe, "kn_done", 4 * tile + KSEQ[(src, half)] + 1)
                elif kind == "LN":
                    need(pe, "xlo_done", tile + 1)
                else:
                    need(pe, "m_free_act", EVACS * tile + sum(1 for u in order[:use + 1] if u[0] in ("V", "KT")))

            def misc_pe(tile, use, par):
                (kind, src, half), ps = use_of(tile, use)
                bank_free(tile, use)
                if kind in "KV":
                    if src == "c":
                        need(pe, "clo_done", tile + 1)
                        left = [(cT_hi[:, c, half * P:(half + 1) * P], cT_lo[:, c, half * P:(half + 1) * P]) for c in range(CK)]
                    else:
                        need(pe, "xlo_done", tile + 1)
                        left = [(xnT_hi[:, par, c, half * P:(half + 1) * P], xnT_lo[:, par, c, half * P:(half + 1) * P])
                                for c in range(CK)]
                    for c in range(CK):
                        last = matmul3(pe, ps[:], left[c], kv_weight(src, 0 if kind == "K" else 1, c), c == 0, c == CK - 1)
                elif kind == "KT":
                    if src == "c":
                        need(pe, "kn_done", 4 * tile + KSEQ[(src, half)] + 1)
                    else:
                        need(pe, "kr_done", 2 * tile + half + 1)
                    for g in range(G):
                        last = pe.transpose(ps[:, g * P:(g + 1) * P], (kn if src == "c" else kr)[:, g], ident[:])
                else:
                    need(pe, "xn_done", tile + 1)
                    for c in range(CK):
                        for t in range(2):
                            last = pe.transpose(ps[:, c * T + t * P:c * T + (t + 1) * P], xn[:, t, c * P:(c + 1) * P], ident[:])
                last.then_inc(sg["m_ready"], 1)

            def project_q(n, tile, par, p):
                b = p % 2
                need(pe, "xlo_done", tile + 1)
                need(pe, "ms_done", n - 1)
                for hh in range(2):
                    for c in range(CK):
                        last = matmul3(pe, q_ps[b][:, hh * T:(hh + 1) * T], q_weight(2 * p + hh, c),
                                       (xnT_hi[:, par, c, :], xnT_lo[:, par, c, :]), c == 0, c == CK - 1)
                last.then_inc(sg["q_ready"], 1)

            def sum_squares(n, b):
                need(pe, "sq_done", n + 1)
                need(pe, "rope_done", n + 1)
                for s in range(ST):
                    last = pe.matmul(q_ps[b][:, s:s + 1], sq[:, b, s], consts["ones"][:, 0:1], start=True, stop=True)
                last.then_inc(sg["st_ready"], 1)

            def scores(n, tile, par, p):
                b, g = p % 2, p // 2
                need(pe, "qr_done", n + 1)
                need(pe, "exp_done", n - 1)
                need(pe, "m_free_act", EVACS * (tile + 1))
                for s in range(ST):
                    pe.matmul(s_ps[b][:, s * P:(s + 1) * P], qT[:, b, s], keysT[:, par, s, g, :], start=True, stop=False,
                              skip_group_check=True)
                    last = pe.matmul(s_ps[b][:, s * P + SEQ:(s + 1) * P], consts["mask_rows"][:], consts["causal"][:],
                                     start=False, stop=True, skip_group_check=True)
                last.then_inc(sg["s_ready"], 1)

            def transpose_probs(m, b):
                need(pe, "pn_done", m + 1)
                need(pe, "pt_done", m)
                for s in range(ST):
                    last = pe.transpose(t_ps[:, s * P:(s + 1) * P], prob[:, b, s], ident[:])
                last.then_inc(sg["t_ready"], 1)

            def attend(m, par, p):
                b, g = p % 2, p // 2
                need(pe, "pt_done", m + 1)
                need(pe, "ot_done", m)
                for s in range(ST):
                    last = pe.matmul(o_ps[:, s * P:(s + 1) * P], vals[:, par, s, g * P:(g + 1) * P], probT[:, b, s],
                                     start=True, stop=True)
                last.then_inc(sg["pv_ready"], 1)

            def project_out(m, tile, p):
                b = p % 2
                need(pe, "ot_done", m + 1)
                if p == 0:
                    need(pe, "x_done", tile)
                for hh in range(2):
                    for t in range(2):
                        last = pe.matmul(out_ps[:, t * D:(t + 1) * D], attT[:, b, hh, t * P:(t + 1) * P], wo[:, 2 * p + hh],
                                         start=(p == 0 and hh == 0 and t == 0), stop=(p == UNITS - 1 and hh == 1),
                                         skip_group_check=True)
                last.then_inc(sg["out_ready"], 1)

            for use in range(NU):
                if use == 0:
                    pe.wait_ge(wlo_done, 1)
                if FIRST[use] == ("K", "s", 0):
                    pe.wait_ge(wlo_done, 2)
                misc_pe(0, use, 0)
            pe.wait_ge(wlo_done, 4)
            project_q(0, 0, 0, 0)
            pe.wait_ge(wo_in, 16)
            with pe.Fori(0, NT // 2) as j:
                for a in range(2):
                    for p in range(UNITS):
                        k = 8 * a + p
                        n, tile = 16 * j + k, 2 * j + a
                        sum_squares(n, p % 2)
                        with pe.If(j > 0) if k == 0 else nullcontext():
                            transpose_probs(n - 1, 1 - p % 2)
                        scores(n, tile, a, p)
                        k1 = k + 1
                        project_q(n + 1, 2 * j + k1 // 8, (k1 // 8) % 2, k1 % 8)
                        with pe.If(j > 0) if k == 0 else nullcontext():
                            attend(n - 1, a if p > 0 else 1 - a, (p - 1) % 8)
                        if MIDDLE[p] is not None:
                            misc_pe(tile + 1, MIDDLE[p], 1 - a)
                        with pe.If(j > 0) if k < 2 else nullcontext():
                            project_out(n - 2, tile - (1 if p < 2 else 0), (p - 2) % 8)
                        if LATE[p] is not None:
                            misc_pe(tile + 1, LATE[p], 1 - a)
            N = NT * UNITS
            transpose_probs(N - 1, 1)
            attend(N - 1, 1, UNITS - 1)
            project_out(N - 2, NT - 1, UNITS - 2)
            project_out(N - 1, NT - 1, UNITS - 1)


def layer0_ffn(nc, dram, xres, consts):
    RANK = 8
    with ExitStack() as ctx:
        taken = Taken(nc, ctx)
        def sb(name, shape, dt=F32):
            return ctx.enter_context(nc.sbuf_tensor(name, shape, dt))

        fac = sb("b_fac", [P, RANK, CK, D])
        fsum = sb("b_fsum", [P, CK, D])
        f_hi = sb("b_f_hi", [P, CK, D], F32R)
        f_lo = sb("b_f_lo", [P, CK, D], F32R)
        bias = sb("b_bias", [P, D])
        xn = sb("b_xn", [P, 2, 2, D])
        xnT_hi = sb("b_xnT_hi", [P, 2, CK, T], F32R)
        xnT_lo = sb("b_xnT_lo", [P, 2, CK, T], F32R)
        bst = sb("b_bst", [P, 2, 6])
        mv = sb("b_mv", [P, 2, 2])
        var = sb("b_var", [P, 2])
        rstd = sb("b_rstd", [P, 2])
        spare = sb("b_spare", [P, 1])
        n_ps = [ctx.enter_context(nc.psum_tensor(f"b_n_ps{k}", [P, 512], F32)) for k in range(2)]
        o_ps = [ctx.enter_context(nc.psum_tensor(f"b_o_ps{k}", [P, 512], F32)) for k in range(2)]

        PE_S = ["b_nT_ready", "b_out_ready"]
        ACT_S = ["b_hi_done"]
        DVE_S = ["b_bst_done", "b_mv_done", "b_var_done", "b_xn_done", "b_lo_done", "b_x_done"]
        POOL_S = ["b_rstd_done", "b_bias_done"]
        sg = Signals(taken, PE_S + ACT_S + DVE_S + POOL_S)
        need = sg.need
        f_in = [taken.take(f"b_f_in{r}") for r in range(RANK)]
        bias_in = taken.take("b_bias_in")
        fsum_done = taken.take("b_fsum_done")
        fhi_done = taken.take("b_fhi_done")
        flo_done = taken.take("b_flo_done")

        block = ctx.enter_context(nc.Block())

        @block.sync
        def _(sp):
            for r in range(RANK):
                sp.dma_start(fac[:, r], dram["factors"][r].rearrange("(c p) n -> p c n", p=P)).then_inc(f_in[r], 16)
            sp.dma_start(bias[:], dram["ffn_bias"].partition_broadcast(P)).then_inc(bias_in, 16)

        @block.gpsimd
        def _(pool):
            sg.give_credit(pool, POOL_S)

            def bias_and_root(tile):
                need(pool, "b_var_done", tile + 1)
                pool.tensor_tensor(rstd[:], var[:], consts["minus_half"][:, 0:2], ALU.pow).then_inc(sg["b_rstd_done"], 1)
                need(pool, "b_xn_done", tile + 1)
                rows = xres[:, ds(X0 + 2 * tile, 2), :] if not isinstance(tile, int) else xres[:, X0 + 2 * tile:X0 + 2 * tile + 2, :]
                pool.tensor_tensor(rows, rows, along(bias[:], 1, 2), ALU.add).then_inc(sg["b_bias_done"], 1)

            pool.wait_ge(bias_in, 16)
            for tile in range(1):
                bias_and_root(tile)
            with pool.Fori(0, NT // 2) as j:
                for a in range(2):
                    bias_and_root(2 * j + a + 1)

        @block.scalar
        def _(act):
            sg.give_credit(act, ACT_S)
            act.wait_ge(fsum_done, 1)
            act.activation(f_hi[:], fsum[:], ACT.Copy).then_inc(fhi_done, 1)

            def high(tile, par):
                need(act, "b_nT_ready", tile + 1)
                need(act, "b_out_ready", tile - 1)
                act.activation(xnT_hi[:, par], n_ps[par][:].rearrange("p (c t) -> p c t", c=CK), ACT.Copy
                               ).then_inc(sg["b_hi_done"], 1)

            high(0, 0)
            with act.Fori(0, NT // 2) as j:
                for a in range(2):
                    high(2 * j + a + 1, 1 - a)

        @block.vector
        def _(dve):
            sg.give_credit(dve, DVE_S)

            def row(r):
                return xres[:, X0 + r, :] if isinstance(r, int) else xres[:, ds(X0 + r, 1), :].rearrange("p a d -> p (a d)")

            def norm(tile, par):
                for t in range(2):
                    last = dve.bn_stats(bst[:, t], row(2 * tile + t))
                last.then_inc(sg["b_bst_done"], 1)
                need(dve, "b_bst_done", tile + 1)
                dve.memset(spare[:], 0.0)
                for t in range(2):
                    last = dve.bn_aggr(mv[:, t], bst[:, t])
                last.then_inc(sg["b_mv_done"], 1)
                need(dve, "b_mv_done", tile + 1)
                dve.tensor_scalar(var[:], mv[:, :, 1], 1e-5, None, ALU.add).then_inc(sg["b_var_done"], 1)
                need(dve, "b_rstd_done", tile + 1)
                need(dve, "b_nT_ready", tile - 1)
                for t in range(2):
                    last = dve.tensor_scalar(xn[:, par, t], row(2 * tile + t), mv[:, t, 0:1], rstd[:, t:t + 1],
                                             ALU.subtract, ALU.mult)
                last.then_inc(sg["b_xn_done"], 1)

            def low(tile, par):
                need(dve, "b_hi_done", tile + 1)
                dve.tensor_tensor(xnT_lo[:, par], n_ps[par][:].rearrange("p (c t) -> p c t", c=CK),
                                  xnT_hi[:, par].bitcast(F32), ALU.subtract).then_inc(sg["b_lo_done"], 1)

            norm(0, 0)
            for r in range(RANK):
                dve.wait_ge(f_in[r], 16)
                if r == 1:
                    dve.tensor_tensor(fsum[:], fac[:, 0], fac[:, 1], ALU.add).then_inc(flo_done, 1)
                elif r > 1:
                    dve.wait_ge(flo_done, r - 1)
                    dve.tensor_tensor(fsum[:], fsum[:], fac[:, r], ALU.add).then_inc(flo_done, 1)
            dve.wait_ge(flo_done, RANK - 1)
            dve.tensor_scalar(fsum[:], fsum[:], RANK ** -0.5, None, ALU.mult).then_inc(fsum_done, 1)
            dve.wait_ge(fhi_done, 1)
            dve.tensor_tensor(f_lo[:], fsum[:], f_hi[:].bitcast(F32), ALU.subtract).then_inc(flo_done, 1)
            low(0, 0)
            with dve.Fori(0, NT // 2) as j:
                for a in range(2):
                    tile = 2 * j + a
                    norm(tile + 1, 1 - a)
                    low(tile + 1, 1 - a)
                    need(dve, "b_out_ready", tile + 1)
                    need(dve, "b_bias_done", tile + 1)
                    dve.tensor_tensor(xres[:, ds(X0 + 2 * tile, 2), :], o_ps[a][:].rearrange("p (t d) -> p t d", t=2),
                                      xres[:, ds(X0 + 2 * tile, 2), :], ALU.add).then_inc(sg["b_x_done"], 1)

        @block.tensor
        def _(pe):
            sg.give_credit(pe, PE_S)

            def transpose_norm(tile, par):
                need(pe, "b_xn_done", tile + 1)
                need(pe, "b_lo_done", tile - 1)
                for c in range(CK):
                    for t in range(2):
                        last = pe.transpose(n_ps[par][:, c * T + t * P:c * T + (t + 1) * P], xn[:, par, t, c * P:(c + 1) * P],
                                            consts["ident"][:])
                last.then_inc(sg["b_nT_ready"], 1)

            transpose_norm(0, 0)
            pe.wait_ge(flo_done, RANK)
            with pe.Fori(0, NT // 2) as j:
                for a in range(2):
                    tile = 2 * j + a
                    need(pe, "b_lo_done", tile + 1)
                    need(pe, "b_x_done", tile - 1)
                    for t in range(2):
                        for c in range(CK):
                            last = matmul3(pe, o_ps[a][:, t * D:(t + 1) * D],
                                           (xnT_hi[:, a, c, t * P:(t + 1) * P], xnT_lo[:, a, c, t * P:(t + 1) * P]),
                                           (f_hi[:, c], f_lo[:, c]), c == 0, c == CK - 1)
                    last.then_inc(sg["b_out_ready"], 1)
                    transpose_norm(tile + 1, 1 - a)


def layer1_attention(nc, dram, xres, consts):
    R, KC, QC = 64, 64, 96
    HR = R // 2
    NU = 2 * TT
    SCALE = float(np.float32(1.0) / np.float32(np.sqrt(HD + R)))
    with ExitStack() as ctx:
        taken = Taken(nc, ctx)
        def sb(name, shape, dt=F32):
            return ctx.enter_context(nc.sbuf_tensor(name, shape, dt))

        wuqT = sb("d_wuqT", [P, H, QC])
        wukT = sb("d_wukT", [P, H, KC])
        wuvT = sb("d_wuvT", [P, H, KC])
        wo = sb("d_wo", [P, H, D])
        wqr = sb("d_wqr", [QC, H, R])
        wdq = sb("d_wdq", [P, CK, QC])
        wkvcT = sb("d_wkvcT", [KC, D])
        wkr = sb("d_wkr", [KC, R])
        wkv = sb("d_wkv", [P, CK, P])
        wq_hi = sb("d_wq_hi", [QC, H, P], F32R)
        wq_lo = sb("d_wq_lo", [QC, H, P], F32R)
        wdq_hi = sb("d_wdq_hi", [P, CK, QC], F32R)
        wdq_lo = sb("d_wdq_lo", [P, CK, QC], F32R)
        wkv_hi = sb("d_wkv_hi", [P, CK, P], F32R)
        wkv_lo = sb("d_wkv_lo", [P, CK, P], F32R)
        wn = sb("d_wn", [P, H // 2, D])
        cos_k = sb("d_cos", [P, R])
        sin_k = sb("d_sin", [P, R])
        cT = sb("d_cT", [P, 2, CK, 512])
        cT_hi = sb("d_cT_hi", [P, CK, 512], F32R)
        cT_lo = sb("d_cT_lo", [P, CK, 512], F32R)
        kv = sb("d_kv", [P, 4, P])
        kvc = sb("d_kvc", [P, 4, R])
        kvs = sb("d_kvs", [P, 4, R])
        keysT = sb("d_keysT", [P, NTOK])
        vdiag = sb("d_vdiag", [P, TT, P])
        vcur = sb("d_vcur", [P, 2, P])
        seg_i = sb("d_seg_i", [SEQ, NSEQ], mybir.dt.int32)
        seg = sb("d_seg", [SEQ, NSEQ])
        seg_lo = sb("d_seg_lo", [SEQ, NSEQ])
        key_no = sb("d_key_no", [SEQ, SEQ])
        bad = sb("d_bad", [SEQ, NSEQ, SEQ])
        bad2 = sb("d_bad2", [SEQ, NSEQ, SEQ])
        mask = sb("d_mask", [P, NSEQ, SEQ], BF16)
        xn = sb("d_xn", [P, 2, D])
        xnT_hi = sb("d_xnT_hi", [P, CK, T], F32R)
        xnT_lo = sb("d_xnT_lo", [P, CK, T], F32R)
        qcT_hi = sb("d_qcT_hi", [QC, 2, T], F32R)
        qcT_lo = sb("d_qcT_lo", [QC, 2, T], F32R)
        qf = sb("d_qf", [P, 8, P])
        qcos = sb("d_qcos", [P, 8, R])
        qsin = sb("d_qsin", [P, 8, R])
        qT = sb("d_qT", [P, 2, 4, 2, 2, SEQ])
        s_max = sb("d_s_max", [P, 8])
        s_sum = sb("d_s_sum", [P, 8])
        s_inv = sb("d_s_inv", [P, 2, 8])
        sc = sb("d_sc", [P, 2, 8, SEQ])
        prob = sb("d_prob", [P, 2, 8, SEQ])
        probT = sb("d_probT", [P, 2, 512])
        attT = sb("d_attT", [P, 2, 4, P])
        bst = sb("d_bst", [P, 2, 6])
        mv = sb("d_mv", [P, 2, 2])
        var = sb("d_var", [P, 2])
        rstd = sb("d_rstd", [P, 2])
        spare = sb("d_spare", [P, 1])

        def bank(name):
            return ctx.enter_context(nc.psum_tensor(name, [P, 512], F32))

        q_ps = ctx.enter_context(nc.psum_tensor("d_q_ps", [P, 2, 512], F32))
        qT_ps, s_ps, t_ps, o_ps, out_ps, m_ps = (bank("d_ps_" + n) for n in ("qT", "s", "t", "o", "out", "m"))

        PE_S = ["d_q_ready", "d_qT_ready", "d_s_ready", "d_t_ready", "d_pv_ready", "d_out_ready", "d_nT_ready", "d_qc_ready"]
        ACT_S = ["d_abs_done", "d_qTa_done", "d_exp_done", "d_pt_done", "d_ot_done", "d_xhi_done", "d_qchi_done"]
        DVE_S = ["d_rope_done", "d_qTb_done", "d_max_done", "d_sub_done", "d_sum_done", "d_inv_done", "d_x_done", "d_v_done",
                 "d_bst_done", "d_mv_done", "d_var_done", "d_xn_done", "d_xlo_done", "d_qclo_done"]
        POOL_S = ["d_qf_done", "d_pn_done", "d_rstd_done"]
        sg = Signals(taken, PE_S + ACT_S + DVE_S + POOL_S, less=("d_ot_done",))
        need = sg.need

        def sem(name):
            return taken.take(name)

        fold_in, uv_in, misc_in, tab_in, seg_in = (sem("d_" + n) for n in ("fold_in", "uv_in", "misc_in", "tab_in", "seg_in"))
        c_in = [sem("d_c_in0"), sem("d_c_in1")]
        fold_ready, fold_hi, fold_lo = sem("d_fold_ready"), sem("d_fold_hi"), sem("d_fold_lo")
        wn_ready, wn_done = sem("d_wn_ready"), sem("d_wn_done")
        wk_ready, wk_done, wsmall_hi, wsmall_lo = sem("d_wk_ready"), sem("d_wk_done"), sem("d_wsmall_hi"), sem("d_wsmall_lo")
        mask_step, mask_done, cleared = sem("d_mask_step"), sem("d_mask_done"), sem("d_cleared")
        chi_done, clo_done = sem("d_chi_done"), sem("d_clo_done")
        kv_ready, kv_act, kv_rope, kv_done, kvT_ready, kvT_done = (sem("d_" + n) for n in (
            "kv_ready", "kv_act", "kv_rope", "kv_done", "kvT_ready", "kvT_done"))
        KB = NTOK // 512

        block = ctx.enter_context(nc.Block())

        @block.sync
        def _(sp):
            sp.dma_start(wkvcT[:], dram["wkvcT"]).then_inc(misc_in, 16)
            sp.dma_start(wkr[:], dram["wkr"]).then_inc(misc_in, 16)
            sp.dma_start(wkv[:, :, 0:KC], dram["wkvc"].rearrange("(c p) n -> p c n", p=P)).then_inc(misc_in, 16)
            sp.dma_start(wdq[:], dram["wdq"].rearrange("(c p) n -> p c n", p=P)).then_inc(misc_in, 16)
            sp.dma_start(cT[:, 0], dram["ctxT"][:, 0:512].rearrange("(c p) n -> p c n", p=P)).then_inc(c_in[0], 16)
            sp.dma_start(cos_k[:], dram["cos_k"]).then_inc(tab_in, 16)
            sp.dma_start(sin_k[:], dram["sin_k"]).then_inc(tab_in, 16)
            sp.dma_start(seg_i[:], dram["segT"]).then_inc(seg_in, 16)
            sp.dma_start(key_no[:], dram["key_no"]).then_inc(seg_in, 16)
            sp.dma_start(wuqT[:], dram["wuqT"].rearrange("(h p) n -> p h n", p=P)).then_inc(fold_in, 16)
            sp.dma_start(wukT[:], dram["wukT"].rearrange("(h p) n -> p h n", p=P)).then_inc(fold_in, 16)
            sp.dma_start(wqr[:], dram["wqr"].rearrange("k (h r) -> k h r", h=H)).then_inc(fold_in, 16)
            sp.dma_start(cT[:, 1], dram["ctxT"][:, 512:1024].rearrange("(c p) n -> p c n", p=P)).then_inc(c_in[1], 16)
            sp.dma_start(wuvT[:], dram["wuvT"].rearrange("(h p) n -> p h n", p=P)).then_inc(uv_in, 16)
            sp.dma_start(wo[:], dram["wo1"].rearrange("(h p) n -> p h n", p=P)).then_inc(uv_in, 16)
            for k in range(2, KB):
                sp.wait_ge(clo_done, k - 1)
                sp.dma_start(cT[:, k % 2], dram["ctxT"][:, k * 512:(k + 1) * 512].rearrange("(c p) n -> p c n", p=P)
                             ).then_inc(c_in[k % 2], 16)

        @block.gpsimd
        def _(pool):
            sg.give_credit(pool, POOL_S)
            pool.memset(mask[:], 0.0)
            pool.memset(vdiag[:], 0.0).then_inc(cleared, 1)
            def root(tile):
                need(pool, "d_var_done", tile + 1)
                pool.tensor_tensor(rstd[:], var[:], consts["minus_half"][:, 0:2], ALU.pow).then_inc(sg["d_rstd_done"], 1)

            def add_rope(n):
                need(pool, "d_rope_done", n + 1)
                need(pool, "d_qT_ready", 2 * n)
                pool.tensor_tensor(qf[:, :, KC:], qcos[:], qsin[:], ALU.add).then_inc(sg["d_qf_done"], 1)

            root(0)
            for k in range(KB):
                pool.wait_ge(kv_rope, k + 1)
                pool.tensor_tensor(kv[:, :, KC:], kvc[:], kvs[:], ALU.add).then_inc(kv_done, 1)
            add_rope(0)
            add_rope(1)
            with pool.Fori(0, NU // 8) as j:
                for k in range(8):
                    n = 8 * j + k
                    need(pool, "d_inv_done", n + 1)
                    pool.tensor_tensor(prob[:, k % 2], prob[:, k % 2], along(s_inv[:, k % 2], 2, SEQ), ALU.mult
                                       ).then_inc(sg["d_pn_done"], 1)
                    if k % 4 == 0:
                        root(2 * j + k // 4 + 1)
                    add_rope(n + 2)

        @block.scalar
        def _(act):
            sg.give_credit(act, ACT_S)
            act.wait_ge(misc_in, 64)
            act.activation(wdq_hi[:], wdq[:], ACT.Copy).then_inc(wsmall_hi, 1)
            act.wait_ge(wk_ready, 1)
            act.activation(wkv[:, :, KC:], m_ps[:, 0:CK * R].rearrange("p (c r) -> p c r", c=CK), ACT.Copy).then_inc(wk_done, 1)
            act.wait_ge(wk_done, 1)
            act.activation(wkv_hi[:], wkv[:], ACT.Copy).then_inc(wsmall_hi, 1)

            def split_context(k):
                act.wait_ge(c_in[k % 2], 16 * (k // 2 + 1))
                act.wait_ge(kv_ready, k)
                act.activation(cT_hi[:], cT[:, k % 2], ACT.Copy).then_inc(chi_done, 1)

            split_context(0)
            act.wait_ge(fold_in, 48)
            act.activation(wq_hi[:, :, KC:], wqr[:], ACT.Copy).then_inc(fold_hi, 1)
            for k in range(2):
                act.wait_ge(fold_ready, k + 1)
                act.activation(wq_hi[:, 8 * k:8 * k + 8, 0:KC], q_ps[0:QC, k].rearrange("p (h c) -> p h c", h=8), ACT.Copy
                               ).then_inc(fold_hi, 1)
            for k in range(H // 4):
                act.wait_ge(wn_ready, k + 1)
                act.activation(wn[:, 2 * k:2 * k + 2, :], (qT_ps if k % 2 == 0 else s_ps)[:].rearrange("p (g d) -> p g d", g=2),
                               ACT.Copy).then_inc(wn_done, 1)
            act.wait_ge(cleared, 1)
            for k in range(KB):
                act.wait_ge(kv_ready, k + 1)
                act.wait_ge(kvT_ready, k)
                ps = (t_ps if k % 2 == 0 else o_ps)[:].rearrange("p (t n) -> p t n", t=4)
                act.activation(kv[:, :, 0:KC], ps[:, :, 0:KC], ACT.Copy)
                for s in range(2):
                    last = act.activation(vdiag[s * SEQ:(s + 1) * SEQ, 4 * k:4 * k + 4, s * KC:(s + 1) * KC],
                                          ps[s * SEQ:(s + 1) * SEQ, :, 0:KC], ACT.Copy)
                last.then_inc(kv_act, 1)
                if k < KB - 1:
                    split_context(k + 1)
                act.wait_ge(kvT_ready, k + 1)
                act.activation(keysT[:, k * 512:(k + 1) * 512], out_ps[:], ACT.Copy).then_inc(kvT_done, 1)

            def norm_high(tile):
                need(act, "d_nT_ready", tile + 1)
                need(act, "d_qc_ready", tile)
                act.activation(xnT_hi[:], m_ps[:].rearrange("p (c t) -> p c t", c=CK), ACT.Copy).then_inc(sg["d_xhi_done"], 1)

            def qc_high(tile, par):
                need(act, "d_qc_ready", tile + 1)
                need(act, "d_q_ready", 4 * (tile - 1))
                act.activation(qcT_hi[:, par], m_ps[0:QC, 0:T], ACT.Copy).then_inc(sg["d_qchi_done"], 1)

            def absorbed(n):
                need(act, "d_q_ready", n + 1)
                need(act, "d_qT_ready", 2 * n)
                act.activation(qf[:, :, 0:KC], q_ps[:].rearrange("p b (h n) -> p (b h) n", n=P)[:, :, 0:KC], ACT.Copy
                               ).then_inc(sg["d_abs_done"], 1)

            def to_sequences(half, b):
                return (qT[:, b, 2 * half:2 * half + 2].rearrange("p q s h t -> p q h s t"),
                        qT_ps[:].rearrange("p (q h s t) -> p q h s t", q=2, h=2, s=2))

            def rowsT(n, b):
                need(act, "d_qT_ready", 2 * n + 1)
                need(act, "d_s_ready", n - 1)
                dst, src = to_sequences(0, b)
                for q in range(2):
                    last = act.activation(dst[:, q], src[:, q], ACT.Copy)
                last.then_inc(sg["d_qTa_done"], 1)

            def probs_out(m, b):
                need(act, "d_t_ready", m + 1)
                need(act, "d_pv_ready", m - 1)
                act.activation(probT[:, b], t_ps[:], ACT.Copy).then_inc(sg["d_pt_done"], 1)

            def attention_out(m, b):
                need(act, "d_pv_ready", m + 1)
                need(act, "d_out_ready", m - 1)
                src = o_ps[:].rearrange("p (q h t) -> p q h t", q=4, h=2)
                for s in range(2):
                    for hh in range(2):
                        last = act.activation(attT[hh * KC:(hh + 1) * KC, b, :, s * SEQ:(s + 1) * SEQ],
                                              src[s * KC:(s + 1) * KC, :, hh, :], ACT.Copy)
                last.then_inc(sg["d_ot_done"], 1)

            act.wait_ge(mask_done, 1)
            norm_high(0)
            qc_high(0, 0)
            absorbed(0)
            rowsT(0, 0)
            absorbed(1)
            with act.Fori(0, NU // 8) as j:
                for k in range(8):
                    n, b = 8 * j + k, k % 2
                    if k % 4 == 1:
                        norm_high(2 * j + k // 4 + 1)
                    if k % 4 == 2:
                        qc_high(2 * j + k // 4 + 1, 1 - k // 4)
                    need(act, "d_sub_done", n + 1)
                    need(act, "d_t_ready", n - 1)
                    act.activation(prob[:, b], sc[:, b], ACT.Exp, scale=SCALE).then_inc(sg["d_exp_done"], 1)
                    attention_out(n - 1, 1 - b)
                    rowsT(n + 1, 1 - b)
                    absorbed(n + 2)
                    probs_out(n, b)
            attention_out(NU - 1, 1)

        @block.vector
        def _(dve):
            sg.give_credit(dve, DVE_S)

            def row(r):
                return xres[:, X0 + r, :] if isinstance(r, int) else xres[:, ds(X0 + r, 1), :].rearrange("p a d -> p (a d)")

            def norm(tile):
                for t in range(2):
                    last = dve.bn_stats(bst[:, t], row(2 * tile + t))
                last.then_inc(sg["d_bst_done"], 1)
                need(dve, "d_bst_done", tile + 1)
                dve.memset(spare[:], 0.0)
                for t in range(2):
                    last = dve.bn_aggr(mv[:, t], bst[:, t])
                last.then_inc(sg["d_mv_done"], 1)
                need(dve, "d_mv_done", tile + 1)
                dve.tensor_scalar(var[:], mv[:, :, 1], 1e-5, None, ALU.add).then_inc(sg["d_var_done"], 1)
                need(dve, "d_rstd_done", tile + 1)
                for t in range(2):
                    last = dve.tensor_scalar(xn[:, t], row(2 * tile + t), mv[:, t, 0:1], rstd[:, t:t + 1],
                                             ALU.subtract, ALU.mult)
                last.then_inc(sg["d_xn_done"], 1)

            def norm_low(tile):
                need(dve, "d_xhi_done", tile + 1)
                dve.tensor_tensor(xnT_lo[:], m_ps[:].rearrange("p (c t) -> p c t", c=CK), xnT_hi[:].bitcast(F32),
                                  ALU.subtract).then_inc(sg["d_xlo_done"], 1)

            def qc_low(tile, par):
                need(dve, "d_qchi_done", tile + 1)
                dve.tensor_tensor(qcT_lo[:, par], m_ps[0:QC, 0:T], qcT_hi[:, par].bitcast(F32), ALU.subtract
                                  ).then_inc(sg["d_qclo_done"], 1)

            def rope(n):
                need(dve, "d_abs_done", n + 1)
                need(dve, "d_qf_done", n)
                q = q_ps[:].rearrange("p b (h n) -> p (b h) n", n=P)
                dve.tensor_tensor(qcos[:], q[:, :, KC:], along(cos_k[:], 1, 8), ALU.mult)
                dve.tensor_tensor(qsin[:, :, 0:HR], q[:, :, KC + HR:], along(sin_k[:, 0:HR], 1, 8), ALU.mult)
                dve.tensor_tensor(qsin[:, :, HR:], q[:, :, KC:KC + HR], along(sin_k[:, HR:], 1, 8), ALU.mult
                                  ).then_inc(sg["d_rope_done"], 1)

            def rowsT(n, b):
                need(dve, "d_qT_ready", 2 * n + 2)
                need(dve, "d_s_ready", n - 1)
                dst = qT[:, b, 2:4].rearrange("p q s h t -> p q h s t")
                src = qT_ps[:].rearrange("p (q h s t) -> p q h s t", q=2, h=2, s=2)
                for q in range(2):
                    last = dve.tensor_copy(dst[:, q], src[:, q])
                last.then_inc(sg["d_qTb_done"], 1)

            dve.wait_ge(seg_in, 32)
            dve.tensor_copy(seg[:], seg_i[:]).then_inc(mask_step, 1)
            dve.wait_ge(mask_step, 1)
            dve.tensor_scalar(seg_lo[:], seg[:], -8.0, None, ALU.add).then_inc(mask_step, 1)
            dve.memset(t_ps[:], 0.0)
            norm(0)
            dve.wait_ge(wsmall_hi, 1)
            dve.tensor_tensor(wdq_lo[:], wdq[:], wdq_hi[:].bitcast(F32), ALU.subtract).then_inc(wsmall_lo, 1)
            dve.wait_ge(wsmall_hi, 2)
            dve.tensor_tensor(wkv_lo[:], wkv[:], wkv_hi[:].bitcast(F32), ALU.subtract).then_inc(wsmall_lo, 1)

            def split_context(k):
                dve.wait_ge(chi_done, k + 1)
                dve.tensor_tensor(cT_lo[:], cT[:, k % 2], cT_hi[:].bitcast(F32), ALU.subtract).then_inc(clo_done, 1)

            split_context(0)
            dve.wait_ge(fold_hi, 1)
            dve.tensor_tensor(wq_lo[:, :, KC:], wqr[:], wq_hi[:, :, KC:].bitcast(F32), ALU.subtract).then_inc(fold_lo, 1)
            for k in range(2):
                dve.wait_ge(fold_hi, k + 2)
                dve.tensor_tensor(wq_lo[:, 8 * k:8 * k + 8, 0:KC], q_ps[0:QC, k].rearrange("p (h c) -> p h c", h=8),
                                  wq_hi[:, 8 * k:8 * k + 8, 0:KC].bitcast(F32), ALU.subtract).then_inc(fold_lo, 1)
            dve.wait_ge(tab_in, 32)
            for k in range(KB):
                dve.wait_ge(kv_act, k + 1)
                dve.wait_ge(kv_done, k)
                ps = (t_ps if k % 2 == 0 else o_ps)[:].rearrange("p (t n) -> p t n", t=4)
                dve.tensor_tensor(kvc[:], ps[:, :, KC:], along(cos_k[:], 1, 4), ALU.mult)
                dve.tensor_tensor(kvs[:, :, 0:HR], ps[:, :, KC + HR:], along(sin_k[:, 0:HR], 1, 4), ALU.mult)
                dve.tensor_tensor(kvs[:, :, HR:], ps[:, :, KC:KC + HR], along(sin_k[:, HR:], 1, 4), ALU.mult
                                  ).then_inc(kv_rope, 1)
                if k < KB - 1:
                    split_context(k + 1)
            dve.wait_ge(mask_step, 2)
            dve.tensor_tensor(bad[:], along(key_no[:], 1, NSEQ), along(seg[:], 2, SEQ), ALU.is_gt)
            dve.tensor_tensor(bad2[:], along(key_no[:], 1, NSEQ), along(seg_lo[:], 2, SEQ), ALU.is_lt).then_inc(mask_step, 1)
            dve.wait_ge(mask_step, 3)
            dve.tensor_tensor(bad[:], bad[:], bad2[:], ALU.add).then_inc(mask_step, 1)
            dve.wait_ge(mask_step, 4)
            dve.wait_ge(cleared, 1)
            dve.tensor_scalar(mask[0:SEQ], bad[:], MASKED, None, ALU.mult)
            dve.wait_ge(kvT_done, KB)
            dve.memset(t_ps[:], 0.0)
            dve.memset(o_ps[:], 0.0).then_inc(mask_done, 1)
            norm_low(0)
            qc_low(0, 0)
            rope(0)
            rowsT(0, 0)
            rope(1)
            with dve.Fori(0, NU // 8) as j:
                for k in range(8):
                    n, b = 8 * j + k, k % 2
                    if k % 2 == 0:
                        with dve.If(j > 0) if k < 4 else nullcontext():
                            need(dve, "d_out_ready", n - 2)
                            r = 4 * j + k // 2
                            dve.tensor_tensor(xres[:, ds(r, 1), :].rearrange("p a d -> p (a d)"), out_ps[:, 0:D],
                                              xres[:, ds(r, 1), :].rearrange("p a d -> p (a d)"), ALU.add
                                              ).then_inc(sg["d_x_done"], 1)
                        need(dve, "d_pv_ready", n - 2)
                        dve.tensor_scalar(vcur[:, (k // 2) % 2], vdiag[:, ds(4 * j + k // 2, 1), :].rearrange("p a d -> p (a d)"),
                                          1.0, None, ALU.mult).then_inc(sg["d_v_done"], 1)
                    if k % 4 == 1:
                        norm_low(2 * j + k // 4 + 1)
                    if k % 4 == 2:
                        qc_low(2 * j + k // 4 + 1, 1 - k // 4)
                    need(dve, "d_s_ready", n + 1)
                    s3 = s_ps[:].rearrange("p (g k) -> p g k", g=8)
                    dve.tensor_reduce(s_max[:], s3, AX, ALU.max).then_inc(sg["d_max_done"], 1)
                    need(dve, "d_max_done", n + 1)
                    need(dve, "d_exp_done", n - 1)
                    dve.tensor_tensor(sc[:, b], s3, along(s_max[:], 2, SEQ), ALU.subtract).then_inc(sg["d_sub_done"], 1)
                    need(dve, "d_exp_done", n + 1)
                    dve.tensor_reduce(s_sum[:], prob[:, b], AX, ALU.add).then_inc(sg["d_sum_done"], 1)
                    need(dve, "d_sum_done", n + 1)
                    need(dve, "d_pn_done", n - 1)
                    dve.reciprocal(s_inv[:, b], s_sum[:]).then_inc(sg["d_inv_done"], 1)
                    if k % 4 == 0:
                        norm(2 * j + k // 4 + 1)
                    rowsT(n + 1, 1 - b)
                    rope(n + 2)
            for t in range(2):
                need(dve, "d_out_ready", NU - 2 + 2 * t)
                dve.tensor_tensor(xres[:, X0 + TT - 2 + t, :], out_ps[:, 0:D], xres[:, X0 + TT - 2 + t, :], ALU.add
                                  ).then_inc(sg["d_x_done"], 1)

        @block.tensor
        def _(pe):
            sg.give_credit(pe, PE_S)
            ident = consts["ident"]
            pe.wait_ge(misc_in, 64)
            for c in range(CK):
                last = pe.matmul(m_ps[:, c * R:(c + 1) * R], wkvcT[:, c * P:(c + 1) * P], wkr[:], start=True, stop=True)
            last.then_inc(wk_ready, 1)
            pe.wait_ge(fold_in, 48)
            for k in range(2):
                for h in range(8):
                    last = pe.matmul(q_ps[0:QC, k, h * KC:(h + 1) * KC], wuqT[:, 8 * k + h], wukT[:, 8 * k + h], start=True, stop=True)
                last.then_inc(fold_ready, 1)
            pe.wait_ge(uv_in, 32)
            for k in range(H // 4):
                if k >= 2:
                    pe.wait_ge(wn_done, k - 1)
                for g in range(2):
                    for hh in range(2):
                        h = 4 * k + 2 * g + hh
                        last = pe.matmul((qT_ps if k % 2 == 0 else s_ps)[hh * KC:(hh + 1) * KC, g * D:(g + 1) * D],
                                         wuvT[:, h], wo[:, h], start=True, stop=True, skip_group_check=True)
                last.then_inc(wn_ready, 1)
            pe.wait_ge(wsmall_lo, 2)
            def keys_of(k):
                pe.wait_ge(clo_done, k + 1)
                if k >= 2:
                    pe.wait_ge(kv_rope, k - 1)
                ps = t_ps if k % 2 == 0 else o_ps
                for t in range(4):
                    for c in range(CK):
                        last = matmul3(pe, ps[:, t * P:(t + 1) * P], (cT_hi[:, c, t * P:(t + 1) * P], cT_lo[:, c, t * P:(t + 1) * P]),
                                       (wkv_hi[:, c], wkv_lo[:, c]), c == 0, c == CK - 1)
                last.then_inc(kv_ready, 1)

            for k in range(KB):
                keys_of(k)
                pe.wait_ge(kv_done, k + 1)
                pe.wait_ge(kvT_done, k)
                for t in range(4):
                    last = pe.transpose(out_ps[:, t * P:(t + 1) * P], kv[:, t], ident[:])
                last.then_inc(kvT_ready, 1)

            def transpose_norm(tile):
                need(pe, "d_xn_done", tile + 1)
                need(pe, "d_qclo_done", tile)
                for c in range(CK):
                    for t in range(2):
                        last = pe.transpose(m_ps[:, c * T + t * P:c * T + (t + 1) * P], xn[:, t, c * P:(c + 1) * P], ident[:])
                last.then_inc(sg["d_nT_ready"], 1)

            def compress(tile):
                need(pe, "d_xlo_done", tile + 1)
                for c in range(CK):
                    last = matmul3(pe, m_ps[0:QC, 0:T], (wdq_hi[:, c], wdq_lo[:, c]), (xnT_hi[:, c], xnT_lo[:, c]),
                                   c == 0, c == CK - 1)
                last.then_inc(sg["d_qc_ready"], 1)

            def queries(n, tile, par, u):
                t, half = u // 2, u % 2
                need(pe, "d_qclo_done", tile + 1)
                need(pe, "d_rope_done", n)
                for g in range(2):
                    last = matmul3(pe, q_ps[:, g], (qcT_hi[:, par, t * P:(t + 1) * P], qcT_lo[:, par, t * P:(t + 1) * P]),
                                   (wq_hi[:, 8 * half + 4 * g:8 * half + 4 * g + 4].rearrange("p h n -> p (h n)"),
                                    wq_lo[:, 8 * half + 4 * g:8 * half + 4 * g + 4].rearrange("p h n -> p (h n)")), True, True)
                last.then_inc(sg["d_q_ready"], 1)

            def transpose_q(n, half):
                if half == 0:
                    need(pe, "d_qf_done", n + 1)
                    need(pe, "d_qTb_done", n)
                else:
                    need(pe, "d_qTa_done", n + 1)
                for h in range(4):
                    last = pe.transpose(qT_ps[:, h * P:(h + 1) * P], qf[:, 4 * half + h], ident[:])
                last.then_inc(sg["d_qT_ready"], 1)

            def scores(n, seq0, b):
                need(pe, "d_qTb_done", n + 1)
                need(pe, "d_qTa_done", n + 1)
                need(pe, "d_sub_done", n)
                for q in range(4):
                    for s in range(2):
                        pe.matmul(s_ps[:, q * P + s * SEQ:q * P + (s + 1) * SEQ], qT[:, b, q, s],
                                  keysT[:, ds((seq0 + s) * SEQ, SEQ)], start=(s == 0), stop=False, skip_group_check=True)
                    last = pe.matmul(s_ps[:, q * P:(q + 1) * P], consts["mask_rows"][:],
                                     mask[:, ds(seq0, 2), :], start=False, stop=True,
                                     skip_group_check=True)
                last.then_inc(sg["d_s_ready"], 1)

            def transpose_probs(m, b):
                need(pe, "d_pn_done", m + 1)
                need(pe, "d_pt_done", m)
                for q in range(4):
                    last = pe.transpose(t_ps[:, q * P:(q + 1) * P], prob[:, b, 2 * q:2 * q + 2].rearrange("p g k -> p (g k)"),
                                        ident[:])
                last.then_inc(sg["d_t_ready"], 1)

            def attend(m, b, tile_par, tiles):
                need(pe, "d_pt_done", m + 1)
                need(pe, "d_ot_done", m)
                need(pe, "d_v_done", tiles)
                pe.matmul(o_ps[:], vcur[:, tile_par], probT[:, b], start=True, stop=True).then_inc(sg["d_pv_ready"], 1)

            def project_out(m, b, x_count):
                need(pe, "d_ot_done", m + 1)
                if b == 0:
                    need(pe, "d_x_done", x_count)
                for q in range(4):
                    last = pe.matmul(out_ps[:, 0:D], attT[:, b, q], wn[:, 4 * b + q], start=(b == 0 and q == 0),
                                     stop=(b == 1 and q == 3))
                last.then_inc(sg["d_out_ready"], 1)

            pe.wait_ge(fold_lo, 3)
            pe.wait_ge(wn_done, H // 4)
            pe.wait_ge(mask_done, 1)
            transpose_norm(0)
            compress(0)
            queries(0, 0, 0, 0)
            transpose_q(0, 0)
            transpose_q(0, 1)
            queries(1, 0, 0, 1)
            with pe.Fori(0, NU // 8) as j:
                for k in range(8):
                    n, b = 8 * j + k, k % 2
                    tok = 4 * j + k // 2
                    k2 = k + 2
                    scores(n, 2 * tok, b)
                    with pe.If(j > 0) if k == 0 else nullcontext():
                        attend(n - 1, 1 - b, ((k - 1) // 2) % 2, 4 * j + (k + 1) // 2)
                    with pe.If(j > 0) if k < 2 else nullcontext():
                        project_out(n - 2, b, 4 * j + k // 2 - 1)
                    transpose_q(n + 1, 0)
                    queries(n + 2, 2 * j + k2 // 4, (k2 // 4) % 2, k2 % 4)
                    transpose_q(n + 1, 1)
                    transpose_probs(n, b)
                    if k % 4 == 0:
                        transpose_norm(2 * j + k // 4 + 1)
                    if k % 4 == 1:
                        compress(2 * j + k // 4 + 1)
            attend(NU - 1, 1, 1, TT)
            project_out(NU - 2, 0, TT - 1)
            project_out(NU - 1, 1, TT - 1)


def set_constants(nc, dram, consts, xres):
    with ExitStack() as ctx:
        taken = Taken(nc, ctx)
        raw = ctx.enter_context(nc.sbuf_tensor("c_raw", [P, P + SEQ], F32))
        c_in = taken.take("const_in")
        made = taken.take("const_made")
        block = ctx.enter_context(nc.Block())

        @block.sync
        def _(sp):
            sp.dma_start(raw[:, 0:P], dram["mask_rows"]).then_inc(c_in, 16)
            sp.dma_start(raw[:, P:], dram["causal"]).then_inc(c_in, 16)
            sp.dma_start(consts["ident"][:], dram["ident"]).then_inc(c_in, 16)

        @block.vector
        def _(dve):
            dve.memset(consts["ones"][:], 1.0)
            dve.memset(consts["minus_half"][:], -0.5)
            dve.memset(xres[:, X0 + TT:, :], 0.0)
            dve.wait_ge(c_in, 48)
            dve.tensor_copy(consts["mask_rows"][:], raw[:, 0:P])
            dve.tensor_copy(consts["causal"][:], raw[:, P:]).then_inc(made, 1)
            dve.wait_ge(made, 1)


PHASES = (0, 1, 2, 3)


M0 = 2 * P


def layer1_ffn(nc, dram, xres, consts):
    with ExitStack() as ctx:
        yT_hi = ctx.enter_context(nc.sbuf_tensor("yT_hi", [P, CK, NTOK + T], F32R))
        yT_lo = ctx.enter_context(nc.sbuf_tensor("yT_lo", [P, CK, NTOK + T], F32R))
        modT = ctx.enter_context(nc.sbuf_tensor("modT", [P, M0 + NTOK + T], F32R))
        layer1_modulation(nc, dram, xres, consts, yT_hi, yT_lo, modT)
        layer1_mlp(nc, dram, xres, consts, yT_hi, yT_lo, modT)


def layer1_modulation(nc, dram, xres, consts, yT_hi, yT_lo, modT):
    RA, HW = 16, 16
    NU = 2 * TT
    HA = 4
    SCALE = 1.0 / HW ** 0.5
    with ExitStack() as ctx:
        taken = Taken(nc, ctx)
        def sb(name, shape, dt=F32):
            return ctx.enter_context(nc.sbuf_tensor(name, shape, dt))

        def sem(name):
            return taken.take(name)

        wqk = sb("e_wqk", [P, 2, CK, D])
        wv = sb("e_wv", [P, CK, D])
        wof = sb("e_wof", [P, CK, D])
        wa = sb("e_wa", [P, CK, RA])
        ln1 = sb("e_ln1", [P, CK])
        ln2 = sb("e_ln2", [P, CK])
        heads = sb("e_heads", [P, 8])
        same_head = sb("e_same_head", [P, CK, H])
        g_sb = sb("e_g", [P, CK, RA])
        gx = sb("e_gx", [P, CK, H, RA])
        qk_hi = sb("e_qk_hi", [P, 2, CK, D], F32R)
        qk_lo = sb("e_qk_lo", [P, 2, CK, D], F32R)
        wu_hi = sb("e_wu_hi", [P, CK, D], F32R)
        wu_lo = sb("e_wu_lo", [P, CK, D], F32R)
        wu_f = sb("e_wu_f", [P, CK, D])
        wa_hi = sb("e_wa_hi", [P, CK, RA], F32R)
        wa_lo = sb("e_wa_lo", [P, CK, RA], F32R)

        bst = sb("e_bst", [P, 2, 6])
        mv = sb("e_mv", [P, 2, 2])
        var = sb("e_var", [P, 2])
        rstd = sb("e_rstd", [P, 2])
        ms1 = sb("e_ms1", [P, 2])
        ms2 = sb("e_ms2", [P, 2])
        ms3 = sb("e_ms3", [P, 2])
        rrms = sb("e_rrms", [P, 2])
        tiny = sb("e_tiny", [P, 2])
        spare = sb("e_spare", [P, 1])
        y = sb("e_y", [P, 2, D])
        yh = sb("e_yh", [P, 2, D])
        yt_hi = sb("e_yt_hi", [P, 2, CK, T], F32R)
        yt_lo = sb("e_yt_lo", [P, 2, CK, T], F32R)
        qd = sb("e_qd", [P, 2, CK, T])
        kd = sb("e_kd", [P, 2, CK, T])
        qm = sb("e_qm", [P, 2, 2, 8, SEQ])
        ub = sb("e_ub", [P, 2, 2, H, 64])
        ha = sb("e_ha", [RA, 2, T])
        s_max = sb("e_s_max", [P, 8])
        s_sum = sb("e_s_sum", [P, 8])
        s_inv = sb("e_s_inv", [P, 2, 8])
        sc = sb("e_sc", [P, 2, 8, SEQ])
        prob = sb("e_prob", [P, 2, 8, SEQ])
        probT = sb("e_probT", [P, 2, 512])
        th = sb("e_th", [RA, 2, SEQ])
        mod = sb("e_mod", [RA, P])

        def bank(name):
            return ctx.enter_context(nc.psum_tensor(name, [P, 512], F32))

        s_ps = [bank("e_ps_s0"), bank("e_ps_s1")]
        q_ps, k_ps, m_ps, t_ps, u_ps = (bank("e_ps_" + n) for n in ("q", "k", "m", "t", "u"))
        w_ps = k_ps

        PE_S = ["e_nT_ready", "e_q_ready", "e_k_ready", "e_u_ready", "e_ha_ready", "e_s_ready", "e_t_ready", "e_mod_ready"]
        ACT_S = ["e_yhi_done", "e_q_done", "e_k_done", "e_u_done", "e_ha_done", "e_exp_done", "e_pt_done", "e_tanh_done", "e_qma_done"]
        DVE_S = ["e_bst_done", "e_mv_done", "e_var_done", "e_y_done", "e_yh_done", "e_ylo_done", "e_max_done", "e_sub_done",
                 "e_sum_done", "e_inv_done", "e_prod_done", "e_modhi_done", "e_mod_done"]
        POOL_S = ["e_rstd_done", "e_ms1_done", "e_ms2_done", "e_ms3_done", "e_rrms_done", "e_x_done", "e_qm_done", "e_pn_done"]
        SP_S = ["e_saved"]
        sg = Signals(taken, PE_S + ACT_S + DVE_S + POOL_S, less=("e_pt_done", "e_tanh_done"))
        need = sg.need
        w_in, small_in = sem("e_w_in"), sem("e_small_in")
        cleared, gx_done, g_ready, g_done, wu_ready = sem("e_cleared"), sem("e_gx_done"), sem("e_g_ready"), sem("e_g_done"), sem("e_wu_ready")
        whi_done, wlo_done = sem("e_whi_done"), sem("e_wlo_done")
        saved = [sem("e_saved0"), sem("e_saved1")]

        block = ctx.enter_context(nc.Block())

        @block.sync
        def _(sp):
            sp.dma_start(ln1[:], dram["ln1_w"]).then_inc(small_in, 16)
            sp.dma_start(ln2[:], dram["ln2_w"]).then_inc(small_in, 16)
            sp.dma_start(heads[:], dram["heads"]).then_inc(small_in, 16)
            sp.dma_start(same_head[:], dram["same_head"].rearrange("(c p) n -> p c n", p=P)).then_inc(small_in, 16)
            sp.dma_start(wof[:], dram["wo_f"].rearrange("(c p) n -> p c n", p=P)).then_inc(w_in, 16)
            sp.dma_start(wa[:], dram["wa"].rearrange("(c p) n -> p c n", p=P)).then_inc(w_in, 16)
            sp.dma_start(wv[:], dram["wv_f"].rearrange("(c p) n -> p c n", p=P)).then_inc(w_in, 16)
            for k, name in enumerate(("wqT_f", "wkT_f")):
                sp.dma_start(wqk[:, k], dram[name].rearrange("(c p) n -> p c n", p=P)).then_inc(w_in, 16)
            for k in range(2):
                sp.sem_inc(saved[k], 32)
            with sp.Fori(0, NT // 2) as j:
                for a in range(2):
                    need(sp, "e_ylo_done", 2 * j + a + 1)
                    sp.dma_start(yT_hi[:, :, ds((2 * j + a) * T, T)].bitcast(F32), yt_hi[:, a].bitcast(F32)).then_inc(saved[a], 16)
                    sp.dma_start(yT_lo[:, :, ds((2 * j + a) * T, T)].bitcast(F32), yt_lo[:, a].bitcast(F32)).then_inc(saved[a], 16)
            for k in range(2):
                sp.wait_ge(saved[k], 32 * (NT // 2 + 1))

        @block.gpsimd
        def _(pool):
            sg.give_credit(pool, POOL_S)
            pool.memset(ub[:], 0.0)
            pool.memset(modT[:].bitcast(F32), 0.0).then_inc(cleared, 1)

            def root_var(tile):
                need(pool, "e_var_done", tile + 1)
                pool.tensor_tensor(rstd[:], var[:], consts["minus_half"][:, 0:2], ALU.pow).then_inc(sg["e_rstd_done"], 1)

            def root_square(tile):
                need(pool, "e_rstd_done", tile + 1)
                pool.tensor_tensor(ms1[:], mv[:, :, 1], rstd[:], ALU.mult).then_inc(sg["e_ms1_done"], 1)
                need(pool, "e_ms1_done", tile + 1)
                pool.tensor_tensor(ms2[:], ms1[:], rstd[:], ALU.mult).then_inc(sg["e_ms2_done"], 1)
                need(pool, "e_ms2_done", tile + 1)
                pool.tensor_tensor(ms3[:], ms2[:], tiny[:], ALU.add).then_inc(sg["e_ms3_done"], 1)
                need(pool, "e_ms3_done", tile + 1)
                pool.tensor_tensor(rrms[:], ms3[:], consts["minus_half"][:, 0:2], ALU.pow).then_inc(sg["e_rrms_done"], 1)

            def add_y(tile):
                need(pool, "e_y_done", tile + 1)
                rows = xres[:, ds(X0 + 2 * tile, 2), :] if not isinstance(tile, int) else xres[:, X0 + 2 * tile:X0 + 2 * tile + 2, :]
                pool.tensor_tensor(rows, rows, y[:], ALU.add).then_inc(sg["e_x_done"], 1)

            def mask_heads(n, tile, par, u, b):
                t, half = u // 2, u % 2
                need(pool, "e_q_done", tile + 1)
                need(pool, "e_s_ready", n - 1)
                for s in range(2):
                    at = t * P + s * SEQ
                    last = pool.tensor_tensor(qm[:, b, s, HA:], along(qd[:, par, half, at:at + SEQ], 1, 8 - HA),
                                              along(heads[:, HA:], 2, SEQ), ALU.mult)
                last.then_inc(sg["e_qm_done"], 1)

            pool.wait_ge(whi_done, 1)
            root_var(0)
            root_square(0)
            add_y(0)
            mask_heads(0, 0, 0, 0, 0)
            with pool.Fori(0, NU // 8) as j:
                for k in range(8):
                    n, b = 8 * j + k, k % 2
                    tile = 2 * j + k // 4
                    if k % 4 == 0:
                        root_var(tile + 1)
                    k1 = k + 1
                    mask_heads(n + 1, 2 * j + k1 // 4, (k1 // 4) % 2, k1 % 4, 1 - b)
                    if k % 4 == 0:
                        root_square(tile + 1)
                    if k % 4 == 1:
                        add_y(tile + 1)
                    need(pool, "e_inv_done", n + 1)
                    pool.tensor_tensor(prob[:, b], prob[:, b], along(s_inv[:, b], 2, SEQ), ALU.mult).then_inc(sg["e_pn_done"], 1)

        @block.scalar
        def _(act):
            sg.give_credit(act, ACT_S)
            act.wait_ge(g_ready, 1)
            act.activation(g_sb[:], w_ps[:, 0:CK * RA].rearrange("p (c r) -> p c r", c=CK), ACT.Copy).then_inc(g_done, 1)
            act.wait_ge(small_in, 64)
            act.wait_ge(w_in, 80)
            for c in range(CK):
                act.activation(qk_hi[:, :, c], wqk[:, :, c], ACT.Copy, scale=ln1[:, c:c + 1])
                last = act.activation(wa_hi[:, c], wa[:, c], ACT.Copy, scale=ln2[:, c:c + 1])
            last.then_inc(whi_done, 1)
            act.wait_ge(wu_ready, 1)
            for c in range(CK):
                last = act.activation(wu_f[:, c], w_ps[:, c * D:(c + 1) * D], ACT.Copy, scale=ln1[:, c:c + 1])
            last.then_inc(g_done, 1)
            act.wait_ge(g_done, 2)
            act.activation(wu_hi[:], wu_f[:], ACT.Copy).then_inc(whi_done, 1)

            def high(tile, par):
                need(act, "e_nT_ready", tile + 1)
                need(act, "e_ha_ready", tile - 1)
                act.wait_ge(saved[par], 16 * (tile - par) + 32)
                act.activation(yt_hi[:, par], m_ps[:].rearrange("p (c t) -> p c t", c=CK), ACT.Copy
                               ).then_inc(sg["e_yhi_done"], 1)

            def copy_q(tile, par):
                need(act, "e_q_ready", tile + 1)
                need(act, "e_qm_done", 4 * (tile - 1))
                act.activation(qd[:, par], q_ps[:].rearrange("p (c t) -> p c t", c=CK), ACT.Copy).then_inc(sg["e_q_done"], 1)

            def copy_k(tile, par):
                need(act, "e_k_ready", tile + 1)
                need(act, "e_s_ready", 4 * (tile - 1))
                act.activation(kd[:, par], k_ps[:].rearrange("p (c t) -> p c t", c=CK), ACT.Copy).then_inc(sg["e_k_done"], 1)

            def copy_u(tile, par):
                need(act, "e_u_ready", tile + 1)
                need(act, "e_mod_ready", 4 * (tile - 1))
                src = m_ps[:].rearrange("p (t h r) -> p t h r", t=2, h=H)
                for s in range(2):
                    last = act.activation(ub[s * SEQ:(s + 1) * SEQ, par, :, :, 32 * s:32 * s + RA], src[s * SEQ:(s + 1) * SEQ],
                                          ACT.Copy)
                last.then_inc(sg["e_u_done"], 1)

            def copy_ha(tile, par):
                need(act, "e_ha_ready", tile + 1)
                need(act, "e_prod_done", 2 * (tile - 1))
                act.activation(ha[:, par], m_ps[0:RA, 0:T], ACT.Copy, scale=0.1).then_inc(sg["e_ha_done"], 1)

            def copy_probs(m, b):
                need(act, "e_t_ready", m + 1)
                need(act, "e_mod_ready", m - 1)
                act.activation(probT[:, b], t_ps[:], ACT.Copy).then_inc(sg["e_pt_done"], 1)

            def tanh(tok):
                need(act, "e_mod_ready", 2 * tok + 2)
                need(act, "e_prod_done", tok)
                for s in range(2):
                    last = act.activation(th[:, s], u_ps[32 * s:32 * s + RA, 0:SEQ], ACT.Tanh)
                last.then_inc(sg["e_tanh_done"], 1)

            def mask_heads(n, tile, par, u, b):
                t, half = u // 2, u % 2
                need(act, "e_q_done", tile + 1)
                need(act, "e_s_ready", n - 1)
                for h in range(HA):
                    last = act.activation(qm[:, b, :, h], qd[:, par, half, t * P:(t + 1) * P].rearrange("p (s t) -> p s t", s=2),
                                          ACT.Copy, scale=heads[:, h:h + 1])
                last.then_inc(sg["e_qma_done"], 1)

            act.wait_ge(cleared, 2)
            high(0, 0)
            copy_q(0, 0)
            copy_k(0, 0)
            mask_heads(0, 0, 0, 0, 0)
            copy_u(0, 0)
            with act.Fori(0, NU // 8) as j:
                for k in range(8):
                    n, b = 8 * j + k, k % 2
                    tile, nxt = 2 * j + k // 4, 1 - k // 4
                    k1 = k + 1
                    mask_heads(n + 1, 2 * j + k1 // 4, (k1 // 4) % 2, k1 % 4, 1 - b)
                    need(act, "e_sub_done", n + 1)
                    need(act, "e_t_ready", n - 1)
                    act.activation(prob[:, b], sc[:, b], ACT.Exp, scale=SCALE).then_inc(sg["e_exp_done"], 1)
                    copy_probs(n - 1, 1 - b)
                    if b == 1:
                        tanh(4 * j + (k - 3) // 2)
                    if k % 4 == 0:
                        copy_ha(tile, k // 4)
                    if k % 4 == 1:
                        high(tile + 1, nxt)
                    if k % 4 == 2:
                        copy_q(tile + 1, nxt)
                        copy_k(tile + 1, nxt)
                    if k % 4 == 3:
                        copy_u(tile + 1, nxt)
            copy_probs(NU - 1, 1)
            tanh(TT - 1)

        @block.vector
        def _(dve):
            sg.give_credit(dve, DVE_S)
            dve.memset(u_ps[:], 0.0)
            dve.memset(t_ps[:], 0.0)
            dve.memset(tiny[:], 1e-6).then_inc(cleared, 1)

            def row(r):
                return xres[:, X0 + r, :] if isinstance(r, int) else xres[:, ds(X0 + r, 1), :].rearrange("p a d -> p (a d)")

            def norm_stats(tile):
                for t in range(2):
                    last = dve.bn_stats(bst[:, t], row(2 * tile + t))
                last.then_inc(sg["e_bst_done"], 1)
                need(dve, "e_bst_done", tile + 1)
                dve.memset(spare[:], 0.0)
                for t in range(2):
                    last = dve.bn_aggr(mv[:, t], bst[:, t])
                last.then_inc(sg["e_mv_done"], 1)
                need(dve, "e_mv_done", tile + 1)
                dve.tensor_scalar(var[:], mv[:, :, 1], 1e-5, None, ALU.add).then_inc(sg["e_var_done"], 1)

            def norm_rows(tile):
                need(dve, "e_rstd_done", tile + 1)
                need(dve, "e_x_done", tile)
                for t in range(2):
                    last = dve.tensor_scalar(y[:, t], row(2 * tile + t), mv[:, t, 0:1], rstd[:, t:t + 1],
                                             ALU.subtract, ALU.mult)
                last.then_inc(sg["e_y_done"], 1)

            def rms_rows(tile):
                need(dve, "e_y_done", tile + 1)
                need(dve, "e_rrms_done", tile + 1)
                for t in range(2):
                    last = dve.tensor_scalar(yh[:, t], y[:, t], rrms[:, t:t + 1], None, ALU.mult)
                last.then_inc(sg["e_yh_done"], 1)

            def low(tile, par):
                need(dve, "e_yhi_done", tile + 1)
                dve.tensor_tensor(yt_lo[:, par], m_ps[:].rearrange("p (c t) -> p c t", c=CK), yt_hi[:, par].bitcast(F32),
                                  ALU.subtract).then_inc(sg["e_ylo_done"], 1)

            def modulation(tok, col, par, t):
                need(dve, "e_mod_done", tok)
                need(dve, "e_tanh_done", tok + 1)
                dve.tensor_tensor(mod[:], th[:].rearrange("p s t -> p (s t)"), ha[:, par, t * P:(t + 1) * P], ALU.mult
                                  ).then_inc(sg["e_prod_done"], 1)
                at = ds(col, P) if not isinstance(col, int) else slice(col, col + P)
                need(dve, "e_prod_done", tok + 1)
                dve.tensor_scalar(modT[0:RA, at], mod[:], 1.0, None, ALU.mult)
                dve.tensor_scalar(modT[64:64 + RA, at], mod[:], 1.0, None, ALU.mult).then_inc(sg["e_modhi_done"], 1)
                need(dve, "e_modhi_done", tok + 1)
                dve.tensor_tensor(modT[32:32 + RA, at], mod[:], modT[0:RA, at].bitcast(F32), ALU.subtract
                                  ).then_inc(sg["e_mod_done"], 1)

            norm_stats(0)
            dve.wait_ge(g_done, 1)
            dve.wait_ge(small_in, 64)
            dve.tensor_tensor(gx[:], along(g_sb[:], 2, H), along(same_head[:], 3, RA), ALU.mult).then_inc(gx_done, 1)
            dve.wait_ge(whi_done, 1)
            for c in range(CK):
                for k in range(2):
                    dve.scalar_tensor_tensor(qk_lo[:, k, c], wqk[:, k, c], ln1[:, c:c + 1], qk_hi[:, k, c].bitcast(F32),
                                             ALU.mult, ALU.subtract)
                dve.scalar_tensor_tensor(wa_lo[:, c], wa[:, c], ln2[:, c:c + 1], wa_hi[:, c].bitcast(F32), ALU.mult, ALU.subtract)
            dve.wait_ge(whi_done, 2)
            dve.tensor_tensor(wu_lo[:], wu_f[:], wu_hi[:].bitcast(F32), ALU.subtract).then_inc(wlo_done, 1)
            norm_rows(0)
            rms_rows(0)
            dve.wait_ge(cleared, 2)
            low(0, 0)
            with dve.Fori(0, NU // 8) as j:
                for k in range(8):
                    n, b = 8 * j + k, k % 2
                    tile, nxt = 2 * j + k // 4, 1 - k // 4
                    if b == 1:
                        with dve.If(j > 0) if k < 4 else nullcontext():
                            tok = 4 * j + k // 2 - 2
                            modulation(tok, (4 * j + k // 2) * P, (k // 4 + 1) % 2, (k // 2) % 2)
                    if k % 4 == 0:
                        norm_stats(tile + 1)
                    if k % 4 == 1:
                        rms_rows(tile + 1)
                    if k % 4 == 2:
                        low(tile + 1, nxt)
                    need(dve, "e_s_ready", n + 1)
                    s3 = s_ps[b][:].rearrange("p (g k) -> p g k", g=8)
                    dve.tensor_reduce(s_max[:], s3, AX, ALU.max).then_inc(sg["e_max_done"], 1)
                    need(dve, "e_max_done", n + 1)
                    need(dve, "e_exp_done", n - 1)
                    dve.tensor_tensor(sc[:, b], s3, along(s_max[:], 2, SEQ), ALU.subtract).then_inc(sg["e_sub_done"], 1)
                    if k % 4 == 0:
                        norm_rows(tile + 1)
                    need(dve, "e_exp_done", n + 1)
                    dve.tensor_reduce(s_sum[:], prob[:, b], AX, ALU.add).then_inc(sg["e_sum_done"], 1)
                    need(dve, "e_sum_done", n + 1)
                    need(dve, "e_pn_done", n - 1)
                    dve.reciprocal(s_inv[:, b], s_sum[:]).then_inc(sg["e_inv_done"], 1)
            for t in range(2):
                modulation(TT - 2 + t, M0 + (TT - 2 + t) * P, 1, t)

        @block.tensor
        def _(pe):
            sg.give_credit(pe, PE_S)
            pe.wait_ge(w_in, 80)
            for c in range(CK):
                for i in range(CK):
                    last = pe.matmul(w_ps[:, c * RA:(c + 1) * RA], wof[:, i, c * P:(c + 1) * P], wa[:, i], start=(i == 0),
                                     stop=(i == CK - 1))
            last.then_inc(g_ready, 1)
            pe.wait_ge(gx_done, 1)
            for c in range(CK):
                for i in range(CK):
                    last = pe.matmul(w_ps[:, c * D:(c + 1) * D], wv[:, i, c * P:(c + 1) * P],
                                     gx[:, i].rearrange("p h r -> p (h r)"), start=(i == 0), stop=(i == CK - 1))
            last.then_inc(wu_ready, 1)

            def transpose_norm(tile):
                need(pe, "e_yh_done", tile + 1)
                need(pe, "e_ha_done", tile)
                for c in range(CK):
                    for t in range(2):
                        last = pe.transpose(m_ps[:, c * T + t * P:c * T + (t + 1) * P], yh[:, t, c * P:(c + 1) * P],
                                            consts["ident"][:])
                last.then_inc(sg["e_nT_ready"], 1)

            def project_qk(which, tile, par):
                if which == 0:
                    need(pe, "e_ylo_done", tile + 1)
                    need(pe, "e_q_done", tile)
                else:
                    need(pe, "e_ylo_done", tile + 1)
                    need(pe, "e_k_done", tile)
                for m in range(2):
                    for c in range(CK):
                        last = matmul3(pe, (k_ps if which else q_ps)[:, m * T:(m + 1) * T], (qk_hi[:, which, c, m * P:(m + 1) * P],
                                                                         qk_lo[:, which, c, m * P:(m + 1) * P]),
                                       (yt_hi[:, par, c], yt_lo[:, par, c]), c == 0, c == CK - 1)
                last.then_inc(sg["e_k_ready" if which else "e_q_ready"], 1)

            def project_u(tile, par):
                for t in range(2):
                    for c in range(CK):
                        last = matmul3(pe, m_ps[:, t * D:(t + 1) * D], (yt_hi[:, par, c, t * P:(t + 1) * P],
                                                                        yt_lo[:, par, c, t * P:(t + 1) * P]),
                                       (wu_hi[:, c], wu_lo[:, c]), c == 0, c == CK - 1)
                last.then_inc(sg["e_u_ready"], 1)

            def project_a(tile, par):
                need(pe, "e_u_done", tile + 1)
                for c in range(CK):
                    last = matmul3(pe, m_ps[0:RA, 0:T], (wa_hi[:, c], wa_lo[:, c]), (yt_hi[:, par, c], yt_lo[:, par, c]),
                                   c == 0, c == CK - 1)
                last.then_inc(sg["e_ha_ready"], 1)

            def scores(n, tile, par, u, b):
                t, half = u // 2, u % 2
                need(pe, "e_qm_done", n + 1)
                need(pe, "e_qma_done", n + 1)
                need(pe, "e_k_done", tile + 1)
                need(pe, "e_sub_done", n - 1)
                for q in range(4):
                    for s in range(2):
                        at = t * P + s * SEQ
                        pe.matmul(s_ps[b][:, q * P + s * SEQ:q * P + (s + 1) * SEQ],
                                  qm[:, b, s, 2 * q:2 * q + 2].rearrange("p h t -> p (h t)"),
                                  kd[:, par, half, at:at + SEQ], start=(s == 0), stop=False, skip_group_check=True)
                    last = pe.matmul(s_ps[b][:, q * P:(q + 1) * P], consts["mask_rows"][:], along(consts["causal"][:], 1, 2),
                                     start=False, stop=True, skip_group_check=True)
                last.then_inc(sg["e_s_ready"], 1)

            def transpose_probs(m, b):
                need(pe, "e_pn_done", m + 1)
                need(pe, "e_pt_done", m)
                for q in range(4):
                    last = pe.transpose(t_ps[:, q * P:(q + 1) * P], prob[:, b, 2 * q:2 * q + 2].rearrange("p g k -> p (g k)"),
                                        consts["ident"][:])
                last.then_inc(sg["e_t_ready"], 1)

            def attend(m, tile, par, u, b, tok):
                t, half = u // 2, u % 2
                need(pe, "e_pt_done", m + 1)
                need(pe, "e_u_done", tile + 1)
                if half == 0:
                    need(pe, "e_tanh_done", tok)
                for h in range(8):
                    last = pe.matmul(u_ps[0:64, 0:SEQ], ub[:, par, t, 8 * half + h], probT[:, b, h * SEQ:(h + 1) * SEQ],
                                     start=(half == 0 and h == 0), stop=(half == 1 and h == 7))
                last.then_inc(sg["e_mod_ready"], 1)

            pe.wait_ge(wlo_done, 1)
            pe.wait_ge(cleared, 2)
            transpose_norm(0)
            project_qk(0, 0, 0)
            project_qk(1, 0, 0)
            project_u(0, 0)
            with pe.Fori(0, NU // 8) as j:
                for k in range(8):
                    n, b = 8 * j + k, k % 2
                    tile, par, nxt = 2 * j + k // 4, k // 4, 1 - k // 4
                    scores(n, tile, par, k % 4, b)
                    with pe.If(j > 0) if k < 2 else nullcontext():
                        m = (k - 2) % 8
                        attend(n - 2, tile if k % 4 > 1 else tile - 1, m // 4, m % 4, b, 4 * j + k // 2 - 1)
                    with pe.If(j > 0) if k == 0 else nullcontext():
                        transpose_probs(n - 1, 1 - b)
                    if k % 4 == 0:
                        project_a(tile, par)
                    if k % 4 == 1:
                        transpose_norm(tile + 1)
                    if k % 4 == 2:
                        project_qk(0, tile + 1, nxt)
                        project_qk(1, tile + 1, nxt)
                    if k % 4 == 3:
                        project_u(tile + 1, nxt)
            transpose_probs(NU - 1, 1)
            attend(NU - 2, NT - 1, 1, 2, 0, TT - 1)
            attend(NU - 1, NT - 1, 1, 3, 1, TT - 1)


def layer1_mlp(nc, dram, xres, consts, yT_hi, yT_lo, modT):
    F = 1024
    FC = F // P
    RA = 16
    NG = NT * FC
    with ExitStack() as ctx:
        taken = Taken(nc, ctx)
        def sb(name, shape, dt=F32):
            return ctx.enter_context(nc.sbuf_tensor(name, shape, dt))

        def sem(name):
            return taken.take(name)

        wg = sb("f_wg", [P, 2, CK, F])
        wd = sb("f_wd", [P, FC, D])
        wg_hi = sb("f_wg_hi", [P, 2, CK, F], F32R)
        wg_lo = sb("f_wg_lo", [P, 2, CK, F], F32R)
        wd_hi = sb("f_wd_hi", [P, FC, D], F32R)
        wd_lo = sb("f_wd_lo", [P, FC, D], F32R)
        wb = sb("f_wb", [P, F])
        wb3 = sb("f_wb3", [P, F], F32R)
        ln2 = sb("f_ln2", [P, CK])
        sg_sb = sb("f_silu", [P, 2, T])
        act_f = sb("f_act", [P, 2, T])
        act_hi = sb("f_act_hi", [P, 2, T], F32R)
        act_lo = sb("f_act_lo", [P, 2, T], F32R)
        gu_ps = [ctx.enter_context(nc.psum_tensor(f"f_gu{k}", [P, 512], F32)) for k in range(4)]
        o_ps = [ctx.enter_context(nc.psum_tensor(f"f_o{k}", [P, 512], F32)) for k in range(2)]

        PE_S = ["f_gu_ready", "f_down_ready"]
        ACT_S = ["f_silu_done", "f_hi_done"]
        DVE_S = ["f_prod_done", "f_lo_done", "f_x_done"]
        sg = Signals(taken, PE_S + ACT_S + DVE_S)
        need = sg.need
        wg_in, wd_in, wb_in, ln_in = [sem("f_w_in"), sem("f_w_up_in")], sem("f_wd_in"), sem("f_wb_in"), sem("f_ln_in")
        wb_clear, whi_done, wlo_done = sem("f_wb_clear"), sem("f_whi_done"), sem("f_wlo_done")
        stored = sem("f_stored")

        block = ctx.enter_context(nc.Block())

        @block.sync
        def _(sp):
            sp.dma_start(ln2[:], dram["ln2_w"]).then_inc(ln_in, 16)
            for k, name in enumerate(("w_inT", "w_upT")):
                sp.dma_start(wg[:, k], dram[name].rearrange("(c p) n -> p c n", p=P)).then_inc(wg_in[k], 16)
            sp.wait_ge(wb_clear, 1)
            for k in range(3):
                sp.dma_start(wb[32 * k:32 * k + RA, :], dram["wb"]).then_inc(wb_in, 16)
            sp.dma_start(wd[:], dram["w_downT"].rearrange("(f p) n -> p f n", p=P)).then_inc(wd_in, 16)
            with sp.Fori(0, NT) as tile:
                need(sp, "f_x_done", tile + 1)
                sp.dma_start(dram["out"][ds(tile * T, T), :].rearrange("(t p) d -> p t d", p=P),
                             xres[:, ds(X0 + 2 * tile, 2), :]).then_inc(stored, 16)
            sp.wait_ge(stored, 16 * NT)

        @block.scalar
        def _(act):
            sg.give_credit(act, ACT_S)
            act.wait_ge(ln_in, 16)
            for k in range(2):
                act.wait_ge(wg_in[k], 16)
                for c in range(CK):
                    last = act.activation(wg_hi[:, k, c], wg[:, k, c], ACT.Copy, scale=ln2[:, c:c + 1])
                last.then_inc(whi_done, 1)
            act.wait_ge(wb_in, 48)
            act.activation(wb3[:], wb[:], ACT.Copy).then_inc(whi_done, 1)
            act.wait_ge(wd_in, 16)
            act.activation(wd_hi[:], wd[:], ACT.Copy).then_inc(whi_done, 1)
            with act.Fori(0, NT // 2) as j:
                for k in range(2 * FC):
                    g, b = 16 * j + k, k % 2
                    need(act, "f_gu_ready", g + 1)
                    need(act, "f_prod_done", g - 1)
                    act.activation(sg_sb[:, b], gu_ps[k % 4][:, 0:T], ACT.Silu).then_inc(sg["f_silu_done"], 1)
                    need(act, "f_prod_done", g + 1)
                    need(act, "f_down_ready", g - 1)
                    act.activation(act_hi[:, b], act_f[:, b], ACT.Copy).then_inc(sg["f_hi_done"], 1)

        @block.vector
        def _(dve):
            sg.give_credit(dve, DVE_S)
            dve.memset(wb[:], 0.0).then_inc(wb_clear, 1)
            for k in range(2):
                dve.wait_ge(whi_done, k + 1)
                for c in range(CK):
                    last = dve.scalar_tensor_tensor(wg_lo[:, k, c], wg[:, k, c], ln2[:, c:c + 1], wg_hi[:, k, c].bitcast(F32),
                                                    ALU.mult, ALU.subtract)
                last.then_inc(wlo_done, 1)
            dve.wait_ge(whi_done, 3)
            dve.tensor_tensor(wb3[64:64 + RA], wb[64:64 + RA], wb3[64:64 + RA].bitcast(F32), ALU.subtract).then_inc(wlo_done, 1)
            dve.wait_ge(whi_done, 4)
            dve.tensor_tensor(wd_lo[:], wd[:], wd_hi[:].bitcast(F32), ALU.subtract).then_inc(wlo_done, 1)
            with dve.Fori(0, NT // 2) as j:
                for k in range(2 * FC):
                    g, b, a = 16 * j + k, k % 2, k // FC
                    need(dve, "f_silu_done", g + 1)
                    need(dve, "f_hi_done", g - 1)
                    dve.tensor_tensor(act_f[:, b], gu_ps[k % 4][:, T:], sg_sb[:, b], ALU.mult).then_inc(sg["f_prod_done"], 1)
                    need(dve, "f_hi_done", g + 1)
                    dve.tensor_tensor(act_lo[:, b], act_f[:, b], act_hi[:, b].bitcast(F32), ALU.subtract
                                      ).then_inc(sg["f_lo_done"], 1)
                    if k % FC == FC - 1:
                        tile = 2 * j + a
                        need(dve, "f_down_ready", g + 1)
                        dve.tensor_tensor(xres[:, ds(X0 + 2 * tile, 2), :], o_ps[a][:].rearrange("p (t d) -> p t d", t=2),
                                          xres[:, ds(X0 + 2 * tile, 2), :], ALU.add).then_inc(sg["f_x_done"], 1)

        @block.tensor
        def _(pe):
            sg.give_credit(pe, PE_S)

            def gate_up(g, bank, tile, f):
                need(pe, "f_prod_done", g - 3)
                tok = ds(tile * T, T) if not isinstance(tile, int) else slice(tile * T, tile * T + T)
                mcol = ds(M0 + tile * T, T) if not isinstance(tile, int) else slice(M0 + tile * T, M0 + tile * T + T)
                ps = gu_ps[bank]
                cols = slice(f * P, (f + 1) * P)
                pe.matmul(ps[:, 0:T], wb3[:, cols], modT[:, mcol], start=True, stop=False)
                for k in range(2):
                    for c in range(CK):
                        last = matmul3(pe, ps[:, k * T:(k + 1) * T], (wg_hi[:, k, c, cols], wg_lo[:, k, c, cols]),
                                       (yT_hi[:, c, tok], yT_lo[:, c, tok]), k == 1 and c == 0, c == CK - 1)
                last.then_inc(sg["f_gu_ready"], 1)

            def down(g, b, a, f, tile):
                need(pe, "f_lo_done", g + 1)
                if f == 0:
                    need(pe, "f_x_done", tile - 1)
                for t in range(2):
                    last = matmul3(pe, o_ps[a][:, t * D:(t + 1) * D], (act_hi[:, b, t * P:(t + 1) * P], act_lo[:, b, t * P:(t + 1) * P]),
                                   (wd_hi[:, f], wd_lo[:, f]), f == 0 and t == 0, f == FC - 1, skip=True)
                last.then_inc(sg["f_down_ready"], 1)

            pe.wait_ge(wlo_done, 3)
            gate_up(0, 0, 0, 0)
            gate_up(1, 1, 0, 1)
            pe.wait_ge(wlo_done, 4)
            with pe.Fori(0, NT // 2) as j:
                for k in range(2 * FC):
                    g = 16 * j + k
                    k2 = k + 2
                    with pe.If(j < NT // 2 - 1) if k2 >= 2 * FC else nullcontext():
                        gate_up(g + 2, k2 % 4, (2 * j + k2 // FC) if k2 < 2 * FC else 2 * j + 2, k2 % FC)
                    down(g, k % 2, k // FC, k % FC, 2 * j + k // FC)


def program(nc, dram, out, stop_after=9):
    with ExitStack() as ctx:
        def sb(name, shape, dt=F32):
            return ctx.enter_context(nc.sbuf_tensor(name, shape, dt))

        xres = sb("xres", [P, TT + 2 * X0, D])
        consts = {"ident": sb("ident", [P, P]), "ones": sb("ones", [P, 8]), "minus_half": sb("minus_half", [P, 32]),
                  "mask_rows": sb("mask_rows", [P, P], BF16), "causal": sb("causal", [P, SEQ], BF16)}
        set_constants(nc, dram, consts, xres)
        for k, phase in enumerate((layer0_attention, layer0_ffn, layer1_attention, layer1_ffn)):
            if k in PHASES:
                phase(nc, dram, xres, consts)
        if PHASES[-1] == 3:
            return
        stored = ctx.enter_context(nc.semaphore("stored"))
        block = ctx.enter_context(nc.Block())

        @block.sync
        def _(sp):
            sp.dma_start(out.rearrange("(t p) d -> p t d", p=P), xres[:, X0:X0 + TT, :]).then_inc(stored, 16)
            sp.wait_ge(stored, 16)


def tables():
    f = np.float32
    inv = (f(1.0) / f(10000.0) ** (np.arange(0, HD, 2, dtype=f) / f(HD))).astype(f)
    ang = np.outer(np.arange(SEQ, dtype=f), inv).astype(f)
    cos, sin = np.cos(ang), np.sin(ang)
    cos2 = np.concatenate([cos, cos], 1)
    c = {}
    c["cos_d"] = cos2.T
    c["sin_d"] = np.concatenate([sin, -sin], 1).T
    c["cos_t"] = np.concatenate([cos2, cos2], 0)
    s2 = np.concatenate([-sin, sin], 1)
    c["sin_t"] = np.concatenate([s2, s2], 0)
    inv = (f(1.0) / f(10000.0) ** (np.arange(32, dtype=f) / f(32))).astype(f)
    ang = (np.arange(SEQ, dtype=f)[:, None] * inv).astype(f)
    cos, sin = np.cos(ang), np.sin(ang)
    c["cos_k"] = np.concatenate([np.concatenate([cos, cos], 1)] * 2, 0)
    c["sin_k"] = np.concatenate([np.concatenate([-sin, sin], 1)] * 2, 0)
    c["key_no"] = np.tile(np.arange(SEQ), (SEQ, 1))
    c["heads"] = np.arange(P)[:, None] // 16 == np.arange(8)
    c["same_head"] = np.arange(D)[:, None] // 16 == np.arange(H)
    c["ident"] = np.eye(P)
    rows = np.zeros((P, P))
    rows[np.arange(SEQ), np.arange(SEQ)] = 1
    rows[np.arange(SEQ), np.arange(SEQ) + SEQ] = 1
    c["mask_rows"] = rows
    causal = np.zeros((P, SEQ))
    causal[:SEQ][np.arange(SEQ)[None, :] > np.arange(SEQ)[:, None]] = MASKED
    c["causal"] = causal
    return {k: np.ascontiguousarray(v, dtype=f) for k, v in c.items()}


def kernel(**inputs):
    import concourse.bacc as bacc
    from concourse.bass_utils import run_bass_kernel_spmd

    a = {}
    a["x"] = inputs["x"].reshape(NTOK, D)
    a["ctxT"] = inputs["ctx_2048"].reshape(NTOK, D).T
    for n in ("wq", "wk", "wv", "wo", "wk_ctx", "wv_ctx", "q_norm_w", "k_norm_w"):
        a[n] = inputs["L0_xattn_" + n]
    a["factors"], a["ffn_bias"] = inputs["L0_ffn_factors"], inputs["L0_ffn_bias"]
    w = {n: inputs["L1_xattn_W_" + n] for n in ("kvc", "dq", "uq", "qr", "uk", "kr", "uv", "o")}
    a.update(wkvcT=w["kvc"].T, wkvc=w["kvc"], wkr=w["kr"], wdq=w["dq"], wuqT=w["uq"].T, wukT=w["uk"].T, wuvT=w["uv"].T,
             wqr=w["qr"], wo1=w["o"], segT=inputs["itok_BxS_0_1023"].T)
    f = {n: inputs["L1_ffn_" + n] for n in ("ln1_w", "ln2_w", "Wq", "Wk", "Wv", "Wo", "A", "B", "W_in_base", "W_up_base", "W_down")}
    a.update(ln1_w=f["ln1_w"].reshape(CK, P).T, ln2_w=f["ln2_w"].reshape(CK, P).T, wqT_f=f["Wq"].T, wkT_f=f["Wk"].T, wv_f=f["Wv"], wo_f=f["Wo"], wa=f["A"],
             wb=f["B"], w_inT=f["W_in_base"].T, w_upT=f["W_up_base"].T, w_downT=f["W_down"].T)
    a.update(tables())
    nc = bacc.Bacc("TRN2", target_bir_lowering=False, num_devices=1)
    arrays, dram = {}, {}
    for name, value in a.items():
        arrays["in_" + name] = np.ascontiguousarray(value)
        dram[name] = nc.dram_tensor("in_" + name, list(value.shape), mybir.dt.from_np(arrays["in_" + name].dtype),
                                    kind="ExternalInput").ap()
    out = dram["out"] = nc.dram_tensor("out", [NTOK, D], F32, kind="ExternalOutput").ap()
    program(nc, dram, out)
    r = run_bass_kernel_spmd(nc, [arrays], core_ids=[0])
    return np.asarray(r.results[0]["out"]).reshape(NSEQ, SEQ, D)
```

```python
from contextlib import ExitStack, nullcontext

import numpy as np

import concourse.bass as bass
from concourse import mybir

P = 128
D = 256
CK = D // P
SEQ = 64
NSEQ = 32
NTOK = NSEQ * SEQ
TT = NTOK // P
T = 256
ST = T // SEQ
NT = NTOK // T
X0 = 2
H = 16
G = 4
HD = 128
UNITS = H // 2
LOOKBACK = 8
MASKED = -float(2 ** 100)

F32 = mybir.dt.float32
F32R = mybir.dt.float32r
BF16 = mybir.dt.bfloat16
ALU = mybir.AluOpType
ACT = mybir.ActivationFunctionType
AX = mybir.AxisListType.X


def ds(start, size):
    return bass.ds(start, size)


def along(ap, axis, n):
    shape = list(ap.shape)
    shape.insert(axis, n)
    return ap.unsqueeze(axis).broadcast_to(shape)


class Taken:

    phases = []

    def __init__(self, nc, ctx):
        self.nc, self.all, self.stack = nc, [], ExitStack()
        self.last = Taken.phases[-1] if Taken.phases else None
        Taken.phases.append(self)
        ctx.callback(self.release_last)

    def take(self, name):
        self.all.append(self.stack.enter_context(self.nc.semaphore(name)))
        return self.all[-1]

    def clear_last(self, pool):
        if self.last is not None:
            for s in self.last.all:
                pool.sem_clear(s)

    def release_last(self):
        if self.last is not None:
            self.last.stack.close()


class Signals:

    CREDIT = 16

    def __init__(self, taken, names, less=()):
        self.sem = {n: taken.take(n) for n in names}
        self.credit = {n: self.CREDIT - (1 if n in less else 0) for n in names}

    def __getitem__(self, name):
        return self.sem[name]

    def give_credit(self, eng, names):
        for n in names:
            eng.sem_inc(self.sem[n], self.credit[n])

    def need(self, eng, name, count):
        if isinstance(count, int) and count <= 0:
            return
        eng.wait_ge(self.sem[name], count + self.CREDIT)


def matmul3(pe, out, left, right, start, stop, skip=False):
    (lh, ll), (rh, rl) = left, right
    pe.matmul(out, ll, rh, start=start, stop=False, skip_group_check=skip)
    pe.matmul(out, lh, rl, start=False, stop=False, skip_group_check=skip)
    return pe.matmul(out, lh, rh, start=False, stop=stop, skip_group_check=skip)


def layer0_attention(nc, dram, xres, consts):
    ident = consts["ident"]
    with ExitStack() as ctx:
        taken = Taken(nc, ctx)
        def sb(name, shape, dt=F32):
            return ctx.enter_context(nc.sbuf_tensor(name, shape, dt))

        def bank(name, shape=(P, 512)):
            return ctx.enter_context(nc.psum_tensor(name, list(shape), F32))

        KVC = G * HD
        QC = H * HD
        w_hi = sb("a_w_hi", [P, 4 * CK * KVC + CK * QC], F32R)
        w_lo = sb("a_w_lo", [P, 4 * CK * KVC + CK * QC], F32R)
        wo_hi = sb("a_wo_hi", [P, H, D], F32R)
        wo_lo = sb("a_wo_lo", [P, H, D], F32R)
        keysT = sb("a_keysT", [P, 2, ST, G, P])
        vals = sb("a_vals", [P, 2, ST, KVC])
        xnT_hi = sb("a_xnT_hi", [P, 2, CK, T], F32R)
        xnT_lo = sb("a_xnT_lo", [P, 2, CK, T], F32R)
        cT = sb("a_cT", [P, 2, CK, T])
        cT_hi = sb("a_cT_hi", [P, CK, T], F32R)
        cT_lo = sb("a_cT_lo", [P, CK, T], F32R)
        xn = sb("a_xn", [P, 2, D])
        cos_d = sb("a_cos_d", [P, SEQ])
        sin_d = sb("a_sin_d", [P, SEQ])
        cos_t = sb("a_cos_t", [P, HD])
        sin_t = sb("a_sin_t", [P, HD])
        kw_t = sb("a_kw_t", [P, HD])
        kw_d = sb("a_kw_d", [P, 1])
        qw_d = sb("a_qw_d", [P, 1])
        sq = sb("a_sq", [P, ST, 2, SEQ])
        qc = sb("a_qc", [P, ST, 2, SEQ])
        qs = sb("a_qs", [P, ST, 2, SEQ])
        qT = sb("a_qT", [P, 2, ST, 2, SEQ])
        q_ms = sb("a_q_ms", [P, 2, ST])
        q_rs = sb("a_q_rs", [P, 2, ST])
        s_max = sb("a_s_max", [P, 2, ST])
        s_bias = sb("a_s_bias", [P, 2, ST])
        s_sum = sb("a_s_sum", [P, 2, ST])
        s_inv = sb("a_s_inv", [P, 2, ST])
        prob = sb("a_prob", [P, 2, ST, P])
        probT = sb("a_probT", [P, 2, ST, P])
        attT_hi = sb("a_attT_hi", [P, 2, 2, T], F32R)
        attT_lo = sb("a_attT_lo", [P, 2, 2, T], F32R)
        k_sq = sb("a_k_sq", [P, G, HD])
        k_ms = sb("a_k_ms", [P, G])
        k_rs = sb("a_k_rs", [P, G])
        kn = sb("a_kn", [P, G, HD])
        kc = sb("a_kc", [P, G, HD])
        ks = sb("a_ks", [P, G, HD])
        kr = sb("a_kr", [P, G, HD])
        bst = sb("a_bst", [P, 2, 6])
        mv = sb("a_mv", [P, 2, 2])
        var = sb("a_var", [P, 2])
        rstd = sb("a_rstd", [P, 2])
        spare = sb("a_spare", [P, 1])

        q_ps = [bank(f"a_q_ps{k}") for k in range(2)]
        s_ps = [bank(f"a_s_ps{k}") for k in range(2)]
        t_ps = bank("a_t_ps")
        o_ps = bank("a_o_ps")
        out_ps = bank("a_out_ps")
        m_ps = bank("a_m_ps")

        PE_S = ["q_ready", "st_ready", "s_ready", "t_ready", "pv_ready", "out_ready", "m_ready"]
        ACT_S = ["sq_done", "exp_done", "ot_done", "ksq_done", "m_free_act", "xhi_done", "chi_done"]
        DVE_S = ["rope_done", "ms_done", "nb_done", "pt_done", "inv_done", "x_done", "kms_done", "kn_done",
                 "kq_done", "var_done", "xn_done", "xlo_done", "clo_done", "bst_done", "mv_done", "max_done", "kred_done", "olo_done"]
        POOL_S = ["qr_done", "qrs_done", "pn_done", "krs_done", "kr_done", "rstd_done", "kc_done"]
        sg = Signals(taken, PE_S + ACT_S + DVE_S + POOL_S, less=("ot_done", "olo_done"))
        need = sg.need
        w_in = [taken.take(f"w_in{k}") for k in range(4)]
        c_in = [taken.take(f"c_in{k}") for k in range(2)]
        small_in = taken.take("small_in")
        x_in = taken.take("tokens_in")
        wo_in = taken.take("wo_in")
        wo_hi_done, wo_lo_done = taken.take("wo_hi_done"), taken.take("wo_lo_done")
        whi_done = taken.take("whi_done")
        wlo_done = taken.take("wlo_done")
        tab_done = taken.take("tab_done")

        stage = [vals[:, 0].rearrange("p s n -> p (s n)"), vals[:, 1].rearrange("p s n -> p (s n)"),
                 keysT[:, 0].rearrange("p s g n -> p (s g n)"), keysT[:, 1].rearrange("p s g n -> p (s g n)")]
        CH = 2048
        wo_stage = [stage[1], stage[3]]

        def kv_weight(kind, which, c):
            at = ((0 if kind == "c" else 2) + which) * CK * KVC + c * KVC
            return w_hi[:, at:at + KVC], w_lo[:, at:at + KVC]

        def q_weight(head, c):
            at = 4 * CK * KVC + c * QC + head * HD
            return w_hi[:, at:at + HD], w_lo[:, at:at + HD]

        USES = [("K", "c", 0), ("KT", "c", 0), ("K", "c", 1), ("KT", "c", 1), ("V", "c", 0), ("V", "c", 1),
                ("LN", "s", 0), ("V", "s", 0), ("K", "s", 0), ("K", "s", 1), ("KT", "s", 0), ("V", "s", 1),
                ("KT", "s", 1)]
        FIRST = [("K", "c", 0), ("K", "c", 1), ("V", "c", 0), ("KT", "c", 0), ("V", "c", 1), ("KT", "c", 1),
                 ("LN", "s", 0), ("K", "s", 0), ("V", "s", 0), ("K", "s", 1), ("V", "s", 1), ("KT", "s", 0),
                 ("KT", "s", 1)]
        FIRST_BANKS = [m_ps, s_ps[0], s_ps[1], t_ps, out_ps]
        NU = len(USES)

        def use_of(tile, use):
            if isinstance(tile, int) and tile == 0:
                return FIRST[use], FIRST_BANKS[use % len(FIRST_BANKS)]
            return USES[use], m_ps

        MIDDLE = [None, 1, 3, 5, 7, None, 10, 12]
        LATE = [0, 2, 4, 6, 8, 9, 11, None]
        SQ_AT = 2
        LAST_C = USES.index(("V", "c", 1)) + 1
        FIRST_LAST_C = FIRST.index(("V", "c", 1)) + 1
        KSEQ = {("c", 0): 0, ("c", 1): 1, ("s", 0): 2, ("s", 1): 3}

        block = ctx.enter_context(nc.Block())

        @block.sync
        def _(sp):
            for k, names in enumerate([("wk_ctx", "wv_ctx"), ("wk", "wv")]):
                for m, name in enumerate(names):
                    sp.dma_start(stage[k][:, m * CK * KVC:(m + 1) * CK * KVC].rearrange("p (c n) -> p c n", c=CK),
                                 dram[name].rearrange("(c p) n -> p c n", p=P)).then_inc(w_in[k], 16)
                if k == 0:
                    sp.dma_start(cT[:, 0], dram["ctxT"][:, 0:T].rearrange("(c p) n -> p c n", p=P)).then_inc(c_in[0], 16)
            for name, tile in (("cos_d", cos_d), ("sin_d", sin_d), ("cos_t", cos_t), ("sin_t", sin_t)):
                sp.dma_start(tile[:], dram[name]).then_inc(small_in, 16)
            sp.dma_start(kw_t[:], dram["k_norm_w"].partition_broadcast(P)).then_inc(small_in, 16)
            sp.dma_start(kw_d[:], dram["k_norm_w"].rearrange("(p a) -> p a", a=1)).then_inc(small_in, 16)
            sp.dma_start(qw_d[:], dram["q_norm_w"].rearrange("(p a) -> p a", a=1)).then_inc(small_in, 16)
            for c in range(CK):
                sp.dma_start(stage[2 + c], dram["wq"][c * P:(c + 1) * P, :]).then_inc(w_in[2 + c], 16)
            sp.dma_start(xres[:, X0:X0 + TT, :], dram["x"].rearrange("(t p) d -> p t d", p=P)).then_inc(x_in, 16)
            sp.dma_start(cT[:, 1], dram["ctxT"][:, T:2 * T].rearrange("(c p) n -> p c n", p=P)).then_inc(c_in[1], 16)
            for k in range(2):
                sp.wait_ge(wlo_done, 2 + 2 * k)
                sp.dma_start(wo_stage[k].rearrange("p (h n) -> p h n", n=D),
                             dram["wo"][k * CH // D * P:(k + 1) * CH // D * P, :].rearrange("(h p) n -> p h n", p=P)
                             ).then_inc(wo_in, 16)
            with sp.Fori(0, NT // 2 - 1) as j:
                for a in range(2):
                    need(sp, "clo_done", 2 * j + a + 1)
                    sp.dma_start(cT[:, a], dram["ctxT"][:, ds((2 * j + a + 2) * T, T)].rearrange("(c p) n -> p c n", p=P)
                                 ).then_inc(c_in[a], 16)
            for a in range(2):
                need(sp, "clo_done", NT - 1 + a)
                sp.dma_start(cT[:, a], dram["ctxT"][:, 0:T].rearrange("(c p) n -> p c n", p=P)).then_inc(c_in[a], 16)
            for a in range(2):
                sp.wait_ge(c_in[a], 16 * (NT // 2 + 1))

        @block.gpsimd
        def _(pool):
            sg.give_credit(pool, POOL_S)
            taken.clear_last(pool)
            def key_rms(tile, src, half):
                n = 4 * tile + KSEQ[(src, half)]
                need(pool, "kms_done", n + 1)
                need(pool, "kn_done", n)
                pool.tensor_tensor(k_rs[:], k_ms[:], consts["minus_half"][:, 0:G],
                                   ALU.pow).then_inc(sg["krs_done"], 1)

            def key_cos(tile, half):
                need(pool, "kn_done", 4 * tile + KSEQ[("s", half)] + 1)
                pool.tensor_tensor(kc[:], kn[:], along(cos_t[:], 1, G), ALU.mult).then_inc(sg["kc_done"], 1)

            def key_add(tile, half):
                m = 2 * tile + half
                need(pool, "kc_done", m + 1)
                need(pool, "kq_done", m + 1)
                if half == 1:
                    order = FIRST if isinstance(tile, int) else USES
                    need(pool, "m_ready", NU * tile + order.index(("KT", "s", 0)) + 1)
                pool.tensor_tensor(kr[:], kc[:], ks[:], ALU.add).then_inc(sg["kr_done"], 1)

            def norm_pool(tile):
                need(pool, "var_done", tile + 1)
                pool.tensor_tensor(rstd[:], var[:], consts["minus_half"][:, 0:2], ALU.pow).then_inc(sg["rstd_done"], 1)

            def add_rope(n, b):
                need(pool, "rope_done", n + 1)
                need(pool, "s_ready", n - 1)
                pool.tensor_tensor(qT[:, b], qc[:], qs[:], ALU.add).then_inc(sg["qr_done"], 1)

            key_rms(0, "c", 0)
            key_rms(0, "c", 1)
            norm_pool(0)
            pool.wait_ge(tab_done, 1)
            for half in range(2):
                key_rms(0, "s", half)
                key_cos(0, half)
                if half == 0:
                    key_add(0, 0)
            key_add(0, 1)
            add_rope(0, 0)
            with pool.Fori(0, NT // 2) as j:
                for a in range(2):
                    for p in range(UNITS):
                        n, b, tile = 16 * j + 8 * a + p, p % 2, 2 * j + a
                        kind, src, half = USES[LATE[p - 1]] if p and LATE[p - 1] is not None else ("", "", 0)
                        need(pool, "ms_done", n + 1)
                        need(pool, "exp_done", n - 1)
                        pool.tensor_tensor(q_rs[:, b], q_ms[:, b], consts["minus_half"][:, 0:ST],
                                           ALU.pow).then_inc(sg["qrs_done"], 1)
                        if kind == "K":
                            key_rms(tile + 1, src, half)
                        if kind == "K" and src == "s":
                            key_cos(tile + 1, half)
                        if p == 2:
                            norm_pool(tile + 1)
                        need(pool, "inv_done", n + 1)
                        pool.tensor_tensor(prob[:, b], prob[:, b], along(s_inv[:, b], 2, P),
                                           ALU.mult).then_inc(sg["pn_done"], 1)
                        add_rope(n + 1, 1 - b)
                        if kind == "K" and src == "s":
                            key_add(tile + 1, half)

        @block.scalar
        def _(act):
            sg.give_credit(act, ACT_S)
            def high_weight(k):
                act.wait_ge(w_in[k], 32 if k < 2 else 16)
                act.activation(w_hi[:, k * CH:(k + 1) * CH], stage[k], ACT.Copy).then_inc(whi_done, 1)

            high_weight(0)
            act.wait_ge(c_in[0], 16)
            act.activation(cT_hi[:], cT[:, 0], ACT.Copy).then_inc(sg["chi_done"], 1)
            high_weight(1)

            def misc_act(tile, use, par):
                (kind, src, half), ps = use_of(tile, use)
                if kind == "K":
                    need(act, "m_ready", NU * tile + use + 1)
                    need(act, "kred_done", 4 * tile + KSEQ[(src, half)])
                    act.activation(k_sq[:], ps[:].rearrange("p (g d) -> p g d", g=G), ACT.Square
                                   ).then_inc(sg["ksq_done"], 1)
                elif kind == "V":
                    need(act, "m_ready", NU * tile + use + 1)
                    need(act, "pv_ready", 8 * (tile - 1))
                    keys = slice(0, SEQ) if src == "c" else slice(SEQ, P)
                    for s in range(2):
                        last = act.activation(vals[keys, par, 2 * half + s, :], ps[s * SEQ:(s + 1) * SEQ, :], ACT.Copy)
                    last.then_inc(sg["m_free_act"], 1)
                elif kind == "KT":
                    need(act, "m_ready", NU * tile + use + 1)
                    need(act, "s_ready", 8 * (tile - 1))
                    keys = slice(0, SEQ) if src == "c" else slice(SEQ, P)
                    dst = keysT[:, par, 2 * half:2 * half + 2, :, keys].rearrange("p s g k -> p g s k")
                    act.activation(dst, ps[:].rearrange("p (g s k) -> p g s k", g=G, s=2), ACT.Copy,
                                   scale=kw_d[:, 0:1] if src == "c" else 1.0).then_inc(sg["m_free_act"], 1)
                else:
                    need(act, "m_ready", NU * tile + use + 1)
                    need(act, "q_ready", 8 * (tile - 1))
                    act.activation(xnT_hi[:, par], ps[:].rearrange("p (c t) -> p c t", c=CK), ACT.Copy
                                   ).then_inc(sg["xhi_done"], 1)

            def square(n, b):
                need(act, "q_ready", n + 1)
                need(act, "st_ready", n)
                act.activation(sq[:].rearrange("p s h t -> p h s t"),
                               q_ps[b][:].rearrange("p (h s t) -> p h s t", h=2, s=ST), ACT.Square
                               ).then_inc(sg["sq_done"], 1)

            act.wait_ge(small_in, 7 * 16)
            for use in range(NU):
                if use in (1, 2):
                    high_weight(use + 1)
                if use in (2, 3):
                    act.wait_ge(wlo_done, 2 if use == 2 else 4)
                if use == NU - 1:
                    act.wait_ge(wo_in, 32)
                    for k in range(2):
                        act.activation(wo_hi[:].rearrange("p h n -> p (h n)")[:, k * CH:(k + 1) * CH], wo_stage[k], ACT.Copy
                                       ).then_inc(wo_hi_done, 1)
                misc_act(0, use, 0)
                if use == FIRST_LAST_C:
                    act.wait_ge(c_in[1], 16)
                    need(act, "m_ready", FIRST_LAST_C)
                    act.activation(cT_hi[:], cT[:, 1], ACT.Copy).then_inc(sg["chi_done"], 1)
            square(0, 0)
            act.wait_ge(wlo_done, 5)
            act.wait_ge(wo_lo_done, 2)
            with act.Fori(0, NT // 2) as j:
                for a in range(2):
                    for p in range(UNITS):
                        n, b, tile = 16 * j + 8 * a + p, p % 2, 2 * j + a
                        if p and LATE[p - 1] is not None:
                            misc_act(tile + 1, LATE[p - 1], 1 - a)
                        need(act, "nb_done", n + 1)
                        need(act, "t_ready", n - 1)
                        need(act, "inv_done", n - 1)
                        for s in range(ST):
                            if s == SQ_AT:
                                square(n + 1, 1 - b)
                            last = act.activation(prob[:, b, s], s_ps[b][:, s * P:(s + 1) * P], ACT.Exp,
                                                  bias=s_bias[:, b, s:s + 1], scale=q_rs[:, b, s:s + 1],
                                                  accum_out=s_sum[:, b, s:s + 1])
                        last.then_inc(sg["exp_done"], 1)
                        if MIDDLE[p] is not None:
                            misc_act(tile + 1, MIDDLE[p], 1 - a)
                        need(act, "pv_ready", n)
                        need(act, "out_ready", n - 2)
                        act.activation(attT_hi[:, 1 - b].rearrange("p h (s t) -> p h s t", s=ST),
                                       o_ps[:].rearrange("p (s h t) -> p h s t", s=ST, h=2), ACT.Copy
                                       ).then_inc(sg["ot_done"], 1)
                        if p == 5:
                            act.wait_ge(c_in[a], 16 * (j + 2))
                            need(act, "m_ready", NU * (tile + 1) + LAST_C)
                            act.activation(cT_hi[:], cT[:, a], ACT.Copy).then_inc(sg["chi_done"], 1)
            N = NT * UNITS
            need(act, "pv_ready", N)
            need(act, "out_ready", N - 2)
            act.activation(attT_hi[:, 1].rearrange("p h (s t) -> p h s t", s=ST),
                           o_ps[:].rearrange("p (s h t) -> p h s t", s=ST, h=2), ACT.Copy).then_inc(sg["ot_done"], 1)

        @block.vector
        def _(dve):
            sg.give_credit(dve, DVE_S)
            def split_context(par, count):
                need(dve, "chi_done", count)
                dve.tensor_tensor(cT_lo[:], cT[:, par], cT_hi[:].bitcast(F32), ALU.subtract).then_inc(sg["clo_done"], 1)

            def x_tile(row):
                return xres[:, X0 + row, :] if isinstance(row, int) else xres[:, ds(X0 + row, 1), :].rearrange("p a d -> p (a d)")

            def norm_stats(tile, row0):
                for t in range(2):
                    last = dve.bn_stats(bst[:, t], x_tile(row0 + t))
                last.then_inc(sg["bst_done"], 1)
                need(dve, "bst_done", tile + 1)
                dve.memset(spare[:], 0.0)
                for t in range(2):
                    last = dve.bn_aggr(mv[:, t], bst[:, t])
                last.then_inc(sg["mv_done"], 1)
                need(dve, "mv_done", tile + 1)
                dve.tensor_scalar(var[:], mv[:, :, 1], 1e-5, None, ALU.add).then_inc(sg["var_done"], 1)

            def norm_x(tile, row0):
                need(dve, "rstd_done", tile + 1)
                for t in range(2):
                    last = dve.tensor_scalar(xn[:, t], x_tile(row0 + t), mv[:, t, 0:1], rstd[:, t:t + 1],
                                             ALU.subtract, ALU.mult)
                last.then_inc(sg["xn_done"], 1)

            def key_stats(tile, src, half):
                n = 4 * tile + KSEQ[(src, half)]
                need(dve, "ksq_done", n + 1)
                dve.tensor_reduce(k_ms[:], k_sq[:], AX, ALU.add).then_inc(sg["kred_done"], 1)
                need(dve, "kred_done", n + 1)
                dve.tensor_scalar(k_ms[:], k_ms[:], 1.0 / HD, 1e-6, ALU.mult, ALU.add).then_inc(sg["kms_done"], 1)

            def key_norm(tile, src, half, use):
                ps = use_of(tile, use)[1]
                n = 4 * tile + KSEQ[(src, half)]
                need(dve, "krs_done", n + 1)
                need(dve, "m_ready", NU * tile + use + 1)
                dve.tensor_tensor(kn[:], ps[:].rearrange("p (g d) -> p g d", g=G), along(k_rs[:], 2, HD),
                                  ALU.mult).then_inc(sg["kn_done"], 1)

            def key_sin(tile, half):
                need(dve, "kn_done", 4 * tile + KSEQ[("s", half)] + 1)
                need(dve, "kr_done", 2 * tile + half)
                dve.tensor_tensor(ks[:, :, 0:HD // 2], kn[:, :, HD // 2:], along(sin_t[:, 0:HD // 2], 1, G), ALU.mult)
                dve.tensor_tensor(ks[:, :, HD // 2:], kn[:, :, 0:HD // 2], along(sin_t[:, HD // 2:], 1, G),
                                  ALU.mult).then_inc(sg["kq_done"], 1)

            def low_x(tile, par):
                ps = use_of(tile, FIRST.index(("LN", "s", 0)))[1]
                need(dve, "xhi_done", tile + 1)
                dve.tensor_tensor(xnT_lo[:, par], ps[:].rearrange("p (c t) -> p c t", c=CK),
                                  xnT_hi[:, par].bitcast(F32), ALU.subtract).then_inc(sg["xlo_done"], 1)

            def rope(n, b, between=lambda: None):
                need(dve, "sq_done", n + 1)
                need(dve, "qr_done", n)
                q = q_ps[b][:].rearrange("p (h s t) -> p s h t", h=2, s=ST)
                half = P // 2
                cw = cos_d[:].unsqueeze(1).unsqueeze(1).broadcast_to([P, ST, 2, SEQ])
                sw = sin_d[:].unsqueeze(1).unsqueeze(1).broadcast_to([P, ST, 2, SEQ])
                dve.tensor_tensor(qc[:], q, cw, ALU.mult)
                between()
                dve.tensor_tensor(qs[0:half], q[half:P], sw[half:P], ALU.mult)
                dve.tensor_tensor(qs[half:P], q[0:half], sw[0:half], ALU.mult).then_inc(sg["rope_done"], 1)

            def low_out(m, b):
                need(dve, "ot_done", m + 1)
                need(dve, "out_ready", m - 1)
                dve.tensor_tensor(attT_lo[:, b].rearrange("p h (s t) -> p h s t", s=ST),
                                  o_ps[:].rearrange("p (s h t) -> p h s t", s=ST, h=2),
                                  attT_hi[:, b].rearrange("p h (s t) -> p h s t", s=ST).bitcast(F32), ALU.subtract
                                  ).then_inc(sg["olo_done"], 1)

            def low_weight(k):
                dve.wait_ge(whi_done, k + 1)
                dve.tensor_tensor(w_lo[:, k * CH:(k + 1) * CH], stage[k], w_hi[:, k * CH:(k + 1) * CH].bitcast(F32),
                                  ALU.subtract).then_inc(wlo_done, 1)

            low_weight(0)
            split_context(0, 1)
            low_weight(1)
            key_stats(0, "c", 0)
            key_norm(0, "c", 0, 0)
            low_weight(2)
            key_stats(0, "c", 1)
            low_weight(3)
            need(dve, "m_ready", FIRST.index(("KT", "c", 0)) + 1)
            key_norm(0, "c", 1, 1)
            dve.wait_ge(small_in, 7 * 16)
            dve.tensor_scalar(cos_d[:], cos_d[:], qw_d[:, 0:1], None, ALU.mult)
            dve.tensor_scalar(sin_d[:], sin_d[:], qw_d[:, 0:1], None, ALU.mult)
            dve.tensor_tensor(cos_t[:], cos_t[:], kw_t[:], ALU.mult)
            dve.tensor_tensor(sin_t[:, 0:HD // 2], sin_t[:, 0:HD // 2], kw_t[:, HD // 2:], ALU.mult)
            dve.tensor_tensor(sin_t[:, HD // 2:], sin_t[:, HD // 2:], kw_t[:, 0:HD // 2], ALU.mult).then_inc(tab_done, 1)
            dve.wait_ge(x_in, 16)
            norm_stats(0, 0)
            norm_x(0, 0)
            split_context(1, 2)
            low_x(0, 0)
            dve.memset(o_ps[:], 0.0).then_inc(wlo_done, 1)
            for half in range(2):
                use = FIRST.index(("K", "s", half))
                key_stats(0, "s", half)
                key_norm(0, "s", half, use)
                if half == 0:
                    dve.wait_ge(tab_done, 1)
                key_sin(0, half)
            for k in range(2):
                cols = slice(k * CH, (k + 1) * CH)
                dve.wait_ge(wo_hi_done, k + 1)
                dve.tensor_tensor(wo_lo[:].rearrange("p h n -> p (h n)")[:, cols], wo_stage[k],
                                  wo_hi[:].rearrange("p h n -> p (h n)")[:, cols].bitcast(F32), ALU.subtract
                                  ).then_inc(wo_lo_done, 1)
            rope(0, 0)
            with dve.Fori(0, NT // 2) as j:
                for a in range(2):
                    for p in range(UNITS):
                        n, b = 16 * j + 8 * a + p, p % 2
                        tile = 2 * j + a
                        late = LATE[p - 1] if p else None
                        kind, src, half = USES[late] if late is not None else ("", "", 0)
                        if kind == "K":
                            key_stats(tile + 1, src, half)
                        elif kind == "LN":
                            low_x(tile + 1, 1 - a)
                        need(dve, "st_ready", n + 1)
                        need(dve, "qrs_done", n - 1)
                        dve.tensor_scalar(q_ms[:, b], q_ps[b][:, 0:ST], HD * 1e-6, None, ALU.add).then_inc(sg["ms_done"], 1)
                        with dve.If(j > 0) if 8 * a + p == 0 else nullcontext():
                            need(dve, "t_ready", n)
                            need(dve, "pv_ready", n - 2)
                            dve.tensor_copy(probT[:, 1 - b], t_ps[:].rearrange("p (s r) -> p s r", s=ST)
                                            ).then_inc(sg["pt_done"], 1)
                        if p == 2:
                            with dve.If(j > 0) if a == 0 else nullcontext():
                                need(dve, "out_ready", 8 * tile)
                                dve.tensor_tensor(xres[:, ds(X0 + 2 * tile - 2, 2), :], out_ps[:].rearrange("p (t d) -> p t d", t=2),
                                                  xres[:, ds(X0 + 2 * tile - 2, 2), :], ALU.add).then_inc(sg["x_done"], 1)
                        need(dve, "s_ready", n + 1)
                        dve.tensor_reduce(s_max[:, b], s_ps[b][:].rearrange("p (s k) -> p s k", s=ST), AX, ALU.max
                                          ).then_inc(sg["max_done"], 1)
                        need(dve, "qrs_done", n + 1)
                        need(dve, "max_done", n + 1)
                        need(dve, "exp_done", n - 1)
                        dve.scalar_tensor_tensor(s_bias[:, b], s_max[:, b], -1.0, q_rs[:, b], ALU.mult, ALU.mult
                                                 ).then_inc(sg["nb_done"], 1)
                        if kind == "K":
                            key_norm(tile + 1, src, half, late)

                        def invert():
                            need(dve, "exp_done", n + 1)
                            need(dve, "pn_done", n - 1)
                            dve.reciprocal(s_inv[:, b], s_sum[:, b]).then_inc(sg["inv_done"], 1)

                        rope(n + 1, 1 - b, between=invert)
                        low_out(n - 1, 1 - b)
                        if kind == "K" and src == "s":
                            key_sin(tile + 1, half)
                        if p == 1:
                            norm_stats(tile + 1, 2 * tile + 2)
                        if p == 2:
                            norm_x(tile + 1, 2 * tile + 2)
                        if p == 6:
                            split_context(a, tile + 3)
            N = NT * UNITS
            need(dve, "t_ready", N)
            need(dve, "pv_ready", N - 2)
            dve.tensor_copy(probT[:, 1], t_ps[:].rearrange("p (s r) -> p s r", s=ST)).then_inc(sg["pt_done"], 1)
            low_out(N - 1, 1)
            need(dve, "out_ready", N)
            dve.tensor_tensor(xres[:, X0 + TT - 2:X0 + TT, :], out_ps[:].rearrange("p (t d) -> p t d", t=2),
                              xres[:, X0 + TT - 2:X0 + TT, :], ALU.add).then_inc(sg["x_done"], 1)

        @block.tensor
        def _(pe):
            sg.give_credit(pe, PE_S)
            EVACS = sum(1 for use in USES if use[0] in ("V", "KT"))

            def bank_free(tile, use):
                order, back = (USES, 1)
                if isinstance(tile, int) and tile == 0:
                    order, back = FIRST, len(FIRST_BANKS)
                elif use == 0:
                    return
                use -= back
                if use < 0:
                    return
                kind, src, half = order[use]
                if kind == "K":
                    need(pe, "kn_done", 4 * tile + KSEQ[(src, half)] + 1)
                elif kind == "LN":
                    need(pe, "xlo_done", tile + 1)
                else:
                    need(pe, "m_free_act", EVACS * tile + sum(1 for u in order[:use + 1] if u[0] in ("V", "KT")))

            def misc_pe(tile, use, par):
                (kind, src, half), ps = use_of(tile, use)
                bank_free(tile, use)
                if kind in "KV":
                    if src == "c":
                        need(pe, "clo_done", tile + 1)
                        left = [(cT_hi[:, c, half * P:(half + 1) * P], cT_lo[:, c, half * P:(half + 1) * P]) for c in range(CK)]
                    else:
                        need(pe, "xlo_done", tile + 1)
                        left = [(xnT_hi[:, par, c, half * P:(half + 1) * P], xnT_lo[:, par, c, half * P:(half + 1) * P])
                                for c in range(CK)]
                    for c in range(CK):
                        last = matmul3(pe, ps[:], left[c], kv_weight(src, 0 if kind == "K" else 1, c), c == 0, c == CK - 1)
                elif kind == "KT":
                    if src == "c":
                        need(pe, "kn_done", 4 * tile + KSEQ[(src, half)] + 1)
                    else:
                        need(pe, "kr_done", 2 * tile + half + 1)
                    for g in range(G):
                        last = pe.transpose(ps[:, g * P:(g + 1) * P], (kn if src == "c" else kr)[:, g], ident[:])
                else:
                    need(pe, "xn_done", tile + 1)
                    for c in range(CK):
                        for t in range(2):
                            last = pe.transpose(ps[:, c * T + t * P:c * T + (t + 1) * P], xn[:, t, c * P:(c + 1) * P], ident[:])
                last.then_inc(sg["m_ready"], 1)

            def project_q(n, tile, par, p):
                b = p % 2
                need(pe, "xlo_done", tile + 1)
                need(pe, "ms_done", n - 1)
                for hh in range(2):
                    for c in range(CK):
                        last = matmul3(pe, q_ps[b][:, hh * T:(hh + 1) * T], q_weight(2 * p + hh, c),
                                       (xnT_hi[:, par, c, :], xnT_lo[:, par, c, :]), c == 0, c == CK - 1)
                last.then_inc(sg["q_ready"], 1)

            def sum_squares(n, b):
                need(pe, "sq_done", n + 1)
                need(pe, "rope_done", n + 1)
                for s in range(ST):
                    last = pe.matmul(q_ps[b][:, s:s + 1], sq[:, s], consts["ones"][:, 0:1], start=True, stop=True)
                last.then_inc(sg["st_ready"], 1)

            def scores(n, tile, par, p):
                b, g = p % 2, p // 2
                need(pe, "qr_done", n + 1)
                need(pe, "exp_done", n - 1)
                need(pe, "m_free_act", EVACS * (tile + 1))
                for s in range(ST):
                    pe.matmul(s_ps[b][:, s * P:(s + 1) * P], qT[:, b, s], keysT[:, par, s, g, :], start=(s == 0), stop=False,
                              skip_group_check=True)
                own = s_ps[b][:].rearrange("p (s c k) -> p s c k", s=ST, c=2)[:, :, 1]
                last = pe.matmul(own, consts["mask_rows"][:], along(consts["causal"][:], 1, ST), start=False, stop=True,
                                 skip_group_check=True)
                last.then_inc(sg["s_ready"], 1)

            def transpose_probs(m, b):
                need(pe, "pn_done", m + 1)
                need(pe, "pt_done", m)
                for s in range(ST):
                    last = pe.transpose(t_ps[:, s * P:(s + 1) * P], prob[:, b, s], ident[:])
                last.then_inc(sg["t_ready"], 1)

            def attend(m, par, p):
                b, g = p % 2, p // 2
                need(pe, "pt_done", m + 1)
                need(pe, "olo_done", m)
                for s in range(ST):
                    last = pe.matmul(o_ps[:, s * P:(s + 1) * P], vals[:, par, s, g * P:(g + 1) * P], probT[:, b, s],
                                     start=True, stop=True)
                last.then_inc(sg["pv_ready"], 1)

            def project_out(m, tile, p):
                b = p % 2
                need(pe, "olo_done", m + 1)
                if p == 0:
                    need(pe, "x_done", tile)
                for hh in range(2):
                    for t in range(2):
                        rows = slice(t * P, (t + 1) * P)
                        last = matmul3(pe, out_ps[:, t * D:(t + 1) * D], (attT_hi[:, b, hh, rows], attT_lo[:, b, hh, rows]),
                                       (wo_hi[:, 2 * p + hh], wo_lo[:, 2 * p + hh]), p == 0 and hh == 0 and t == 0,
                                       p == UNITS - 1 and hh == 1, skip=True)
                last.then_inc(sg["out_ready"], 1)

            for use in range(NU):
                if use == 0:
                    pe.wait_ge(wlo_done, 1)
                if FIRST[use] == ("K", "s", 0):
                    pe.wait_ge(wlo_done, 2)
                misc_pe(0, use, 0)
            pe.wait_ge(wlo_done, 4)
            project_q(0, 0, 0, 0)
            pe.wait_ge(wo_lo_done, 2)
            with pe.Fori(0, NT // 2) as j:
                for a in range(2):
                    for p in range(UNITS):
                        k = 8 * a + p
                        n, tile = 16 * j + k, 2 * j + a
                        sum_squares(n, p % 2)
                        with pe.If(j > 0) if k == 0 else nullcontext():
                            transpose_probs(n - 1, 1 - p % 2)
                        scores(n, tile, a, p)
                        k1 = k + 1
                        project_q(n + 1, 2 * j + k1 // 8, (k1 // 8) % 2, k1 % 8)
                        with pe.If(j > 0) if k == 0 else nullcontext():
                            attend(n - 1, a if p > 0 else 1 - a, (p - 1) % 8)
                        if MIDDLE[p] is not None:
                            misc_pe(tile + 1, MIDDLE[p], 1 - a)
                        with pe.If(j > 0) if k < 2 else nullcontext():
                            project_out(n - 2, tile - (1 if p < 2 else 0), (p - 2) % 8)
                        if LATE[p] is not None:
                            misc_pe(tile + 1, LATE[p], 1 - a)
            N = NT * UNITS
            transpose_probs(N - 1, 1)
            attend(N - 1, 1, UNITS - 1)
            project_out(N - 2, NT - 1, UNITS - 2)
            project_out(N - 1, NT - 1, UNITS - 1)


LAYER1_ATTENTION = {
    "wkvcT": ([64, D], F32, None),
    "wkr": ([64, 64], F32, None),
    "wkvc": ([P, CK, 64], F32, "(c p) n -> p c n"),
    "wdq": ([P, CK, 96], F32, "(c p) n -> p c n"),
    "cos_k": ([P, 64], F32, None),
    "sin_k": ([P, 64], F32, None),
    "segT": ([SEQ, NSEQ], mybir.dt.int32, None),
    "key_no": ([SEQ, SEQ], F32, None),
    "wuqT": ([P, H, 96], F32, "(h p) n -> p h n"),
    "wukT": ([P, H, 64], F32, "(h p) n -> p h n"),
    "wqr": ([96, H, 64], F32, "k (h r) -> k h r"),
    "wuvT": ([P, H, 64], F32, "(h p) n -> p h n"),
    "wo1": ([P, H, D], F32, "(h p) n -> p h n"),
}


def layer0_ffn(nc, dram, xres, consts, ahead):
    RANK = 8
    with ExitStack() as ctx:
        taken = Taken(nc, ctx)
        def sb(name, shape, dt=F32):
            return ctx.enter_context(nc.sbuf_tensor(name, shape, dt))

        fac = sb("b_fac", [P, RANK, CK, D])
        fsum = sb("b_fsum", [P, CK, D])
        f_hi = sb("b_f_hi", [P, CK, D], F32R)
        f_lo = sb("b_f_lo", [P, CK, D], F32R)
        bias = sb("b_bias", [P, D])
        xn = sb("b_xn", [P, 2, 2, D])
        xnT_hi = sb("b_xnT_hi", [P, 2, CK, T], F32R)
        xnT_lo = sb("b_xnT_lo", [P, 2, CK, T], F32R)
        bst = sb("b_bst", [P, 2, 6])
        mv = sb("b_mv", [P, 2, 2])
        var = sb("b_var", [P, 2])
        rstd = sb("b_rstd", [P, 2])
        spare = sb("b_spare", [P, 1])
        n_ps = [ctx.enter_context(nc.psum_tensor(f"b_n_ps{k}", [P, 512], F32)) for k in range(2)]
        o_ps = [ctx.enter_context(nc.psum_tensor(f"b_o_ps{k}", [P, 512], F32)) for k in range(2)]

        PE_S = ["b_nT_ready", "b_out_ready"]
        ACT_S = ["b_hi_done"]
        DVE_S = ["b_bst_done", "b_mv_done", "b_var_done", "b_xn_done", "b_lo_done", "b_x_done"]
        POOL_S = ["b_rstd_done", "b_bias_done"]
        sg = Signals(taken, PE_S + ACT_S + DVE_S + POOL_S)
        need = sg.need
        f_in = [taken.take(f"b_f_in{r}") for r in range(RANK)]
        bias_in = taken.take("b_bias_in")
        ahead_in = taken.take("b_ahead_in")
        fsum_done = taken.take("b_fsum_done")
        fhi_done = taken.take("b_fhi_done")
        flo_done = taken.take("b_flo_done")

        block = ctx.enter_context(nc.Block())

        @block.sync
        def _(sp):
            for r in range(RANK):
                sp.dma_start(fac[:, r], dram["factors"][r].rearrange("(c p) n -> p c n", p=P)).then_inc(f_in[r], 16)
            sp.dma_start(bias[:], dram["ffn_bias"].partition_broadcast(P)).then_inc(bias_in, 16)
            for name, (_, _, how) in LAYER1_ATTENTION.items():
                src = dram[name] if how is None else dram[name].rearrange(how, **{"p": P} if "p)" in how else {"h": H})
                sp.dma_start(ahead[name][:], src).then_inc(ahead_in, 16)
            sp.wait_ge(ahead_in, 16 * len(LAYER1_ATTENTION))

        @block.gpsimd
        def _(pool):
            sg.give_credit(pool, POOL_S)
            taken.clear_last(pool)

            def root(tile):
                need(pool, "b_var_done", tile + 1)
                pool.tensor_tensor(rstd[:], var[:], consts["minus_half"][:, 0:2], ALU.pow).then_inc(sg["b_rstd_done"], 1)

            def add_bias(tile):
                need(pool, "b_xn_done", tile + 1)
                rows = xres[:, ds(X0 + 2 * tile, 2), :] if not isinstance(tile, int) else xres[:, X0 + 2 * tile:X0 + 2 * tile + 2, :]
                pool.tensor_tensor(rows, rows, along(bias[:], 1, 2), ALU.add).then_inc(sg["b_bias_done"], 1)

            root(0)
            need(pool, "b_xn_done", 1)
            root(1)
            pool.wait_ge(bias_in, 16)
            add_bias(0)
            add_bias(1)
            with pool.Fori(0, NT // 2 - 1) as j:
                for a in range(2):
                    root(2 * j + a + 2)
                    add_bias(2 * j + a + 2)

        @block.scalar
        def _(act):
            sg.give_credit(act, ACT_S)
            act.wait_ge(fsum_done, 1)
            act.activation(f_hi[:], fsum[:], ACT.Copy).then_inc(fhi_done, 1)

            def high(tile, par):
                need(act, "b_nT_ready", tile + 1)
                need(act, "b_out_ready", tile - 1)
                act.activation(xnT_hi[:, par], n_ps[par][:].rearrange("p (c t) -> p c t", c=CK), ACT.Copy
                               ).then_inc(sg["b_hi_done"], 1)

            high(0, 0)
            with act.Fori(0, NT // 2 - 1) as j:
                for a in range(2):
                    high(2 * j + a + 1, 1 - a)
            high(NT - 1, 1)

        @block.vector
        def _(dve):
            sg.give_credit(dve, DVE_S)

            def row(r):
                return xres[:, X0 + r, :] if isinstance(r, int) else xres[:, ds(X0 + r, 1), :].rearrange("p a d -> p (a d)")

            def norm_stats(tile):
                for t in range(2):
                    last = dve.bn_stats(bst[:, t], row(2 * tile + t))
                last.then_inc(sg["b_bst_done"], 1)
                need(dve, "b_bst_done", tile + 1)
                dve.memset(spare[:], 0.0)
                for t in range(2):
                    last = dve.bn_aggr(mv[:, t], bst[:, t])
                last.then_inc(sg["b_mv_done"], 1)
                need(dve, "b_mv_done", tile + 1)
                dve.tensor_scalar(var[:], mv[:, :, 1], 1e-5, None, ALU.add).then_inc(sg["b_var_done"], 1)

            def norm_rows(tile, par):
                need(dve, "b_rstd_done", tile + 1)
                need(dve, "b_nT_ready", tile - 1)
                for t in range(2):
                    last = dve.tensor_scalar(xn[:, par, t], row(2 * tile + t), mv[:, t, 0:1], rstd[:, t:t + 1],
                                             ALU.subtract, ALU.mult)
                last.then_inc(sg["b_xn_done"], 1)

            def low(tile, par):
                need(dve, "b_hi_done", tile + 1)
                dve.tensor_tensor(xnT_lo[:, par], n_ps[par][:].rearrange("p (c t) -> p c t", c=CK),
                                  xnT_hi[:, par].bitcast(F32), ALU.subtract).then_inc(sg["b_lo_done"], 1)

            for tile in range(2):
                norm_stats(tile)
                norm_rows(tile, tile)
            for r in range(RANK):
                dve.wait_ge(f_in[r], 16)
                if r == 1:
                    dve.tensor_tensor(fsum[:], fac[:, 0], fac[:, 1], ALU.add).then_inc(flo_done, 1)
                elif r > 1:
                    dve.wait_ge(flo_done, r - 1)
                    dve.tensor_tensor(fsum[:], fsum[:], fac[:, r], ALU.add).then_inc(flo_done, 1)
            dve.wait_ge(flo_done, RANK - 1)
            dve.tensor_scalar(fsum[:], fsum[:], RANK ** -0.5, None, ALU.mult).then_inc(fsum_done, 1)
            dve.wait_ge(fhi_done, 1)
            dve.tensor_tensor(f_lo[:], fsum[:], f_hi[:].bitcast(F32), ALU.subtract).then_inc(flo_done, 1)
            low(0, 0)

            def add_x(tile, a):
                need(dve, "b_out_ready", tile + 1)
                need(dve, "b_bias_done", tile + 1)
                rows = xres[:, ds(X0 + 2 * tile, 2), :] if not isinstance(tile, int) else xres[:, X0 + 2 * tile:X0 + 2 * tile + 2, :]
                dve.tensor_tensor(rows, o_ps[a][:].rearrange("p (t d) -> p t d", t=2), rows, ALU.add).then_inc(sg["b_x_done"], 1)

            with dve.Fori(0, NT // 2 - 1) as j:
                for a in range(2):
                    tile = 2 * j + a
                    norm_stats(tile + 2)
                    low(tile + 1, 1 - a)
                    norm_rows(tile + 2, a)
                    add_x(tile, a)
            low(NT - 1, 1)
            add_x(NT - 2, 0)
            add_x(NT - 1, 1)

        @block.tensor
        def _(pe):
            sg.give_credit(pe, PE_S)

            def transpose_norm(tile, par):
                need(pe, "b_xn_done", tile + 1)
                need(pe, "b_lo_done", tile - 1)
                for c in range(CK):
                    for t in range(2):
                        last = pe.transpose(n_ps[par][:, c * T + t * P:c * T + (t + 1) * P], xn[:, par, t, c * P:(c + 1) * P],
                                            consts["ident"][:])
                last.then_inc(sg["b_nT_ready"], 1)

            def product(tile, a):
                need(pe, "b_lo_done", tile + 1)
                need(pe, "b_x_done", tile - 1)
                for t in range(2):
                    for c in range(CK):
                        last = matmul3(pe, o_ps[a][:, t * D:(t + 1) * D],
                                       (xnT_hi[:, a, c, t * P:(t + 1) * P], xnT_lo[:, a, c, t * P:(t + 1) * P]),
                                       (f_hi[:, c], f_lo[:, c]), c == 0, c == CK - 1)
                last.then_inc(sg["b_out_ready"], 1)

            transpose_norm(0, 0)
            transpose_norm(1, 1)
            pe.wait_ge(flo_done, RANK)
            with pe.Fori(0, NT // 2 - 1) as j:
                for a in range(2):
                    product(2 * j + a, a)
                    transpose_norm(2 * j + a + 2, a)
            product(NT - 2, 0)
            product(NT - 1, 1)


def layer1_attention(nc, dram, xres, consts, ahead):
    R, KC, QC = 64, 64, 96
    HR = R // 2
    NU = 2 * TT
    SCALE = float(np.float32(1.0) / np.float32(np.sqrt(HD + R)))
    with ExitStack() as ctx:
        taken = Taken(nc, ctx)
        def sb(name, shape, dt=F32):
            return ctx.enter_context(nc.sbuf_tensor(name, shape, dt))

        wuqT, wukT, wuvT, wo, wqr = (ahead[n] for n in ("wuqT", "wukT", "wuvT", "wo1", "wqr"))
        wdq, wkvcT, wkr, wkvc = (ahead[n] for n in ("wdq", "wkvcT", "wkr", "wkvc"))
        cos_k, sin_k, seg_i, key_no = (ahead[n] for n in ("cos_k", "sin_k", "segT", "key_no"))
        wkv = sb("d_wkv", [P, CK, P])
        wq_hi = sb("d_wq_hi", [QC, H, P], F32R)
        wq_lo = sb("d_wq_lo", [QC, H, P], F32R)
        wdq_hi = sb("d_wdq_hi", [P, CK, QC], F32R)
        wdq_lo = sb("d_wdq_lo", [P, CK, QC], F32R)
        wkv_hi = sb("d_wkv_hi", [P, CK, P], F32R)
        wkv_lo = sb("d_wkv_lo", [P, CK, P], F32R)
        wn = sb("d_wn", [P, H // 2, D])
        cT = sb("d_cT", [P, 2, CK, 512])
        cT_hi = sb("d_cT_hi", [P, 2, CK, 512], F32R)
        cT_lo = sb("d_cT_lo", [P, 2, CK, 512], F32R)
        kv = sb("d_kv", [P, 4, P])
        kvc = sb("d_kvc", [P, 4, R])
        kvs = sb("d_kvs", [P, 4, R])
        keysT = sb("d_keysT", [P, NTOK])
        vdiag = sb("d_vdiag", [P, TT, P])
        vcur = sb("d_vcur", [P, 2, P])
        seg = sb("d_seg", [SEQ, NSEQ])
        seg_lo = sb("d_seg_lo", [SEQ, NSEQ])
        bad = sb("d_bad", [SEQ, NSEQ, SEQ])
        bad2 = sb("d_bad2", [SEQ, NSEQ, SEQ])
        mask = sb("d_mask", [P, NSEQ, SEQ], BF16)
        xn = sb("d_xn", [P, 2, D])
        xnT_hi = sb("d_xnT_hi", [P, CK, T], F32R)
        xnT_lo = sb("d_xnT_lo", [P, CK, T], F32R)
        qcT_hi = sb("d_qcT_hi", [QC, 2, T], F32R)
        qcT_lo = sb("d_qcT_lo", [QC, 2, T], F32R)
        qf = sb("d_qf", [P, 8, P])
        qcos = sb("d_qcos", [P, 8, R])
        qsin = sb("d_qsin", [P, 8, R])
        qT = sb("d_qT", [P, 2, 4, 2, 2, SEQ])
        s_max = sb("d_s_max", [P, 8])
        s_sum = sb("d_s_sum", [P, 8])
        s_inv = sb("d_s_inv", [P, 2, 8])
        sc = sb("d_sc", [P, 2, 8, SEQ])
        prob = sb("d_prob", [P, 2, 8, SEQ])
        probT = sb("d_probT", [P, 2, 512])
        attT = sb("d_attT", [P, 2, 4, P])
        bst = sb("d_bst", [P, 2, 6])
        mv = sb("d_mv", [P, 2, 2])
        var = sb("d_var", [P, 2])
        rstd = sb("d_rstd", [P, 2])
        spare = sb("d_spare", [P, 1])

        def bank(name):
            return ctx.enter_context(nc.psum_tensor(name, [P, 512], F32))

        q_ps = ctx.enter_context(nc.psum_tensor("d_q_ps", [P, 2, 512], F32))
        qT_ps, s_ps, t_ps, o_ps, out_ps, m_ps = (bank("d_ps_" + n) for n in ("qT", "s", "t", "o", "out", "m"))

        PE_S = ["d_q_ready", "d_qT_ready", "d_s_ready", "d_t_ready", "d_pv_ready", "d_out_ready", "d_nT_ready", "d_qc_ready"]
        ACT_S = ["d_abs_done", "d_qTa_done", "d_exp_done", "d_pt_done", "d_ot_done", "d_xhi_done", "d_qchi_done"]
        DVE_S = ["d_rope_done", "d_qTb_done", "d_max_done", "d_sub_done", "d_sum_done", "d_inv_done", "d_x_done", "d_v_done",
                 "d_bst_done", "d_mv_done", "d_var_done", "d_xn_done", "d_xlo_done", "d_qclo_done"]
        POOL_S = ["d_qf_done", "d_pn_done", "d_rstd_done"]
        sg = Signals(taken, PE_S + ACT_S + DVE_S + POOL_S, less=("d_ot_done",))
        need = sg.need

        def sem(name):
            return taken.take(name)

        c_in = [sem("d_c_in0"), sem("d_c_in1")]
        fold_ready, fold_hi, fold_lo = sem("d_fold_ready"), sem("d_fold_hi"), sem("d_fold_lo")
        wn_ready, wn_done = sem("d_wn_ready"), sem("d_wn_done")
        wk_ready, wk_done, wsmall_hi, wsmall_lo = sem("d_wk_ready"), sem("d_wk_done"), sem("d_wsmall_hi"), sem("d_wsmall_lo")
        mask_step, mask_done, cleared = sem("d_mask_step"), sem("d_mask_done"), sem("d_cleared")
        chi_done, clo_done = sem("d_chi_done"), sem("d_clo_done")
        kv_ready, kv_act, kv_rope, kv_done, kvT_ready, kvT_done = (sem("d_" + n) for n in (
            "kv_ready", "kv_act", "kv_rope", "kv_done", "kvT_ready", "kvT_done"))
        KB = NTOK // 512
        kv_banks, kvT_banks = (t_ps, o_ps), (out_ps, qT_ps)

        block = ctx.enter_context(nc.Block())

        @block.sync
        def _(sp):
            for k in range(2):
                sp.dma_start(cT[:, k], dram["ctxT"][:, k * 512:(k + 1) * 512].rearrange("(c p) n -> p c n", p=P)
                             ).then_inc(c_in[k], 16)
            for k in range(2, KB):
                sp.wait_ge(clo_done, k - 1)
                sp.dma_start(cT[:, k % 2], dram["ctxT"][:, k * 512:(k + 1) * 512].rearrange("(c p) n -> p c n", p=P)
                             ).then_inc(c_in[k % 2], 16)

        @block.gpsimd
        def _(pool):
            sg.give_credit(pool, POOL_S)
            taken.clear_last(pool)
            pool.memset(mask[:], 0.0)
            pool.memset(vdiag[:], 0.0).then_inc(cleared, 1)
            def root(tile):
                need(pool, "d_var_done", tile + 1)
                pool.tensor_tensor(rstd[:], var[:], consts["minus_half"][:, 0:2], ALU.pow).then_inc(sg["d_rstd_done"], 1)

            def add_rope(n):
                need(pool, "d_rope_done", n + 1)
                need(pool, "d_qT_ready", 2 * n)
                pool.tensor_tensor(qf[:, :, KC:], qcos[:], qsin[:], ALU.add).then_inc(sg["d_qf_done"], 1)

            root(0)
            for k in range(KB):
                pool.wait_ge(kv_rope, k + 1)
                pool.tensor_tensor(kv[:, :, KC:], kvc[:], kvs[:], ALU.add).then_inc(kv_done, 1)
            add_rope(0)
            add_rope(1)
            with pool.Fori(0, NU // 8) as j:
                for k in range(8):
                    n = 8 * j + k
                    need(pool, "d_inv_done", n + 1)
                    pool.tensor_tensor(prob[:, k % 2], prob[:, k % 2], along(s_inv[:, k % 2], 2, SEQ), ALU.mult
                                       ).then_inc(sg["d_pn_done"], 1)
                    if k % 4 == 0:
                        root(2 * j + k // 4 + 1)
                    add_rope(n + 2)

        @block.scalar
        def _(act):
            sg.give_credit(act, ACT_S)
            act.activation(wdq_hi[:], wdq[:], ACT.Copy).then_inc(wsmall_hi, 1)
            act.activation(wkv[:, :, 0:KC], wkvc[:], ACT.Copy).then_inc(wk_done, 1)
            act.wait_ge(wk_ready, 1)
            act.activation(wkv[:, :, KC:], m_ps[:, 0:CK * R].rearrange("p (c r) -> p c r", c=CK), ACT.Copy).then_inc(wk_done, 1)
            act.wait_ge(wk_done, 2)
            act.activation(wkv_hi[:], wkv[:], ACT.Copy).then_inc(wsmall_hi, 1)

            def split_context(k):
                act.wait_ge(c_in[k % 2], 16 * (k // 2 + 1))
                if k >= 2:
                    act.wait_ge(kv_ready, k - 1)
                act.activation(cT_hi[:, k % 2], cT[:, k % 2], ACT.Copy).then_inc(chi_done, 1)

            def keys_out(k):
                act.wait_ge(kv_ready, k + 1)
                if k >= 1:
                    act.wait_ge(kvT_ready, k)
                ps = kv_banks[k % 2][:].rearrange("p (t n) -> p t n", t=4)
                act.activation(kv[:, :, 0:KC], ps[:, :, 0:KC], ACT.Copy)
                for s in range(2):
                    last = act.activation(vdiag[s * SEQ:(s + 1) * SEQ, 4 * k:4 * k + 4, s * KC:(s + 1) * KC],
                                          ps[s * SEQ:(s + 1) * SEQ, :, 0:KC], ACT.Copy)
                last.then_inc(kv_act, 1)

            def keys_transposed(k):
                act.wait_ge(kvT_ready, k + 1)
                act.activation(keysT[:, k * 512:(k + 1) * 512], kvT_banks[k % 2][:], ACT.Copy).then_inc(kvT_done, 1)

            def fold_queries_out(k):
                act.wait_ge(fold_ready, k + 1)
                act.activation(wq_hi[:, 8 * k:8 * k + 8, 0:KC], q_ps[0:QC, k].rearrange("p (h c) -> p h c", h=8), ACT.Copy
                               ).then_inc(fold_hi, 1)

            def fold_values_out(k):
                act.wait_ge(wn_ready, k + 1)
                act.activation(wn[:, 2 * k:2 * k + 2, :], s_ps[:].rearrange("p (g d) -> p g d", g=2), ACT.Copy
                               ).then_inc(wn_done, 1)

            def norm_high(tile):
                need(act, "d_nT_ready", tile + 1)
                need(act, "d_qc_ready", tile)
                act.activation(xnT_hi[:], m_ps[:].rearrange("p (c t) -> p c t", c=CK), ACT.Copy).then_inc(sg["d_xhi_done"], 1)

            def qc_high(tile, par):
                need(act, "d_qc_ready", tile + 1)
                need(act, "d_q_ready", 4 * (tile - 1))
                act.activation(qcT_hi[:, par], m_ps[0:QC, 0:T], ACT.Copy).then_inc(sg["d_qchi_done"], 1)

            def absorbed(n):
                need(act, "d_q_ready", n + 1)
                need(act, "d_qT_ready", 2 * n)
                act.activation(qf[:, :, 0:KC], q_ps[:].rearrange("p b (h n) -> p (b h) n", n=P)[:, :, 0:KC], ACT.Copy
                               ).then_inc(sg["d_abs_done"], 1)

            def to_sequences(half, b):
                return (qT[:, b, 2 * half:2 * half + 2].rearrange("p q s h t -> p q h s t"),
                        qT_ps[:].rearrange("p (q h s t) -> p q h s t", q=2, h=2, s=2))

            def rowsT(n, b):
                need(act, "d_qT_ready", 2 * n + 1)
                need(act, "d_s_ready", n - 1)
                dst, src = to_sequences(0, b)
                for q in range(2):
                    last = act.activation(dst[:, q], src[:, q], ACT.Copy)
                last.then_inc(sg["d_qTa_done"], 1)

            def probs_out(m, b):
                need(act, "d_t_ready", m + 1)
                need(act, "d_pv_ready", m - 1)
                act.activation(probT[:, b], t_ps[:], ACT.Copy).then_inc(sg["d_pt_done"], 1)

            def attention_out(m, b):
                need(act, "d_pv_ready", m + 1)
                need(act, "d_out_ready", m - 1)
                src = o_ps[:].rearrange("p (q h t) -> p q h t", q=4, h=2)
                for s in range(2):
                    for hh in range(2):
                        last = act.activation(attT[hh * KC:(hh + 1) * KC, b, :, s * SEQ:(s + 1) * SEQ],
                                              src[s * KC:(s + 1) * KC, :, hh, :], ACT.Copy)
                last.then_inc(sg["d_ot_done"], 1)

            split_context(0)
            split_context(1)
            act.wait_ge(cleared, 1)
            keys_out(0)
            act.activation(wq_hi[:, :, KC:], wqr[:], ACT.Copy).then_inc(fold_hi, 1)
            fold_queries_out(0)
            fold_queries_out(1)
            keys_transposed(0)
            norm_high(0)
            keys_out(1)
            split_context(2)
            qc_high(0, 0)
            keys_transposed(1)
            fold_values_out(0)
            keys_out(2)
            split_context(3)
            absorbed(0)
            fold_values_out(1)
            keys_transposed(2)
            keys_out(3)
            keys_transposed(3)
            fold_values_out(2)
            rowsT(0, 0)
            fold_values_out(3)
            absorbed(1)
            act.wait_ge(mask_done, 1)
            with act.Fori(0, NU // 8) as j:
                for k in range(8):
                    n, b = 8 * j + k, k % 2
                    if k % 4 == 1:
                        norm_high(2 * j + k // 4 + 1)
                    if k % 4 == 2:
                        qc_high(2 * j + k // 4 + 1, 1 - k // 4)
                    need(act, "d_sub_done", n + 1)
                    need(act, "d_t_ready", n - 1)
                    act.activation(prob[:, b], sc[:, b], ACT.Exp, scale=SCALE).then_inc(sg["d_exp_done"], 1)
                    rowsT(n + 1, 1 - b)
                    attention_out(n - 1, 1 - b)
                    absorbed(n + 2)
                    probs_out(n, b)
            attention_out(NU - 1, 1)

        @block.vector
        def _(dve):
            sg.give_credit(dve, DVE_S)

            def row(r):
                return xres[:, X0 + r, :] if isinstance(r, int) else xres[:, ds(X0 + r, 1), :].rearrange("p a d -> p (a d)")

            def norm(tile):
                for t in range(2):
                    last = dve.bn_stats(bst[:, t], row(2 * tile + t))
                last.then_inc(sg["d_bst_done"], 1)
                need(dve, "d_bst_done", tile + 1)
                dve.memset(spare[:], 0.0)
                for t in range(2):
                    last = dve.bn_aggr(mv[:, t], bst[:, t])
                last.then_inc(sg["d_mv_done"], 1)
                need(dve, "d_mv_done", tile + 1)
                dve.tensor_scalar(var[:], mv[:, :, 1], 1e-5, None, ALU.add).then_inc(sg["d_var_done"], 1)
                need(dve, "d_rstd_done", tile + 1)
                for t in range(2):
                    last = dve.tensor_scalar(xn[:, t], row(2 * tile + t), mv[:, t, 0:1], rstd[:, t:t + 1],
                                             ALU.subtract, ALU.mult)
                last.then_inc(sg["d_xn_done"], 1)

            def norm_low(tile):
                need(dve, "d_xhi_done", tile + 1)
                dve.tensor_tensor(xnT_lo[:], m_ps[:].rearrange("p (c t) -> p c t", c=CK), xnT_hi[:].bitcast(F32),
                                  ALU.subtract).then_inc(sg["d_xlo_done"], 1)

            def qc_low(tile, par):
                need(dve, "d_qchi_done", tile + 1)
                dve.tensor_tensor(qcT_lo[:, par], m_ps[0:QC, 0:T], qcT_hi[:, par].bitcast(F32), ALU.subtract
                                  ).then_inc(sg["d_qclo_done"], 1)

            def rope(n):
                need(dve, "d_abs_done", n + 1)
                need(dve, "d_qf_done", n)
                q = q_ps[:].rearrange("p b (h n) -> p (b h) n", n=P)
                dve.tensor_tensor(qcos[:], q[:, :, KC:], along(cos_k[:], 1, 8), ALU.mult)
                dve.tensor_tensor(qsin[:, :, 0:HR], q[:, :, KC + HR:], along(sin_k[:, 0:HR], 1, 8), ALU.mult)
                dve.tensor_tensor(qsin[:, :, HR:], q[:, :, KC:KC + HR], along(sin_k[:, HR:], 1, 8), ALU.mult
                                  ).then_inc(sg["d_rope_done"], 1)

            def rowsT(n, b):
                need(dve, "d_qT_ready", 2 * n + 2)
                need(dve, "d_s_ready", n - 1)
                dst = qT[:, b, 2:4].rearrange("p q s h t -> p q h s t")
                src = qT_ps[:].rearrange("p (q h s t) -> p q h s t", q=2, h=2, s=2)
                for q in range(2):
                    last = dve.tensor_copy(dst[:, q], src[:, q])
                last.then_inc(sg["d_qTb_done"], 1)

            def split_context(k):
                dve.wait_ge(chi_done, k + 1)
                dve.tensor_tensor(cT_lo[:, k % 2], cT[:, k % 2], cT_hi[:, k % 2].bitcast(F32), ALU.subtract
                                  ).then_inc(clo_done, 1)

            def rotate_keys(k):
                dve.wait_ge(kv_act, k + 1)
                if k >= 1:
                    dve.wait_ge(kv_done, k)
                ps = kv_banks[k % 2][:].rearrange("p (t n) -> p t n", t=4)
                dve.tensor_tensor(kvc[:], ps[:, :, KC:], along(cos_k[:], 1, 4), ALU.mult)
                dve.tensor_tensor(kvs[:, :, 0:HR], ps[:, :, KC + HR:], along(sin_k[:, 0:HR], 1, 4), ALU.mult)
                dve.tensor_tensor(kvs[:, :, HR:], ps[:, :, KC:KC + HR], along(sin_k[:, HR:], 1, 4), ALU.mult
                                  ).then_inc(kv_rope, 1)

            def fold_queries_low(k):
                dve.wait_ge(fold_hi, k + 2)
                dve.tensor_tensor(wq_lo[:, 8 * k:8 * k + 8, 0:KC], q_ps[0:QC, k].rearrange("p (h c) -> p h c", h=8),
                                  wq_hi[:, 8 * k:8 * k + 8, 0:KC].bitcast(F32), ALU.subtract).then_inc(fold_lo, 1)

            dve.wait_ge(wsmall_hi, 1)
            dve.tensor_tensor(wdq_lo[:], wdq[:], wdq_hi[:].bitcast(F32), ALU.subtract).then_inc(wsmall_lo, 1)
            dve.wait_ge(wsmall_hi, 2)
            dve.tensor_tensor(wkv_lo[:], wkv[:], wkv_hi[:].bitcast(F32), ALU.subtract).then_inc(wsmall_lo, 1)
            split_context(0)
            norm(0)
            split_context(1)
            dve.tensor_copy(seg[:], seg_i[:]).then_inc(mask_step, 1)
            dve.wait_ge(mask_step, 1)
            dve.tensor_scalar(seg_lo[:], seg[:], -float(LOOKBACK), None, ALU.add).then_inc(mask_step, 1)
            rotate_keys(0)
            dve.wait_ge(fold_hi, 1)
            dve.tensor_tensor(wq_lo[:, :, KC:], wqr[:], wq_hi[:, :, KC:].bitcast(F32), ALU.subtract).then_inc(fold_lo, 1)
            fold_queries_low(0)
            fold_queries_low(1)
            norm_low(0)
            rotate_keys(1)
            split_context(2)
            qc_low(0, 0)
            dve.wait_ge(mask_step, 2)
            dve.tensor_tensor(bad[:], along(key_no[:], 1, NSEQ), along(seg[:], 2, SEQ), ALU.is_gt)
            rotate_keys(2)
            split_context(3)
            dve.tensor_tensor(bad2[:], along(key_no[:], 1, NSEQ), along(seg_lo[:], 2, SEQ), ALU.is_lt).then_inc(mask_step, 1)
            rope(0)
            rotate_keys(3)
            dve.wait_ge(mask_step, 3)
            dve.tensor_tensor(bad[:], bad[:], bad2[:], ALU.add).then_inc(mask_step, 1)
            dve.wait_ge(mask_step, 4)
            dve.wait_ge(cleared, 1)
            dve.tensor_scalar(mask[0:SEQ], bad[:], MASKED, None, ALU.mult).then_inc(mask_step, 1)
            dve.memset(o_ps[:], 0.0).then_inc(mask_done, 1)
            rowsT(0, 0)
            rope(1)
            with dve.Fori(0, NU // 8) as j:
                for k in range(8):
                    n, b = 8 * j + k, k % 2
                    if k % 2 == 0:
                        with dve.If(j > 0) if k < 4 else nullcontext():
                            need(dve, "d_out_ready", n - 2)
                            r = 4 * j + k // 2
                            dve.tensor_tensor(xres[:, ds(r, 1), :].rearrange("p a d -> p (a d)"), out_ps[:, 0:D],
                                              xres[:, ds(r, 1), :].rearrange("p a d -> p (a d)"), ALU.add
                                              ).then_inc(sg["d_x_done"], 1)
                        need(dve, "d_pv_ready", n - 2)
                        dve.tensor_scalar(vcur[:, (k // 2) % 2], vdiag[:, ds(4 * j + k // 2, 1), :].rearrange("p a d -> p (a d)"),
                                          1.0, None, ALU.mult).then_inc(sg["d_v_done"], 1)
                    if k % 4 == 1:
                        norm_low(2 * j + k // 4 + 1)
                    if k % 4 == 2:
                        qc_low(2 * j + k // 4 + 1, 1 - k // 4)
                    need(dve, "d_s_ready", n + 1)
                    s3 = s_ps[:].rearrange("p (g k) -> p g k", g=8)
                    dve.tensor_reduce(s_max[:], s3, AX, ALU.max).then_inc(sg["d_max_done"], 1)
                    need(dve, "d_max_done", n + 1)
                    need(dve, "d_exp_done", n - 1)
                    dve.tensor_tensor(sc[:, b], s3, along(s_max[:], 2, SEQ), ALU.subtract).then_inc(sg["d_sub_done"], 1)
                    need(dve, "d_exp_done", n + 1)
                    dve.tensor_reduce(s_sum[:], prob[:, b], AX, ALU.add).then_inc(sg["d_sum_done"], 1)
                    need(dve, "d_sum_done", n + 1)
                    need(dve, "d_pn_done", n - 1)
                    dve.reciprocal(s_inv[:, b], s_sum[:]).then_inc(sg["d_inv_done"], 1)
                    if k % 4 == 0:
                        norm(2 * j + k // 4 + 1)
                    rowsT(n + 1, 1 - b)
                    rope(n + 2)
            for t in range(2):
                need(dve, "d_out_ready", NU - 2 + 2 * t)
                dve.tensor_tensor(xres[:, X0 + TT - 2 + t, :], out_ps[:, 0:D], xres[:, X0 + TT - 2 + t, :], ALU.add
                                  ).then_inc(sg["d_x_done"], 1)

        @block.tensor
        def _(pe):
            sg.give_credit(pe, PE_S)
            ident = consts["ident"]
            for c in range(CK):
                last = pe.matmul(m_ps[:, c * R:(c + 1) * R], wkvcT[:, c * P:(c + 1) * P], wkr[:], start=True, stop=True)
            last.then_inc(wk_ready, 1)
            def keys_of(k):
                pe.wait_ge(clo_done, k + 1)
                if k >= 2:
                    pe.wait_ge(kv_rope, k - 1)
                ps = kv_banks[k % 2]
                for t in range(4):
                    for c in range(CK):
                        last = matmul3(pe, ps[:, t * P:(t + 1) * P], (cT_hi[:, k % 2, c, t * P:(t + 1) * P],
                                                                      cT_lo[:, k % 2, c, t * P:(t + 1) * P]),
                                       (wkv_hi[:, c], wkv_lo[:, c]), c == 0, c == CK - 1)
                last.then_inc(kv_ready, 1)

            def transpose_keys(k):
                pe.wait_ge(kv_done, k + 1)
                if k >= 2:
                    pe.wait_ge(kvT_done, k - 1)
                for t in range(4):
                    last = pe.transpose(kvT_banks[k % 2][:, t * P:(t + 1) * P], kv[:, t], ident[:])
                last.then_inc(kvT_ready, 1)

            def fold_values(k):
                if k >= 1:
                    pe.wait_ge(wn_done, k)
                for g in range(2):
                    for hh in range(2):
                        h = 4 * k + 2 * g + hh
                        last = pe.matmul(s_ps[hh * KC:(hh + 1) * KC, g * D:(g + 1) * D],
                                         wuvT[:, h], wo[:, h], start=True, stop=True, skip_group_check=True)
                last.then_inc(wn_ready, 1)

            def transpose_norm(tile):
                need(pe, "d_xn_done", tile + 1)
                need(pe, "d_qclo_done", tile)
                for c in range(CK):
                    for t in range(2):
                        last = pe.transpose(m_ps[:, c * T + t * P:c * T + (t + 1) * P], xn[:, t, c * P:(c + 1) * P], ident[:])
                last.then_inc(sg["d_nT_ready"], 1)

            def compress(tile):
                need(pe, "d_xlo_done", tile + 1)
                for c in range(CK):
                    last = matmul3(pe, m_ps[0:QC, 0:T], (wdq_hi[:, c], wdq_lo[:, c]), (xnT_hi[:, c], xnT_lo[:, c]),
                                   c == 0, c == CK - 1)
                last.then_inc(sg["d_qc_ready"], 1)

            def queries(n, tile, par, u):
                t, half = u // 2, u % 2
                need(pe, "d_qclo_done", tile + 1)
                need(pe, "d_rope_done", n)
                for g in range(2):
                    last = matmul3(pe, q_ps[:, g], (qcT_hi[:, par, t * P:(t + 1) * P], qcT_lo[:, par, t * P:(t + 1) * P]),
                                   (wq_hi[:, 8 * half + 4 * g:8 * half + 4 * g + 4].rearrange("p h n -> p (h n)"),
                                    wq_lo[:, 8 * half + 4 * g:8 * half + 4 * g + 4].rearrange("p h n -> p (h n)")), True, True)
                last.then_inc(sg["d_q_ready"], 1)

            def transpose_q(n, half):
                if half == 0:
                    need(pe, "d_qf_done", n + 1)
                    need(pe, "d_qTb_done", n)
                else:
                    need(pe, "d_qTa_done", n + 1)
                for h in range(4):
                    last = pe.transpose(qT_ps[:, h * P:(h + 1) * P], qf[:, 4 * half + h], ident[:])
                last.then_inc(sg["d_qT_ready"], 1)

            def scores(n, seq0, b):
                need(pe, "d_qTb_done", n + 1)
                need(pe, "d_qTa_done", n + 1)
                need(pe, "d_sub_done", n)
                for q in range(4):
                    for s in range(2):
                        pe.matmul(s_ps[:, q * P + s * SEQ:q * P + (s + 1) * SEQ], qT[:, b, q, s],
                                  keysT[:, ds((seq0 + s) * SEQ, SEQ)], start=(q == 0 and s == 0), stop=False,
                                  skip_group_check=True)
                for q in range(4):
                    last = pe.matmul(s_ps[:, q * P:(q + 1) * P], consts["mask_rows"][:],
                                     mask[:, ds(seq0, 2), :], start=False, stop=True, skip_group_check=True)
                last.then_inc(sg["d_s_ready"], 1)

            def transpose_probs(m, b):
                need(pe, "d_pn_done", m + 1)
                need(pe, "d_pt_done", m)
                for q in range(4):
                    last = pe.transpose(t_ps[:, q * P:(q + 1) * P], prob[:, b, 2 * q:2 * q + 2].rearrange("p g k -> p (g k)"),
                                        ident[:])
                last.then_inc(sg["d_t_ready"], 1)

            def attend(m, b, tile_par, tiles):
                need(pe, "d_pt_done", m + 1)
                need(pe, "d_ot_done", m)
                need(pe, "d_v_done", tiles)
                pe.matmul(o_ps[:], vcur[:, tile_par], probT[:, b], start=True, stop=True).then_inc(sg["d_pv_ready"], 1)

            def project_out(m, b, x_count):
                need(pe, "d_ot_done", m + 1)
                if b == 0:
                    need(pe, "d_x_done", x_count)
                for q in range(4):
                    last = pe.matmul(out_ps[:, 0:D], attT[:, b, q], wn[:, 4 * b + q], start=(b == 0 and q == 0),
                                     stop=(b == 1 and q == 3))
                last.then_inc(sg["d_out_ready"], 1)

            pe.wait_ge(wsmall_lo, 2)
            keys_of(0)
            keys_of(1)
            for k in range(2):
                for h in range(8):
                    last = pe.matmul(q_ps[0:QC, k, h * KC:(h + 1) * KC], wuqT[:, 8 * k + h], wukT[:, 8 * k + h], start=True, stop=True)
                last.then_inc(fold_ready, 1)
            transpose_keys(0)
            transpose_norm(0)
            keys_of(2)
            compress(0)
            transpose_keys(1)
            fold_values(0)
            keys_of(3)
            pe.wait_ge(fold_lo, 3)
            queries(0, 0, 0, 0)
            fold_values(1)
            transpose_keys(2)
            transpose_keys(3)
            fold_values(2)
            pe.wait_ge(kvT_done, KB)
            transpose_q(0, 0)
            fold_values(3)
            transpose_q(0, 1)
            queries(1, 0, 0, 1)
            pe.wait_ge(wn_done, H // 4)
            pe.wait_ge(mask_done, 1)
            with pe.Fori(0, NU // 8) as j:
                for k in range(8):
                    n, b = 8 * j + k, k % 2
                    tok = 4 * j + k // 2
                    k2 = k + 2
                    scores(n, 2 * tok, b)
                    with pe.If(j > 0) if k == 0 else nullcontext():
                        attend(n - 1, 1 - b, ((k - 1) // 2) % 2, 4 * j + (k + 1) // 2)
                    transpose_q(n + 1, 0)
                    queries(n + 2, 2 * j + k2 // 4, (k2 // 4) % 2, k2 % 4)
                    transpose_q(n + 1, 1)
                    with pe.If(j > 0) if k < 2 else nullcontext():
                        project_out(n - 2, b, 4 * j + k // 2 - 1)
                    transpose_probs(n, b)
                    if k % 4 == 0:
                        transpose_norm(2 * j + k // 4 + 1)
                    if k % 4 == 1:
                        compress(2 * j + k // 4 + 1)
            attend(NU - 1, 1, 1, TT)
            project_out(NU - 2, 0, TT - 1)
            project_out(NU - 1, 1, TT - 1)


def set_constants(nc, dram, consts, xres):
    with ExitStack() as ctx:
        taken = Taken(nc, ctx)
        raw = ctx.enter_context(nc.sbuf_tensor("c_raw", [P, P + SEQ], F32))
        c_in = taken.take("const_in")
        made = taken.take("const_made")
        block = ctx.enter_context(nc.Block())

        @block.sync
        def _(sp):
            sp.dma_start(raw[:, 0:P], dram["mask_rows"]).then_inc(c_in, 16)
            sp.dma_start(raw[:, P:], dram["causal"]).then_inc(c_in, 16)
            sp.dma_start(consts["ident"][:], dram["ident"]).then_inc(c_in, 16)

        @block.vector
        def _(dve):
            dve.memset(consts["ones"][:], 1.0)
            dve.memset(consts["minus_half"][:], -0.5)
            dve.memset(xres[:, X0 + TT:, :], 0.0)
            dve.wait_ge(c_in, 48)
            dve.tensor_copy(consts["mask_rows"][:], raw[:, 0:P])
            dve.tensor_copy(consts["causal"][:], raw[:, P:]).then_inc(made, 1)
            dve.wait_ge(made, 1)


M0 = 2 * P
F_MLP = 1024


def layer1_ffn(nc, dram, xres, consts):
    with ExitStack() as ctx:
        yT_hi = ctx.enter_context(nc.sbuf_tensor("yT_hi", [P, CK, NTOK + T], F32R))
        yT_lo = ctx.enter_context(nc.sbuf_tensor("yT_lo", [P, CK, NTOK + T], F32R))
        modT = ctx.enter_context(nc.sbuf_tensor("modT", [P, M0 + NTOK + T], F32R))
        mlp = {name: ctx.enter_context(nc.sbuf_tensor("f_" + name, shape, dt)) for name, shape, dt in (
            ("wg", [P, 2 * CK, F_MLP], F32), ("wd", [P, F_MLP // P, D], F32), ("wb", [P, F_MLP], F32), ("ln2", [P, CK], F32),
            ("wg_hi0", [P, 2 * CK, F_MLP // 2], F32R), ("wg_lo0", [P, 2 * CK, F_MLP // 2], F32R), ("wb3", [P, F_MLP], F32R))}
        layer1_modulation(nc, dram, xres, consts, yT_hi, yT_lo, modT, mlp)
        layer1_mlp(nc, dram, xres, yT_hi, yT_lo, modT, mlp)


def layer1_modulation(nc, dram, xres, consts, yT_hi, yT_lo, modT, mlp):
    RA, HW = 16, 16
    NU = 2 * TT
    HA = 4
    SCALE = 1.0 / HW ** 0.5
    with ExitStack() as ctx:
        taken = Taken(nc, ctx)
        def sb(name, shape, dt=F32):
            return ctx.enter_context(nc.sbuf_tensor(name, shape, dt))

        def sem(name):
            return taken.take(name)

        wqk = sb("e_wqk", [P, 2, CK, D])
        wv = sb("e_wv", [P, CK, D])
        wof = sb("e_wof", [P, CK, D])
        wa = sb("e_wa", [P, CK, RA])
        ln1 = sb("e_ln1", [P, CK])
        ln2 = mlp["ln2"]
        heads = sb("e_heads", [P, 8])
        same_head = sb("e_same_head", [P, CK, H])
        g_sb = sb("e_g", [P, CK, RA])
        gx = sb("e_gx", [P, CK, H, RA])
        qk_hi = sb("e_qk_hi", [P, 2, CK, D], F32R)
        qk_lo = sb("e_qk_lo", [P, 2, CK, D], F32R)
        wu_hi = sb("e_wu_hi", [P, CK, D], F32R)
        wu_lo = sb("e_wu_lo", [P, CK, D], F32R)
        wu_f = sb("e_wu_f", [P, CK, D])
        wa_hi = sb("e_wa_hi", [P, CK, RA], F32R)
        wa_lo = sb("e_wa_lo", [P, CK, RA], F32R)

        bst = sb("e_bst", [P, 2, 6])
        mv = sb("e_mv", [P, 2, 2])
        var = sb("e_var", [P, 2])
        rstd = sb("e_rstd", [P, 2])
        ms1 = sb("e_ms1", [P, 2])
        ms2 = sb("e_ms2", [P, 2])
        ms3 = sb("e_ms3", [P, 2])
        rrms = sb("e_rrms", [P, 2])
        tiny = sb("e_tiny", [P, 2])
        spare = sb("e_spare", [P, 1])
        y = sb("e_y", [P, 2, D])
        yh = sb("e_yh", [P, 2, D])
        yt_hi = sb("e_yt_hi", [P, 2, CK, T], F32R)
        yt_lo = sb("e_yt_lo", [P, 2, CK, T], F32R)
        qd = sb("e_qd", [P, 2, CK, T])
        kd = sb("e_kd", [P, 2, CK, T])
        qm = sb("e_qm", [P, 2, 2, 8, SEQ])
        ub = sb("e_ub", [P, 2, 2, H, 64])
        ha = sb("e_ha", [RA, 2, T])
        s_max = sb("e_s_max", [P, 8])
        s_sum = sb("e_s_sum", [P, 8])
        s_inv = sb("e_s_inv", [P, 2, 8])
        sc = sb("e_sc", [P, 2, 8, SEQ])
        prob = sb("e_prob", [P, 2, 8, SEQ])
        probT = sb("e_probT", [P, 2, 512])
        th = sb("e_th", [RA, 2, SEQ])
        mod = sb("e_mod", [RA, P])

        def bank(name):
            return ctx.enter_context(nc.psum_tensor(name, [P, 512], F32))

        s_ps = [bank("e_ps_s0"), bank("e_ps_s1")]
        q_ps, k_ps, m_ps, t_ps, u_ps = (bank("e_ps_" + n) for n in ("q", "k", "m", "t", "u"))
        w_ps = k_ps

        PE_S = ["e_nT_ready", "e_q_ready", "e_k_ready", "e_u_ready", "e_ha_ready", "e_s_ready", "e_t_ready", "e_mod_ready"]
        ACT_S = ["e_wghi_done", "e_yhi_done", "e_q_done", "e_k_done", "e_u_done", "e_ha_done", "e_exp_done", "e_pt_done", "e_tanh_done", "e_qma_done"]
        DVE_S = ["e_bst_done", "e_mv_done", "e_var_done", "e_y_done", "e_yh_done", "e_ylo_done", "e_max_done", "e_sub_done",
                 "e_sum_done", "e_inv_done", "e_prod_done", "e_modhi_done", "e_mod_done"]
        POOL_S = ["e_rstd_done", "e_ms1_done", "e_ms2_done", "e_ms3_done", "e_rrms_done", "e_x_done", "e_qm_done", "e_pn_done"]
        sg = Signals(taken, PE_S + ACT_S + DVE_S + POOL_S, less=("e_pt_done", "e_tanh_done"))
        need = sg.need
        w_in, small_in, g_in, mlp_in = sem("e_w_in"), sem("e_small_in"), sem("e_g_in"), sem("e_mlp_in")
        cleared, gx_done, g_ready, g_done, wu_ready = sem("e_cleared"), sem("e_gx_done"), sem("e_g_ready"), sem("e_g_done"), sem("e_wu_ready")
        whi_done, wlo_done = sem("e_whi_done"), sem("e_wlo_done")
        saved = [sem("e_saved0"), sem("e_saved1")]
        wbhi_done = sem("e_wbhi_done")
        GC = F_MLP // 2 // (NU // 8)

        block = ctx.enter_context(nc.Block())

        @block.sync
        def _(sp):
            sp.dma_start(wof[:], dram["wo_f"].rearrange("(c p) n -> p c n", p=P)).then_inc(g_in, 16)
            sp.dma_start(wa[:], dram["wa"].rearrange("(c p) n -> p c n", p=P)).then_inc(g_in, 16)
            sp.dma_start(same_head[:], dram["same_head"].rearrange("(c p) n -> p c n", p=P)).then_inc(small_in, 16)
            sp.dma_start(ln1[:], dram["ln1_w"]).then_inc(small_in, 16)
            sp.dma_start(ln2[:], dram["ln2_w"]).then_inc(small_in, 16)
            sp.dma_start(wv[:], dram["wv_f"].rearrange("(c p) n -> p c n", p=P)).then_inc(w_in, 16)
            for k, name in enumerate(("wqT_f", "wkT_f")):
                sp.dma_start(wqk[:, k], dram[name].rearrange("(c p) n -> p c n", p=P)).then_inc(w_in, 16)
            sp.dma_start(heads[:], dram["heads"]).then_inc(small_in, 16)
            for k, name in enumerate(("w_inT", "w_upT")):
                sp.dma_start(mlp["wg"][:, CK * k:CK * (k + 1)], dram[name].rearrange("(c p) n -> p c n", p=P)).then_inc(mlp_in, 16)
            sp.wait_ge(cleared, 2)
            for k in range(3):
                sp.dma_start(mlp["wb"][32 * k:32 * k + RA, :], dram["wb"]).then_inc(mlp_in, 16)
            sp.dma_start(mlp["wd"][:], dram["w_downT"].rearrange("(f p) n -> p f n", p=P)).then_inc(mlp_in, 16)
            for k in range(2):
                sp.sem_inc(saved[k], 32)
            with sp.Fori(0, NT // 2) as j:
                for a in range(2):
                    need(sp, "e_ylo_done", 2 * j + a + 1)
                    sp.dma_start(yT_hi[:, :, ds((2 * j + a) * T, T)].bitcast(F32), yt_hi[:, a].bitcast(F32)).then_inc(saved[a], 16)
                    sp.dma_start(yT_lo[:, :, ds((2 * j + a) * T, T)].bitcast(F32), yt_lo[:, a].bitcast(F32)).then_inc(saved[a], 16)
            for k in range(2):
                sp.wait_ge(saved[k], 32 * (NT // 2 + 1))
            sp.wait_ge(mlp_in, 6 * 16)

        @block.gpsimd
        def _(pool):
            sg.give_credit(pool, POOL_S)
            pool.memset(mlp["wb"][:], 0.0)
            pool.memset(ub[:], 0.0)
            pool.memset(modT[:].bitcast(F32), 0.0).then_inc(cleared, 1)

            def root_var(tile):
                need(pool, "e_var_done", tile + 1)
                pool.tensor_tensor(rstd[:], var[:], consts["minus_half"][:, 0:2], ALU.pow).then_inc(sg["e_rstd_done"], 1)

            def root_square(tile):
                need(pool, "e_rstd_done", tile + 1)
                pool.tensor_tensor(ms1[:], mv[:, :, 1], rstd[:], ALU.mult).then_inc(sg["e_ms1_done"], 1)
                need(pool, "e_ms1_done", tile + 1)
                pool.tensor_tensor(ms2[:], ms1[:], rstd[:], ALU.mult).then_inc(sg["e_ms2_done"], 1)
                need(pool, "e_ms2_done", tile + 1)
                pool.tensor_tensor(ms3[:], ms2[:], tiny[:], ALU.add).then_inc(sg["e_ms3_done"], 1)
                need(pool, "e_ms3_done", tile + 1)
                pool.tensor_tensor(rrms[:], ms3[:], consts["minus_half"][:, 0:2], ALU.pow).then_inc(sg["e_rrms_done"], 1)

            def add_y(tile):
                need(pool, "e_y_done", tile + 1)
                rows = xres[:, ds(X0 + 2 * tile, 2), :] if not isinstance(tile, int) else xres[:, X0 + 2 * tile:X0 + 2 * tile + 2, :]
                pool.tensor_tensor(rows, rows, y[:], ALU.add).then_inc(sg["e_x_done"], 1)

            def mask_heads(n, tile, par, u, b):
                t, half = u // 2, u % 2
                need(pool, "e_q_done", tile + 1)
                need(pool, "e_s_ready", n - 1)
                for s in range(2):
                    at = t * P + s * SEQ
                    last = pool.tensor_tensor(qm[:, b, s, HA:], along(qd[:, par, half, at:at + SEQ], 1, 8 - HA),
                                              along(heads[:, HA:], 2, SEQ), ALU.mult)
                last.then_inc(sg["e_qm_done"], 1)

            root_var(0)
            root_square(0)
            add_y(0)
            pool.wait_ge(small_in, 64)
            taken.clear_last(pool)
            mask_heads(0, 0, 0, 0, 0)
            with pool.Fori(0, NU // 8) as j:
                for k in range(8):
                    n, b = 8 * j + k, k % 2
                    tile = 2 * j + k // 4
                    if k % 4 == 0:
                        root_var(tile + 1)
                    k1 = k + 1
                    mask_heads(n + 1, 2 * j + k1 // 4, (k1 // 4) % 2, k1 % 4, 1 - b)
                    if k % 4 == 0:
                        root_square(tile + 1)
                    if k % 4 == 1:
                        add_y(tile + 1)
                    need(pool, "e_inv_done", n + 1)
                    pool.tensor_tensor(prob[:, b], prob[:, b], along(s_inv[:, b], 2, SEQ), ALU.mult).then_inc(sg["e_pn_done"], 1)

        @block.scalar
        def _(act):
            sg.give_credit(act, ACT_S)
            act.wait_ge(g_ready, 1)
            act.activation(g_sb[:], w_ps[:, 0:CK * RA].rearrange("p (c r) -> p c r", c=CK), ACT.Copy).then_inc(g_done, 1)
            act.wait_ge(small_in, 64)
            act.wait_ge(w_in, 48)
            for c in range(CK):
                act.activation(qk_hi[:, :, c], wqk[:, :, c], ACT.Copy, scale=ln1[:, c:c + 1])
                last = act.activation(wa_hi[:, c], wa[:, c], ACT.Copy, scale=ln2[:, c:c + 1])
            last.then_inc(whi_done, 1)

            def high(tile, par):
                need(act, "e_nT_ready", tile + 1)
                need(act, "e_ha_ready", tile - 1)
                act.wait_ge(saved[par], 16 * (tile - par) + 32)
                act.activation(yt_hi[:, par], m_ps[:].rearrange("p (c t) -> p c t", c=CK), ACT.Copy
                               ).then_inc(sg["e_yhi_done"], 1)

            def copy_q(tile, par):
                need(act, "e_q_ready", tile + 1)
                need(act, "e_qm_done", 4 * (tile - 1))
                act.activation(qd[:, par], q_ps[:].rearrange("p (c t) -> p c t", c=CK), ACT.Copy).then_inc(sg["e_q_done"], 1)

            def copy_k(tile, par):
                need(act, "e_k_ready", tile + 1)
                need(act, "e_s_ready", 4 * (tile - 1))
                act.activation(kd[:, par], k_ps[:].rearrange("p (c t) -> p c t", c=CK), ACT.Copy).then_inc(sg["e_k_done"], 1)

            def copy_u(tile, par):
                need(act, "e_u_ready", tile + 1)
                need(act, "e_mod_ready", 4 * (tile - 1))
                src = m_ps[:].rearrange("p (t h r) -> p t h r", t=2, h=H)
                for s in range(2):
                    last = act.activation(ub[s * SEQ:(s + 1) * SEQ, par, :, :, 32 * s:32 * s + RA], src[s * SEQ:(s + 1) * SEQ],
                                          ACT.Copy)
                last.then_inc(sg["e_u_done"], 1)

            def copy_ha(tile, par):
                need(act, "e_ha_ready", tile + 1)
                need(act, "e_prod_done", 2 * (tile - 1))
                act.activation(ha[:, par], m_ps[0:RA, 0:T], ACT.Copy, scale=0.1).then_inc(sg["e_ha_done"], 1)

            def copy_probs(m, b):
                need(act, "e_t_ready", m + 1)
                need(act, "e_mod_ready", m - 1)
                act.activation(probT[:, b], t_ps[:], ACT.Copy).then_inc(sg["e_pt_done"], 1)

            def tanh(tok):
                need(act, "e_mod_ready", 2 * tok + 2)
                need(act, "e_prod_done", tok)
                for s in range(2):
                    last = act.activation(th[:, s], u_ps[32 * s:32 * s + RA, 0:SEQ], ACT.Tanh)
                last.then_inc(sg["e_tanh_done"], 1)

            def mask_heads(n, tile, par, u, b):
                t, half = u // 2, u % 2
                need(act, "e_q_done", tile + 1)
                need(act, "e_s_ready", n - 1)
                for h in range(HA):
                    last = act.activation(qm[:, b, :, h], qd[:, par, half, t * P:(t + 1) * P].rearrange("p (s t) -> p s t", s=2),
                                          ACT.Copy, scale=heads[:, h:h + 1])
                last.then_inc(sg["e_qma_done"], 1)

            act.wait_ge(cleared, 2)
            high(0, 0)
            act.wait_ge(wu_ready, 1)
            for c in range(CK):
                last = act.activation(wu_f[:, c], w_ps[:, c * D:(c + 1) * D], ACT.Copy, scale=ln1[:, c:c + 1])
            last.then_inc(g_done, 1)
            act.wait_ge(g_done, 2)
            act.activation(wu_hi[:], wu_f[:], ACT.Copy).then_inc(whi_done, 1)
            copy_q(0, 0)
            copy_k(0, 0)
            mask_heads(0, 0, 0, 0, 0)
            copy_u(0, 0)

            def mlp_high(j, k):
                if k % 2 == 0:
                    r, cols = k // 2, ds(j * GC, GC)
                    act.activation(mlp["wg_hi0"][:, r, cols], mlp["wg"][:, r, cols], ACT.Copy,
                                   scale=ln2[:, r % CK:r % CK + 1]).then_inc(sg["e_wghi_done"], 1)

            act.wait_ge(mlp_in, 6 * 16)
            with act.Fori(0, NU // 8) as j:
                for k in range(8):
                    n, b = 8 * j + k, k % 2
                    tile, nxt = 2 * j + k // 4, 1 - k // 4
                    k1 = k + 1
                    mask_heads(n + 1, 2 * j + k1 // 4, (k1 // 4) % 2, k1 % 4, 1 - b)
                    mlp_high(j, k)
                    need(act, "e_sub_done", n + 1)
                    need(act, "e_t_ready", n - 1)
                    act.activation(prob[:, b], sc[:, b], ACT.Exp, scale=SCALE).then_inc(sg["e_exp_done"], 1)
                    copy_probs(n - 1, 1 - b)
                    if b == 1:
                        tanh(4 * j + (k - 3) // 2)
                    if k % 4 == 0:
                        copy_ha(tile, k // 4)
                    if k % 4 == 1:
                        high(tile + 1, nxt)
                    if k % 4 == 2:
                        copy_q(tile + 1, nxt)
                        copy_k(tile + 1, nxt)
                    if k % 4 == 3:
                        copy_u(tile + 1, nxt)
            act.activation(mlp["wb3"][:], mlp["wb"][:], ACT.Copy).then_inc(wbhi_done, 1)
            copy_probs(NU - 1, 1)
            tanh(TT - 1)

        @block.vector
        def _(dve):
            sg.give_credit(dve, DVE_S)
            dve.memset(u_ps[:], 0.0)
            dve.memset(t_ps[:], 0.0)
            dve.memset(tiny[:], 1e-6).then_inc(cleared, 1)

            def row(r):
                return xres[:, X0 + r, :] if isinstance(r, int) else xres[:, ds(X0 + r, 1), :].rearrange("p a d -> p (a d)")

            def norm_stats(tile):
                for t in range(2):
                    last = dve.bn_stats(bst[:, t], row(2 * tile + t))
                last.then_inc(sg["e_bst_done"], 1)
                need(dve, "e_bst_done", tile + 1)
                dve.memset(spare[:], 0.0)
                for t in range(2):
                    last = dve.bn_aggr(mv[:, t], bst[:, t])
                last.then_inc(sg["e_mv_done"], 1)
                need(dve, "e_mv_done", tile + 1)
                dve.tensor_scalar(var[:], mv[:, :, 1], 1e-5, None, ALU.add).then_inc(sg["e_var_done"], 1)

            def norm_rows(tile):
                need(dve, "e_rstd_done", tile + 1)
                need(dve, "e_x_done", tile)
                for t in range(2):
                    last = dve.tensor_scalar(y[:, t], row(2 * tile + t), mv[:, t, 0:1], rstd[:, t:t + 1],
                                             ALU.subtract, ALU.mult)
                last.then_inc(sg["e_y_done"], 1)

            def rms_rows(tile):
                need(dve, "e_y_done", tile + 1)
                need(dve, "e_rrms_done", tile + 1)
                for t in range(2):
                    last = dve.tensor_scalar(yh[:, t], y[:, t], rrms[:, t:t + 1], None, ALU.mult)
                last.then_inc(sg["e_yh_done"], 1)

            def low(tile, par):
                need(dve, "e_yhi_done", tile + 1)
                dve.tensor_tensor(yt_lo[:, par], m_ps[:].rearrange("p (c t) -> p c t", c=CK), yt_hi[:, par].bitcast(F32),
                                  ALU.subtract).then_inc(sg["e_ylo_done"], 1)

            def modulation(tok, col, par, t):
                need(dve, "e_mod_done", tok)
                need(dve, "e_tanh_done", tok + 1)
                dve.tensor_tensor(mod[:], th[:].rearrange("p s t -> p (s t)"), ha[:, par, t * P:(t + 1) * P], ALU.mult
                                  ).then_inc(sg["e_prod_done"], 1)
                at = ds(col, P) if not isinstance(col, int) else slice(col, col + P)
                need(dve, "e_prod_done", tok + 1)
                dve.tensor_scalar(modT[0:RA, at], mod[:], 1.0, None, ALU.mult)
                dve.tensor_scalar(modT[64:64 + RA, at], mod[:], 1.0, None, ALU.mult).then_inc(sg["e_modhi_done"], 1)
                need(dve, "e_modhi_done", tok + 1)
                dve.tensor_tensor(modT[32:32 + RA, at], mod[:], modT[0:RA, at].bitcast(F32), ALU.subtract
                                  ).then_inc(sg["e_mod_done"], 1)

            norm_stats(0)
            norm_rows(0)
            rms_rows(0)
            dve.wait_ge(g_done, 1)
            dve.wait_ge(small_in, 64)
            dve.tensor_tensor(gx[:], along(g_sb[:], 2, H), along(same_head[:], 3, RA), ALU.mult).then_inc(gx_done, 1)
            dve.wait_ge(whi_done, 1)
            for c in range(CK):
                for k in range(2):
                    dve.scalar_tensor_tensor(qk_lo[:, k, c], wqk[:, k, c], ln1[:, c:c + 1], qk_hi[:, k, c].bitcast(F32),
                                             ALU.mult, ALU.subtract)
                last = dve.scalar_tensor_tensor(wa_lo[:, c], wa[:, c], ln2[:, c:c + 1], wa_hi[:, c].bitcast(F32),
                                                ALU.mult, ALU.subtract)
            last.then_inc(wlo_done, 1)
            dve.wait_ge(cleared, 2)
            low(0, 0)
            dve.wait_ge(whi_done, 2)
            dve.tensor_tensor(wu_lo[:], wu_f[:], wu_hi[:].bitcast(F32), ALU.subtract).then_inc(wlo_done, 1)

            def mlp_low(j, k):
                if k % 2 == 0:
                    r, cols = k // 2, ds(j * GC, GC)
                    need(dve, "e_wghi_done", 4 * j + r + 1)
                    dve.scalar_tensor_tensor(mlp["wg_lo0"][:, r, cols], mlp["wg"][:, r, cols], ln2[:, r % CK:r % CK + 1],
                                             mlp["wg_hi0"][:, r, cols].bitcast(F32), ALU.mult, ALU.subtract)

            dve.wait_ge(mlp_in, 6 * 16)
            with dve.Fori(0, NU // 8) as j:
                for k in range(8):
                    n, b = 8 * j + k, k % 2
                    tile, nxt = 2 * j + k // 4, 1 - k // 4
                    if b == 1:
                        with dve.If(j > 0) if k < 4 else nullcontext():
                            tok = 4 * j + k // 2 - 2
                            modulation(tok, (4 * j + k // 2) * P, (k // 4 + 1) % 2, (k // 2) % 2)
                    if k % 4 == 0:
                        norm_stats(tile + 1)
                    if k % 4 == 1:
                        rms_rows(tile + 1)
                    if k % 4 == 2:
                        low(tile + 1, nxt)
                    need(dve, "e_s_ready", n + 1)
                    s3 = s_ps[b][:].rearrange("p (g k) -> p g k", g=8)
                    dve.tensor_reduce(s_max[:], s3, AX, ALU.max).then_inc(sg["e_max_done"], 1)
                    need(dve, "e_max_done", n + 1)
                    need(dve, "e_exp_done", n - 1)
                    dve.tensor_tensor(sc[:, b], s3, along(s_max[:], 2, SEQ), ALU.subtract).then_inc(sg["e_sub_done"], 1)
                    if k % 4 == 0:
                        norm_rows(tile + 1)
                    mlp_low(j, k)
                    need(dve, "e_exp_done", n + 1)
                    dve.tensor_reduce(s_sum[:], prob[:, b], AX, ALU.add).then_inc(sg["e_sum_done"], 1)
                    need(dve, "e_sum_done", n + 1)
                    need(dve, "e_pn_done", n - 1)
                    dve.reciprocal(s_inv[:, b], s_sum[:]).then_inc(sg["e_inv_done"], 1)
            for t in range(2):
                modulation(TT - 2 + t, M0 + (TT - 2 + t) * P, 1, t)
                if t == 0:
                    dve.wait_ge(wbhi_done, 1)
                    dve.tensor_tensor(mlp["wb3"][64:64 + RA], mlp["wb"][64:64 + RA], mlp["wb3"][64:64 + RA].bitcast(F32),
                                      ALU.subtract)

        @block.tensor
        def _(pe):
            sg.give_credit(pe, PE_S)
            def transpose_norm(tile):
                need(pe, "e_yh_done", tile + 1)
                need(pe, "e_ha_done", tile)
                for c in range(CK):
                    for t in range(2):
                        last = pe.transpose(m_ps[:, c * T + t * P:c * T + (t + 1) * P], yh[:, t, c * P:(c + 1) * P],
                                            consts["ident"][:])
                last.then_inc(sg["e_nT_ready"], 1)

            def project_qk(which, tile, par):
                if which == 0:
                    need(pe, "e_ylo_done", tile + 1)
                    need(pe, "e_q_done", tile)
                else:
                    need(pe, "e_ylo_done", tile + 1)
                    need(pe, "e_k_done", tile)
                for m in range(2):
                    for c in range(CK):
                        last = matmul3(pe, (k_ps if which else q_ps)[:, m * T:(m + 1) * T], (qk_hi[:, which, c, m * P:(m + 1) * P],
                                                                         qk_lo[:, which, c, m * P:(m + 1) * P]),
                                       (yt_hi[:, par, c], yt_lo[:, par, c]), c == 0, c == CK - 1)
                last.then_inc(sg["e_k_ready" if which else "e_q_ready"], 1)

            def project_u(tile, par):
                for t in range(2):
                    for c in range(CK):
                        last = matmul3(pe, m_ps[:, t * D:(t + 1) * D], (yt_hi[:, par, c, t * P:(t + 1) * P],
                                                                        yt_lo[:, par, c, t * P:(t + 1) * P]),
                                       (wu_hi[:, c], wu_lo[:, c]), c == 0, c == CK - 1)
                last.then_inc(sg["e_u_ready"], 1)

            def project_a(tile, par):
                need(pe, "e_u_done", tile + 1)
                for c in range(CK):
                    last = matmul3(pe, m_ps[0:RA, 0:T], (wa_hi[:, c], wa_lo[:, c]), (yt_hi[:, par, c], yt_lo[:, par, c]),
                                   c == 0, c == CK - 1)
                last.then_inc(sg["e_ha_ready"], 1)

            def scores(n, tile, par, u, b):
                t, half = u // 2, u % 2
                need(pe, "e_qm_done", n + 1)
                need(pe, "e_qma_done", n + 1)
                need(pe, "e_k_done", tile + 1)
                need(pe, "e_sub_done", n - 1)
                for q in range(4):
                    for s in range(2):
                        at = t * P + s * SEQ
                        pe.matmul(s_ps[b][:, q * P + s * SEQ:q * P + (s + 1) * SEQ],
                                  qm[:, b, s, 2 * q:2 * q + 2].rearrange("p h t -> p (h t)"),
                                  kd[:, par, half, at:at + SEQ], start=(q == 0 and s == 0), stop=False,
                                  skip_group_check=True)
                last = pe.matmul(s_ps[b][:], consts["mask_rows"][:], along(consts["causal"][:], 1, 8),
                                 start=False, stop=True, skip_group_check=True)
                last.then_inc(sg["e_s_ready"], 1)

            def transpose_probs(m, b):
                need(pe, "e_pn_done", m + 1)
                need(pe, "e_pt_done", m)
                for q in range(4):
                    last = pe.transpose(t_ps[:, q * P:(q + 1) * P], prob[:, b, 2 * q:2 * q + 2].rearrange("p g k -> p (g k)"),
                                        consts["ident"][:])
                last.then_inc(sg["e_t_ready"], 1)

            def attend(m, tile, par, u, b, tok):
                t, half = u // 2, u % 2
                need(pe, "e_pt_done", m + 1)
                need(pe, "e_u_done", tile + 1)
                if half == 0:
                    need(pe, "e_tanh_done", tok)
                for h in range(8):
                    last = pe.matmul(u_ps[0:64, 0:SEQ], ub[:, par, t, 8 * half + h], probT[:, b, h * SEQ:(h + 1) * SEQ],
                                     start=(half == 0 and h == 0), stop=(half == 1 and h == 7))
                last.then_inc(sg["e_mod_ready"], 1)

            pe.wait_ge(g_in, 32)
            for c in range(CK):
                for i in range(CK):
                    last = pe.matmul(w_ps[:, c * RA:(c + 1) * RA], wof[:, i, c * P:(c + 1) * P], wa[:, i], start=(i == 0),
                                     stop=(i == CK - 1))
            last.then_inc(g_ready, 1)
            transpose_norm(0)
            pe.wait_ge(gx_done, 1)
            pe.wait_ge(w_in, 48)
            for c in range(CK):
                for i in range(CK):
                    last = pe.matmul(w_ps[:, c * D:(c + 1) * D], wv[:, i, c * P:(c + 1) * P],
                                     gx[:, i].rearrange("p h r -> p (h r)"), start=(i == 0), stop=(i == CK - 1))
            last.then_inc(wu_ready, 1)
            pe.wait_ge(wlo_done, 1)
            pe.wait_ge(cleared, 2)
            project_qk(0, 0, 0)
            pe.wait_ge(g_done, 2)
            project_qk(1, 0, 0)
            pe.wait_ge(wlo_done, 2)
            project_u(0, 0)
            with pe.Fori(0, NU // 8) as j:
                for k in range(8):
                    n, b = 8 * j + k, k % 2
                    tile, par, nxt = 2 * j + k // 4, k // 4, 1 - k // 4
                    scores(n, tile, par, k % 4, b)
                    with pe.If(j > 0) if k < 2 else nullcontext():
                        m = (k - 2) % 8
                        attend(n - 2, tile if k % 4 > 1 else tile - 1, m // 4, m % 4, b, 4 * j + k // 2 - 1)
                    with pe.If(j > 0) if k == 0 else nullcontext():
                        transpose_probs(n - 1, 1 - b)
                    if k % 4 == 0:
                        project_a(tile, par)
                    if k % 4 == 1:
                        transpose_norm(tile + 1)
                    if k % 4 == 2:
                        project_qk(0, tile + 1, nxt)
                        project_qk(1, tile + 1, nxt)
                    if k % 4 == 3:
                        project_u(tile + 1, nxt)
            transpose_probs(NU - 1, 1)
            attend(NU - 2, NT - 1, 1, 2, 0, TT - 1)
            attend(NU - 1, NT - 1, 1, 3, 1, TT - 1)


def layer1_mlp(nc, dram, xres, yT_hi, yT_lo, modT, mlp):
    F = F_MLP
    FC = F // P
    with ExitStack() as ctx:
        taken = Taken(nc, ctx)
        def sb(name, shape, dt=F32):
            return ctx.enter_context(nc.sbuf_tensor(name, shape, dt))

        def sem(name):
            return taken.take(name)

        wg, wd, wb3, ln2 = (mlp[n] for n in ("wg", "wd", "wb3", "ln2"))
        wg_hi = [mlp["wg_hi0"], sb("f_wg_hi1", [P, 2 * CK, F // 2], F32R)]
        wg_lo = [mlp["wg_lo0"], sb("f_wg_lo1", [P, 2 * CK, F // 2], F32R)]
        wd_hi = sb("f_wd_hi", [P, FC, D], F32R)
        wd_lo = sb("f_wd_lo", [P, FC, D], F32R)
        sg_sb = sb("f_silu", [P, 2, T])
        act_f = sb("f_act", [P, 2, T])
        act_hi = sb("f_act_hi", [P, 2, T], F32R)
        act_lo = sb("f_act_lo", [P, 2, T], F32R)
        gu_ps = [ctx.enter_context(nc.psum_tensor(f"f_gu{k}", [P, 512], F32)) for k in range(4)]
        o_ps = [ctx.enter_context(nc.psum_tensor(f"f_o{k}", [P, 512], F32)) for k in range(2)]

        PE_S = ["f_gu_ready", "f_down_ready"]
        ACT_S = ["f_silu_done", "f_hi_done"]
        DVE_S = ["f_prod_done", "f_lo_done", "f_x_done"]
        sg = Signals(taken, PE_S + ACT_S + DVE_S)
        need = sg.need
        whi_done, wlo_done = sem("f_whi_done"), sem("f_wlo_done")
        stored = sem("f_stored")

        block = ctx.enter_context(nc.Block())

        @block.sync
        def _(sp):
            with sp.Fori(0, NT) as tile:
                need(sp, "f_x_done", tile + 1)
                sp.dma_start(dram["out"][ds(tile * T, T), :].rearrange("(t p) d -> p t d", p=P),
                             xres[:, ds(X0 + 2 * tile, 2), :]).then_inc(stored, 16)
            sp.wait_ge(stored, 16 * NT)

        @block.scalar
        def _(act):
            sg.give_credit(act, ACT_S)
            act.activation(wd_hi[:], wd[:], ACT.Copy).then_inc(whi_done, 1)
            for r in range(2 * CK):
                last = act.activation(wg_hi[1][:, r], wg[:, r, F // 2:], ACT.Copy, scale=ln2[:, r % CK:r % CK + 1])
            last.then_inc(whi_done, 1)
            with act.Fori(0, NT // 2) as j:
                for k in range(2 * FC):
                    g, b = 16 * j + k, k % 2
                    need(act, "f_gu_ready", g + 1)
                    need(act, "f_prod_done", g - 1)
                    act.activation(sg_sb[:, b], gu_ps[k % 4][:, 0:T], ACT.Silu).then_inc(sg["f_silu_done"], 1)
                    need(act, "f_prod_done", g + 1)
                    need(act, "f_down_ready", g - 1)
                    act.activation(act_hi[:, b], act_f[:, b], ACT.Copy).then_inc(sg["f_hi_done"], 1)

        @block.vector
        def _(dve):
            sg.give_credit(dve, DVE_S)
            dve.wait_ge(whi_done, 1)
            dve.tensor_tensor(wd_lo[:], wd[:], wd_hi[:].bitcast(F32), ALU.subtract).then_inc(wlo_done, 1)
            dve.wait_ge(whi_done, 2)
            for r in range(2 * CK):
                last = dve.scalar_tensor_tensor(wg_lo[1][:, r], wg[:, r, F // 2:], ln2[:, r % CK:r % CK + 1],
                                                wg_hi[1][:, r].bitcast(F32), ALU.mult, ALU.subtract)
            last.then_inc(wlo_done, 1)

            def add_x(tile, a):
                need(dve, "f_down_ready", FC * tile + FC)
                rows = (xres[:, X0 + 2 * tile:X0 + 2 * tile + 2, :] if isinstance(tile, int)
                        else xres[:, ds(X0 + 2 * tile, 2), :])
                dve.tensor_tensor(rows, o_ps[a][:].rearrange("p (t d) -> p t d", t=2), rows, ALU.add
                                  ).then_inc(sg["f_x_done"], 1)

            with dve.Fori(0, NT // 2) as j:
                for k in range(2 * FC):
                    g, b, a = 16 * j + k, k % 2, k // FC
                    need(dve, "f_silu_done", g + 1)
                    need(dve, "f_hi_done", g - 1)
                    dve.tensor_tensor(act_f[:, b], gu_ps[k % 4][:, T:], sg_sb[:, b], ALU.mult).then_inc(sg["f_prod_done"], 1)
                    need(dve, "f_hi_done", g + 1)
                    dve.tensor_tensor(act_lo[:, b], act_f[:, b], act_hi[:, b].bitcast(F32), ALU.subtract
                                      ).then_inc(sg["f_lo_done"], 1)
                    if k % FC == 0:
                        with dve.If(j > 0) if k == 0 else nullcontext():
                            add_x(2 * j + a - 1, 1 - a)
            add_x(NT - 1, 1)

        @block.tensor
        def _(pe):
            sg.give_credit(pe, PE_S)

            def gate_up(g, bank, tile, f):
                need(pe, "f_prod_done", g - 3)
                tok = ds(tile * T, T) if not isinstance(tile, int) else slice(tile * T, tile * T + T)
                mcol = ds(M0 + tile * T, T) if not isinstance(tile, int) else slice(M0 + tile * T, M0 + tile * T + T)
                ps = gu_ps[bank]
                cols = slice(f * P, (f + 1) * P)
                half, fh = f // (FC // 2), f % (FC // 2)
                hcols = slice(fh * P, (fh + 1) * P)
                pe.matmul(ps[:, 0:T], wb3[:, cols], modT[:, mcol], start=True, stop=False)
                for k in range(2):
                    for c in range(CK):
                        last = matmul3(pe, ps[:, k * T:(k + 1) * T], (wg_hi[half][:, CK * k + c, hcols], wg_lo[half][:, CK * k + c, hcols]),
                                       (yT_hi[:, c, tok], yT_lo[:, c, tok]), k == 1 and c == 0, c == CK - 1)
                last.then_inc(sg["f_gu_ready"], 1)

            def down(g, b, a, f, tile):
                need(pe, "f_lo_done", g + 1)
                if f == 0:
                    need(pe, "f_x_done", tile - 1)
                for t in range(2):
                    last = matmul3(pe, o_ps[a][:, t * D:(t + 1) * D], (act_hi[:, b, t * P:(t + 1) * P], act_lo[:, b, t * P:(t + 1) * P]),
                                   (wd_hi[:, f], wd_lo[:, f]), f == 0 and t == 0, f == FC - 1, skip=True)
                last.then_inc(sg["f_down_ready"], 1)

            gate_up(0, 0, 0, 0)
            gate_up(1, 1, 0, 1)
            pe.wait_ge(wlo_done, 1)
            with pe.Fori(0, NT // 2) as j:
                for k in range(2 * FC):
                    g = 16 * j + k
                    k2 = k + 2
                    if k2 == FC // 2:
                        pe.wait_ge(wlo_done, 2)
                    with pe.If(j < NT // 2 - 1) if k2 >= 2 * FC else nullcontext():
                        gate_up(g + 2, k2 % 4, (2 * j + k2 // FC) if k2 < 2 * FC else 2 * j + 2, k2 % FC)
                    down(g, k % 2, k // FC, k % FC, 2 * j + k // FC)


def program(nc, dram):
    Taken.phases = []
    with ExitStack() as ctx:
        def sb(name, shape, dt=F32):
            return ctx.enter_context(nc.sbuf_tensor(name, shape, dt))

        xres = sb("xres", [P, TT + 2 * X0, D])
        consts = {"ident": sb("ident", [P, P]), "ones": sb("ones", [P, 8]), "minus_half": sb("minus_half", [P, 32]),
                  "mask_rows": sb("mask_rows", [P, P], BF16), "causal": sb("causal", [P, SEQ], BF16)}
        set_constants(nc, dram, consts, xres)
        layer0_attention(nc, dram, xres, consts)
        ahead = {}
        with ExitStack() as early:
            for name, (shape, dt, _) in LAYER1_ATTENTION.items():
                ahead[name] = early.enter_context(nc.sbuf_tensor("d_" + name, shape, dt))
            layer0_ffn(nc, dram, xres, consts, ahead)
            layer1_attention(nc, dram, xres, consts, ahead)
        layer1_ffn(nc, dram, xres, consts)


def tables():
    f = np.float32
    inv = (f(1.0) / f(10000.0) ** (np.arange(0, HD, 2, dtype=f) / f(HD))).astype(f)
    ang = np.outer(np.arange(SEQ, dtype=f), inv).astype(f)
    cos, sin = np.cos(ang), np.sin(ang)
    cos2 = np.concatenate([cos, cos], 1)
    c = {}
    c["cos_d"] = cos2.T
    c["sin_d"] = np.concatenate([sin, -sin], 1).T
    c["cos_t"] = np.concatenate([cos2, cos2], 0)
    s2 = np.concatenate([-sin, sin], 1)
    c["sin_t"] = np.concatenate([s2, s2], 0)
    inv = (f(1.0) / f(10000.0) ** (np.arange(32, dtype=f) / f(32))).astype(f)
    ang = (np.arange(SEQ, dtype=f)[:, None] * inv).astype(f)
    cos, sin = np.cos(ang), np.sin(ang)
    c["cos_k"] = np.concatenate([np.concatenate([cos, cos], 1)] * 2, 0)
    c["sin_k"] = np.concatenate([np.concatenate([-sin, sin], 1)] * 2, 0)
    c["key_no"] = np.tile(np.arange(SEQ), (SEQ, 1))
    c["heads"] = np.arange(P)[:, None] // 16 == np.arange(8)
    c["same_head"] = np.arange(D)[:, None] // 16 == np.arange(H)
    c["ident"] = np.eye(P)
    rows = np.zeros((P, P))
    rows[np.arange(SEQ), np.arange(SEQ)] = 1
    rows[np.arange(SEQ), np.arange(SEQ) + SEQ] = 1
    c["mask_rows"] = rows
    causal = np.zeros((P, SEQ))
    causal[:SEQ][np.arange(SEQ)[None, :] > np.arange(SEQ)[:, None]] = MASKED
    c["causal"] = causal
    return {k: np.ascontiguousarray(v, dtype=f) for k, v in c.items()}


def kernel(**inputs):
    import concourse.bacc as bacc
    from concourse.bass_utils import run_bass_kernel_spmd

    a = {}
    a["x"] = inputs["x"].reshape(NTOK, D)
    a["ctxT"] = inputs["ctx_2048"].reshape(NTOK, D).T
    for n in ("wq", "wk", "wv", "wo", "wk_ctx", "wv_ctx", "q_norm_w", "k_norm_w"):
        a[n] = inputs["L0_xattn_" + n]
    a["factors"], a["ffn_bias"] = inputs["L0_ffn_factors"], inputs["L0_ffn_bias"]
    w = {n: inputs["L1_xattn_W_" + n] for n in ("kvc", "dq", "uq", "qr", "uk", "kr", "uv", "o")}
    a.update(wkvcT=w["kvc"].T, wkvc=w["kvc"], wkr=w["kr"], wdq=w["dq"], wuqT=w["uq"].T, wukT=w["uk"].T, wuvT=w["uv"].T,
             wqr=w["qr"], wo1=w["o"], segT=inputs["itok_BxS_0_1023"].T)
    f = {n: inputs["L1_ffn_" + n] for n in ("ln1_w", "ln2_w", "Wq", "Wk", "Wv", "Wo", "A", "B", "W_in_base", "W_up_base", "W_down")}
    a.update(ln1_w=f["ln1_w"].reshape(CK, P).T, ln2_w=f["ln2_w"].reshape(CK, P).T, wqT_f=f["Wq"].T, wkT_f=f["Wk"].T, wv_f=f["Wv"], wo_f=f["Wo"], wa=f["A"],
             wb=f["B"], w_inT=f["W_in_base"].T, w_upT=f["W_up_base"].T, w_downT=f["W_down"].T)
    a.update(tables())
    nc = bacc.Bacc("TRN2", target_bir_lowering=False, num_devices=1)
    arrays, dram = {}, {}
    for name, value in a.items():
        arrays["in_" + name] = np.ascontiguousarray(value)
        dram[name] = nc.dram_tensor("in_" + name, list(value.shape), mybir.dt.from_np(arrays["in_" + name].dtype),
                                    kind="ExternalInput").ap()
    out = dram["out"] = nc.dram_tensor("out", [NTOK, D], F32, kind="ExternalOutput").ap()
    program(nc, dram)
    r = run_bass_kernel_spmd(nc, [arrays], core_ids=[0])
    return np.asarray(r.results[0]["out"]).reshape(NSEQ, SEQ, D)
```
